# Optimizing a Trainium2 kernel written in Bass

```python
import numpy as np
import jax
import jax.numpy as jnp

def _softmax(x, axis=-1):
    return jax.nn.softmax(x, axis=axis)

def _gelu(x):
    return jax.nn.gelu(x, approximate=True)

def _silu(x):
    return jax.nn.silu(x)

def _sigmoid(x):
    return jax.nn.sigmoid(x)

def _layernorm(x, axis=-1, eps=1e-05):
    m = jnp.mean(x, axis=axis, keepdims=True)
    v = jnp.var(x, axis=axis, keepdims=True)
    return (x - m) / jnp.sqrt(v + eps)

def _scatter_add(tgt, idx, src, axis=0):
    return tgt.at[idx].add(src)

def _segment_sum(src, seg, n):
    return jax.ops.segment_sum(src, seg, n)
kernel_name = 'mk_xattn_seq_d4_seqx_r4_0c6d8c'

def setup_inputs(seed: int=0):
    np.random.seed(seed)
    _w = jnp.asarray

    def _rec_inputs():
        import jax
        import jax.numpy as jnp
        _rk = jax.random.key(seed)
        x = -0.0003929 + 0.9999 * jax.random.normal(jax.random.fold_in(_rk, 1), (2, 1024, 256), jnp.float32)
        _lenS = 1024 - jax.random.randint(jax.random.fold_in(_rk, 7), (2,), 0, max(1, 1024 // 4) + 1, jnp.int32)
        _lenS2 = 77 - jax.random.randint(jax.random.fold_in(_rk, 8), (2,), 0, max(1, 77 // 4) + 1, jnp.int32)
        _ctx_1024P = jax.random.normal(jax.random.fold_in(_rk, 11), (2, 16, 256), jnp.float32)
        _ctx_1024c = jax.random.dirichlet(jax.random.fold_in(_rk, 511), 0.3 * jnp.ones((16,), jnp.float32), (2, 77))
        _ctx_1024t = jnp.einsum('bsk,bkd->bsd', _ctx_1024c, _ctx_1024P)
        _ctx_1024t = _ctx_1024t * jax.lax.rsqrt(jnp.mean(jnp.square(_ctx_1024t)) + 1e-12) * 0.953939
        ctx_1024 = -0.000514642 + 1.00011 * (_ctx_1024t + 0.3 * jax.random.normal(jax.random.fold_in(_rk, 611), (2, 77, 256), jnp.float32))
        _validS = jnp.arange(1024)[None, :] < _lenS[:, None]
        _validS2 = jnp.arange(77)[None, :] < _lenS2[:, None]
        _causal = jnp.tril(jnp.ones((1024, 1024), dtype=bool))
        mask_1xS2_bf0 = jnp.logical_not(jnp.ones((1, 77), dtype=bool))
        return (x, ctx_1024, mask_1xS2_bf0)
    x, ctx_1024, mask_1xS2_bf0 = _rec_inputs()

    def _L0_xattn_setup():
        import jax, jax.numpy as jnp
        import numpy as np
        EPS = 1e-06

        def _rms(x, scale):
            return x * scale * jax.lax.rsqrt(jnp.mean(x * x, axis=-1, keepdims=True) + EPS)

        def _forward(x, mem_k, mem_v, norm1_scale, norm2_scale, Wq, bq, Wk, bk, Wv, bv, Wz, bz, Wgz, bgz, Wgh, bgh, Wg1, bg1, Wg2, bg2, Wgc1, bgc1, Wgc2, bgc2, Awq, abq, Awk, abk, Awv, abv, Awo, abo, Wf1, bf1, Wf2, bf2):
            B, S, D = x.shape
            M = mem_k.shape[1]
            H = 8
            hd = D // H
            x_norm = _rms(x, norm1_scale)
            q = x_norm @ Wq + bq
            k = x_norm @ Wk + bk
            v = x_norm @ Wv + bv
            z = x_norm @ Wz + bz
            gamma_base = jax.nn.sigmoid(jax.nn.gelu(z @ Wg1 + bg1) @ Wg2 + bg2)
            gamma_mod = jax.nn.sigmoid(jax.nn.gelu(k @ Wgc1 + bgc1) @ Wgc2 + bgc2)
            gamma = jnp.clip(gamma_base * gamma_mod, 1e-06, 1.0 - 1e-06)

            def step(h_prev, zt_gt):
                z_t, g_t = zt_gt
                gate = jax.nn.sigmoid(z_t @ Wgz + bgz + h_prev @ Wgh + bgh)
                h_tilde = (1.0 - gate) * h_prev + gate * z_t
                h_t = h_tilde + g_t * h_prev
                return (h_t, h_t)
            h0 = jnp.zeros((B, D), dtype=x.dtype)
            z_T = jnp.swapaxes(z, 0, 1)
            gamma_T = jnp.swapaxes(gamma, 0, 1)
            _, h_seq_T = jax.lax.scan(step, h0, (z_T, gamma_T))
            h_seq = jnp.swapaxes(h_seq_T, 0, 1)
            qh = (q @ Awq + abq).reshape(B, S, H, hd)
            kh = (mem_k @ Awk + abk).reshape(B, M, H, hd)
            vh = (mem_v @ Awv + abv).reshape(B, M, H, hd)
            scores = jnp.einsum('bshd,bmhd->bhsm', qh, kh) / jnp.sqrt(jnp.asarray(hd, x.dtype))
            probs = jax.nn.softmax(scores, axis=-1)
            mem_out = jnp.einsum('bhsm,bmhd->bshd', probs, vh).reshape(B, S, D) @ Awo + abo
            combined = h_seq + mem_out + v * 0.1
            x_res = x + combined
            x_norm2 = _rms(x_res, norm2_scale)
            ffn = jax.nn.gelu(x_norm2 @ Wf1 + bf1) @ Wf2 + bf2
            return x_res + ffn
        key = jax.random.key(seed)
        B, S, D, H, F, M = (4, 1024, 256, 8, 1024, 128)
        Dq = D // 4
        ks = jax.random.split(key, 24)

        def w(i, shape):
            return jax.random.normal(ks[i], shape, dtype=jnp.float32) * 0.02
        d = {'x': jax.random.normal(ks[0], (B, S, D), dtype=jnp.float32), 'mem_k': jax.random.normal(ks[1], (B, M, D), dtype=jnp.float32), 'mem_v': jax.random.normal(ks[2], (B, M, D), dtype=jnp.float32), 'norm1_scale': jnp.ones((D,), jnp.float32), 'norm2_scale': jnp.ones((D,), jnp.float32), 'Wq': w(3, (D, D)), 'bq': jnp.zeros((D,), jnp.float32), 'Wk': w(4, (D, D)), 'bk': jnp.zeros((D,), jnp.float32), 'Wv': w(5, (D, D)), 'bv': jnp.zeros((D,), jnp.float32), 'Wz': w(6, (D, D)), 'bz': jnp.zeros((D,), jnp.float32), 'Wgz': w(7, (D, D)), 'bgz': jnp.zeros((D,), jnp.float32), 'Wgh': w(8, (D, D)), 'bgh': jnp.zeros((D,), jnp.float32), 'Wg1': w(9, (D, Dq)), 'bg1': jnp.zeros((Dq,), jnp.float32), 'Wg2': w(10, (Dq, D)), 'bg2': jnp.zeros((D,), jnp.float32), 'Wgc1': w(11, (D, Dq)), 'bgc1': jnp.zeros((Dq,), jnp.float32), 'Wgc2': w(12, (Dq, D)), 'bgc2': jnp.zeros((D,), jnp.float32), 'Awq': w(13, (D, D)), 'abq': jnp.zeros((D,), jnp.float32), 'Awk': w(14, (D, D)), 'abk': jnp.zeros((D,), jnp.float32), 'Awv': w(15, (D, D)), 'abv': jnp.zeros((D,), jnp.float32), 'Awo': w(16, (D, D)), 'abo': jnp.zeros((D,), jnp.float32), 'Wf1': w(17, (D, F)), 'bf1': jnp.zeros((F,), jnp.float32), 'Wf2': w(18, (F, D)), 'bf2': jnp.zeros((D,), jnp.float32)}
        return d
    _L0_xattn_all = _L0_xattn_setup()
    _L0_xattn_in = {k: v for k, v in _L0_xattn_all.items() if k in ('norm1_scale', 'norm2_scale', 'Wq', 'bq', 'Wk', 'bk', 'Wv', 'bv', 'Wz', 'bz', 'Wgz', 'bgz', 'Wgh', 'bgh', 'Wg1', 'bg1', 'Wg2', 'bg2', 'Wgc1', 'bgc1', 'Wgc2', 'bgc2', 'Awq', 'abq', 'Awk', 'abk', 'Awv', 'abv', 'Awo', 'abo', 'Wf1', 'bf1', 'Wf2', 'bf2')}
    del _L0_xattn_all

    def _L1_xattn_setup():
        import jax, jax.numpy as jnp
        import numpy as np
        EMBED_DIM = 256
        LN_EPS = 1e-05

        def _layernorm(x, w, b):
            m = jnp.mean(x, axis=-1, keepdims=True)
            v = jnp.mean(jnp.square(x - m), axis=-1, keepdims=True)
            return (x - m) * jax.lax.rsqrt(v + LN_EPS) * w + b

        def _attention(q, k, v, scale):
            scores = jnp.einsum('bqd,bkd->bqk', q, k) * scale
            probs = jax.nn.softmax(scores, axis=-1)
            return jnp.einsum('bqk,bkd->bqd', probs, v)
        key = jax.random.key(seed)
        ks = jax.random.split(key, 16)
        B, SQ, SK, D, H = (8, 577, 13271, EMBED_DIM, 4)
        return {'input_features': jax.random.normal(ks[0], (B, SK, D), jnp.float32), 'query_feature': jax.random.normal(ks[1], (B, SQ, D), jnp.float32), 'norm1_w': jax.random.uniform(ks[2], (D,), jnp.float32, 0.5, 1.5), 'norm1_b': jax.random.normal(ks[3], (D,), jnp.float32) * 0.1, 'norm2_w': jax.random.uniform(ks[4], (D,), jnp.float32, 0.5, 1.5), 'norm2_b': jax.random.normal(ks[5], (D,), jnp.float32) * 0.1, 'norm3_w': jax.random.uniform(ks[6], (D,), jnp.float32, 0.5, 1.5), 'norm3_b': jax.random.normal(ks[7], (D,), jnp.float32) * 0.1, 'gamma1': jax.random.uniform(ks[8], (D,), jnp.float32, 0.5, 1.5), 'gamma2': jax.random.uniform(ks[9], (D,), jnp.float32, 0.5, 1.5), 'fc1_w': jax.random.normal(ks[10], (H, D), jnp.float32) * (1.0 / np.sqrt(D)), 'fc1_b': jax.random.normal(ks[11], (H,), jnp.float32) * 0.01, 'fc2_w': jax.random.normal(ks[12], (D, H), jnp.float32) * (1.0 / np.sqrt(H)), 'fc2_b': jax.random.normal(ks[13], (D,), jnp.float32) * 0.01}
    _L1_xattn_all = _L1_xattn_setup()
    _L1_xattn_in = {k: v for k, v in _L1_xattn_all.items() if k in ('norm1_w', 'norm1_b', 'norm2_w', 'norm2_b', 'norm3_w', 'norm3_b', 'gamma1', 'gamma2', 'fc1_w', 'fc1_b', 'fc2_w', 'fc2_b')}
    del _L1_xattn_all

    def _L2_xattn_setup():
        import jax, jax.numpy as jnp
        import numpy as np
        HEAD_NUM = 16
        DIM = 256
        key = jax.random.key(seed)
        ks = jax.random.split(key, 12)
        B, SQ, SKV, D = (4, 512, 1024, DIM)
        s = 1.0 / np.sqrt(D)
        inp = {'query_seq': jax.random.normal(ks[0], (B, SQ, D), jnp.float32), 'key_value_seq': jax.random.normal(ks[1], (B, SKV, D), jnp.float32), 'Wq': jax.random.normal(ks[2], (D, D), jnp.float32) * s, 'bq': jax.random.normal(ks[3], (D,), jnp.float32) * 0.01, 'Wk': jax.random.normal(ks[4], (D, D), jnp.float32) * s, 'bk': jax.random.normal(ks[5], (D,), jnp.float32) * 0.01, 'Wv': jax.random.normal(ks[6], (D, D), jnp.float32) * s, 'bv': jax.random.normal(ks[7], (D,), jnp.float32) * 0.01, 'Wo': jax.random.normal(ks[8], (D, D), jnp.float32) * s, 'ln_gamma': jnp.ones((D,), jnp.float32), 'ln_beta': jnp.zeros((D,), jnp.float32)}
        return inp
    _L2_xattn_all = _L2_xattn_setup()
    _L2_xattn_in = {k: v for k, v in _L2_xattn_all.items() if k in ('Wq', 'bq', 'Wk', 'bk', 'Wv', 'bv', 'Wo', 'ln_gamma', 'ln_beta')}
    del _L2_xattn_all

    def _L3_xattn_setup():
        import jax, jax.numpy as jnp
        import numpy as np
        D = 256
        D_STATE = 128
        N_HEADS = 8
        D_INNER = 2 * D
        HEADDIM = 64
        H_M = D_INNER // HEADDIM
        D_CONV = 4
        CONV_DIM = D_INNER + 2 * D_STATE
        D_IN_PROJ = 2 * D_INNER + 2 * D_STATE + H_M
        B = 1
        LQ = 256
        LK = 512
        EPS = 1e-05

        def _rms(x, w):
            return x * jax.lax.rsqrt(jnp.mean(x * x, axis=-1, keepdims=True) + EPS) * w

        def _ln(x, w, b):
            mu = jnp.mean(x, axis=-1, keepdims=True)
            v = jnp.mean((x - mu) ** 2, axis=-1, keepdims=True)
            return (x - mu) * jax.lax.rsqrt(v + EPS) * w + b

        def _mamba2_block(x, norm_w, in_proj_w, conv_w, conv_b, dt_bias, A_log, D_skip, gnorm_w, out_proj_w):
            b, L, _ = x.shape
            resid = x
            zxbcdt = _rms(x, norm_w) @ in_proj_w
            z = zxbcdt[..., :D_INNER]
            xBC = zxbcdt[..., D_INNER:D_INNER + CONV_DIM]
            dt = jax.nn.softplus(zxbcdt[..., -H_M:] + dt_bias)
            padded = jnp.pad(xBC, ((0, 0), (D_CONV - 1, 0), (0, 0)))
            conv = conv_b + sum((padded[:, k:k + L, :] * conv_w[:, k] for k in range(D_CONV)))
            xBC = jax.nn.silu(conv)
            xh = xBC[..., :D_INNER].reshape(b, L, H_M, HEADDIM)
            Bm = xBC[..., D_INNER:D_INNER + D_STATE]
            Cm = xBC[..., D_INNER + D_STATE:]
            A = -jnp.exp(A_log)
            decay = jnp.exp(dt * A)
            dbx = dt[..., None] * xh

            def step(h, inp):
                dec, u, bt, ct = inp
                h = h * dec[:, :, None, None] + u[..., None] * bt[:, None, None, :]
                y = jnp.einsum('bhpn,bn->bhp', h, ct)
                return (h, y)
            h0 = jnp.zeros((b, H_M, HEADDIM, D_STATE), x.dtype)
            xs = (decay.transpose(1, 0, 2), dbx.transpose(1, 0, 2, 3), Bm.transpose(1, 0, 2), Cm.transpose(1, 0, 2))
            _, ys = jax.lax.scan(step, h0, xs)
            y = ys.transpose(1, 0, 2, 3) + D_skip[None, None, :, None] * xh
            u = _rms(y.reshape(b, L, D_INNER) * jax.nn.silu(z), gnorm_w)
            return resid + u @ out_proj_w

        def _cross_attention(x, enc, pad_mask, ln_w, ln_b, Wq, Wk, Wv, Wo):
            b, Lq, _ = x.shape
            Lk = enc.shape[1]
            dh = D // N_HEADS
            resid = x
            xn = _ln(x, ln_w, ln_b)
            q = (xn @ Wq).reshape(b, Lq, N_HEADS, dh)
            k = (enc @ Wk).reshape(b, Lk, N_HEADS, dh)
            v = (enc @ Wv).reshape(b, Lk, N_HEADS, dh)
            scores = jnp.einsum('bqhd,bkhd->bhqk', q, k) * np.float32(1.0 / np.sqrt(dh))
            scores = jnp.where(pad_mask[:, None, None, :], jnp.float32(-1000000000.0), scores)
            p = jax.nn.softmax(scores, axis=-1)
            ctx = jnp.einsum('bhqk,bkhd->bqhd', p, v).reshape(b, Lq, D)
            return resid + ctx @ Wo
        key = jax.random.key(seed)
        ks = jax.random.split(key, 10)
        s = 0.02
        return {'x': jax.random.normal(ks[0], (B, LQ, D), jnp.float32), 'encoder_out': jax.random.normal(ks[1], (B, LK, D), jnp.float32), 'encoder_padding_mask': jnp.zeros((B, LK), dtype=bool), 'm_norm_w': jnp.ones((D,), jnp.float32), 'in_proj_w': s * jax.random.normal(ks[2], (D, D_IN_PROJ), jnp.float32), 'conv_w': s * jax.random.normal(ks[3], (CONV_DIM, D_CONV), jnp.float32), 'conv_b': jnp.zeros((CONV_DIM,), jnp.float32), 'dt_bias': jnp.full((H_M,), float(np.log(np.expm1(0.01))), jnp.float32), 'A_log': jnp.log(jnp.linspace(1.0, 16.0, H_M)).astype(jnp.float32), 'D_skip': jnp.ones((H_M,), jnp.float32), 'gnorm_w': jnp.ones((D_INNER,), jnp.float32), 'out_proj_w': s * jax.random.normal(ks[4], (D_INNER, D), jnp.float32), 'ca_ln_w': jnp.ones((D,), jnp.float32), 'ca_ln_b': jnp.zeros((D,), jnp.float32), 'Wq': s * jax.random.normal(ks[5], (D, D), jnp.float32), 'Wk': s * jax.random.normal(ks[6], (D, D), jnp.float32), 'Wv': s * jax.random.normal(ks[7], (D, D), jnp.float32), 'Wo': s * jax.random.normal(ks[8], (D, D), jnp.float32)}
    _L3_xattn_all = _L3_xattn_setup()
    _L3_xattn_in = {k: v for k, v in _L3_xattn_all.items() if k in ('m_norm_w', 'in_proj_w', 'conv_w', 'conv_b', 'dt_bias', 'A_log', 'D_skip', 'gnorm_w', 'out_proj_w', 'ca_ln_w', 'ca_ln_b', 'Wq', 'Wk', 'Wv', 'Wo')}
    del _L3_xattn_all
    return {'x': x, 'ctx_1024': ctx_1024, 'mask_1xS2_bf0': mask_1xS2_bf0, 'L0_xattn_norm1_scale': _L0_xattn_in['norm1_scale'], 'L0_xattn_norm2_scale': _L0_xattn_in['norm2_scale'], 'L0_xattn_Wq': _L0_xattn_in['Wq'], 'L0_xattn_bq': _L0_xattn_in['bq'], 'L0_xattn_Wk': _L0_xattn_in['Wk'], 'L0_xattn_bk': _L0_xattn_in['bk'], 'L0_xattn_Wv': _L0_xattn_in['Wv'], 'L0_xattn_bv': _L0_xattn_in['bv'], 'L0_xattn_Wz': _L0_xattn_in['Wz'], 'L0_xattn_bz': _L0_xattn_in['bz'], 'L0_xattn_Wgz': _L0_xattn_in['Wgz'], 'L0_xattn_bgz': _L0_xattn_in['bgz'], 'L0_xattn_Wgh': _L0_xattn_in['Wgh'], 'L0_xattn_bgh': _L0_xattn_in['bgh'], 'L0_xattn_Wg1': _L0_xattn_in['Wg1'], 'L0_xattn_bg1': _L0_xattn_in['bg1'], 'L0_xattn_Wg2': _L0_xattn_in['Wg2'], 'L0_xattn_bg2': _L0_xattn_in['bg2'], 'L0_xattn_Wgc1': _L0_xattn_in['Wgc1'], 'L0_xattn_bgc1': _L0_xattn_in['bgc1'], 'L0_xattn_Wgc2': _L0_xattn_in['Wgc2'], 'L0_xattn_bgc2': _L0_xattn_in['bgc2'], 'L0_xattn_Awq': _L0_xattn_in['Awq'], 'L0_xattn_abq': _L0_xattn_in['abq'], 'L0_xattn_Awk': _L0_xattn_in['Awk'], 'L0_xattn_abk': _L0_xattn_in['abk'], 'L0_xattn_Awv': _L0_xattn_in['Awv'], 'L0_xattn_abv': _L0_xattn_in['abv'], 'L0_xattn_Awo': _L0_xattn_in['Awo'], 'L0_xattn_abo': _L0_xattn_in['abo'], 'L0_xattn_Wf1': _L0_xattn_in['Wf1'], 'L0_xattn_bf1': _L0_xattn_in['bf1'], 'L0_xattn_Wf2': _L0_xattn_in['Wf2'], 'L0_xattn_bf2': _L0_xattn_in['bf2'], 'L1_xattn_norm1_w': _L1_xattn_in['norm1_w'], 'L1_xattn_norm1_b': _L1_xattn_in['norm1_b'], 'L1_xattn_norm2_w': _L1_xattn_in['norm2_w'], 'L1_xattn_norm2_b': _L1_xattn_in['norm2_b'], 'L1_xattn_norm3_w': _L1_xattn_in['norm3_w'], 'L1_xattn_norm3_b': _L1_xattn_in['norm3_b'], 'L1_xattn_gamma1': _L1_xattn_in['gamma1'], 'L1_xattn_gamma2': _L1_xattn_in['gamma2'], 'L1_xattn_fc1_w': _L1_xattn_in['fc1_w'], 'L1_xattn_fc1_b': _L1_xattn_in['fc1_b'], 'L1_xattn_fc2_w': _L1_xattn_in['fc2_w'], 'L1_xattn_fc2_b': _L1_xattn_in['fc2_b'], 'L2_xattn_Wq': _L2_xattn_in['Wq'], 'L2_xattn_bq': _L2_xattn_in['bq'], 'L2_xattn_Wk': _L2_xattn_in['Wk'], 'L2_xattn_bk': _L2_xattn_in['bk'], 'L2_xattn_Wv': _L2_xattn_in['Wv'], 'L2_xattn_bv': _L2_xattn_in['bv'], 'L2_xattn_Wo': _L2_xattn_in['Wo'], 'L2_xattn_ln_gamma': _L2_xattn_in['ln_gamma'], 'L2_xattn_ln_beta': _L2_xattn_in['ln_beta'], 'L3_xattn_m_norm_w': _L3_xattn_in['m_norm_w'], 'L3_xattn_in_proj_w': _L3_xattn_in['in_proj_w'], 'L3_xattn_conv_w': _L3_xattn_in['conv_w'], 'L3_xattn_conv_b': _L3_xattn_in['conv_b'], 'L3_xattn_dt_bias': _L3_xattn_in['dt_bias'], 'L3_xattn_A_log': _L3_xattn_in['A_log'], 'L3_xattn_D_skip': _L3_xattn_in['D_skip'], 'L3_xattn_gnorm_w': _L3_xattn_in['gnorm_w'], 'L3_xattn_out_proj_w': _L3_xattn_in['out_proj_w'], 'L3_xattn_ca_ln_w': _L3_xattn_in['ca_ln_w'], 'L3_xattn_ca_ln_b': _L3_xattn_in['ca_ln_b'], 'L3_xattn_Wq': _L3_xattn_in['Wq'], 'L3_xattn_Wk': _L3_xattn_in['Wk'], 'L3_xattn_Wv': _L3_xattn_in['Wv'], 'L3_xattn_Wo': _L3_xattn_in['Wo']}

def reference(x, ctx_1024, mask_1xS2_bf0, L0_xattn_norm1_scale, L0_xattn_norm2_scale, L0_xattn_Wq, L0_xattn_bq, L0_xattn_Wk, L0_xattn_bk, L0_xattn_Wv, L0_xattn_bv, L0_xattn_Wz, L0_xattn_bz, L0_xattn_Wgz, L0_xattn_bgz, L0_xattn_Wgh, L0_xattn_bgh, L0_xattn_Wg1, L0_xattn_bg1, L0_xattn_Wg2, L0_xattn_bg2, L0_xattn_Wgc1, L0_xattn_bgc1, L0_xattn_Wgc2, L0_xattn_bgc2, L0_xattn_Awq, L0_xattn_abq, L0_xattn_Awk, L0_xattn_abk, L0_xattn_Awv, L0_xattn_abv, L0_xattn_Awo, L0_xattn_abo, L0_xattn_Wf1, L0_xattn_bf1, L0_xattn_Wf2, L0_xattn_bf2, L1_xattn_norm1_w, L1_xattn_norm1_b, L1_xattn_norm2_w, L1_xattn_norm2_b, L1_xattn_norm3_w, L1_xattn_norm3_b, L1_xattn_gamma1, L1_xattn_gamma2, L1_xattn_fc1_w, L1_xattn_fc1_b, L1_xattn_fc2_w, L1_xattn_fc2_b, L2_xattn_Wq, L2_xattn_bq, L2_xattn_Wk, L2_xattn_bk, L2_xattn_Wv, L2_xattn_bv, L2_xattn_Wo, L2_xattn_ln_gamma, L2_xattn_ln_beta, L3_xattn_m_norm_w, L3_xattn_in_proj_w, L3_xattn_conv_w, L3_xattn_conv_b, L3_xattn_dt_bias, L3_xattn_A_log, L3_xattn_D_skip, L3_xattn_gnorm_w, L3_xattn_out_proj_w, L3_xattn_ca_ln_w, L3_xattn_ca_ln_b, L3_xattn_Wq, L3_xattn_Wk, L3_xattn_Wv, L3_xattn_Wo):
    import jax
    import jax.numpy as jnp

    def _L0_xattn_ref(x, mem_k, mem_v, norm1_scale, norm2_scale, Wq, bq, Wk, bk, Wv, bv, Wz, bz, Wgz, bgz, Wgh, bgh, Wg1, bg1, Wg2, bg2, Wgc1, bgc1, Wgc2, bgc2, Awq, abq, Awk, abk, Awv, abv, Awo, abo, Wf1, bf1, Wf2, bf2):
        import jax, jax.numpy as jnp
        import numpy as np
        EPS = 1e-06

        def _rms(x, scale):
            return x * scale * jax.lax.rsqrt(jnp.mean(x * x, axis=-1, keepdims=True) + EPS)

        def _forward(x, mem_k, mem_v, norm1_scale, norm2_scale, Wq, bq, Wk, bk, Wv, bv, Wz, bz, Wgz, bgz, Wgh, bgh, Wg1, bg1, Wg2, bg2, Wgc1, bgc1, Wgc2, bgc2, Awq, abq, Awk, abk, Awv, abv, Awo, abo, Wf1, bf1, Wf2, bf2):
            B, S, D = x.shape
            M = mem_k.shape[1]
            H = 8
            hd = D // H
            x_norm = _rms(x, norm1_scale)
            q = x_norm @ Wq + bq
            k = x_norm @ Wk + bk
            v = x_norm @ Wv + bv
            z = x_norm @ Wz + bz
            gamma_base = jax.nn.sigmoid(jax.nn.gelu(z @ Wg1 + bg1) @ Wg2 + bg2)
            gamma_mod = jax.nn.sigmoid(jax.nn.gelu(k @ Wgc1 + bgc1) @ Wgc2 + bgc2)
            gamma = jnp.clip(gamma_base * gamma_mod, 1e-06, 1.0 - 1e-06)

            def step(h_prev, zt_gt):
                z_t, g_t = zt_gt
                gate = jax.nn.sigmoid(z_t @ Wgz + bgz + h_prev @ Wgh + bgh)
                h_tilde = (1.0 - gate) * h_prev + gate * z_t
                h_t = h_tilde + g_t * h_prev
                return (h_t, h_t)
            h0 = jnp.zeros((B, D), dtype=x.dtype)
            z_T = jnp.swapaxes(z, 0, 1)
            gamma_T = jnp.swapaxes(gamma, 0, 1)
            _, h_seq_T = jax.lax.scan(step, h0, (z_T, gamma_T))
            h_seq = jnp.swapaxes(h_seq_T, 0, 1)
            qh = (q @ Awq + abq).reshape(B, S, H, hd)
            kh = (mem_k @ Awk + abk).reshape(B, M, H, hd)
            vh = (mem_v @ Awv + abv).reshape(B, M, H, hd)
            scores = jnp.einsum('bshd,bmhd->bhsm', qh, kh) / jnp.sqrt(jnp.asarray(hd, x.dtype))
            probs = jax.nn.softmax(scores, axis=-1)
            mem_out = jnp.einsum('bhsm,bmhd->bshd', probs, vh).reshape(B, S, D) @ Awo + abo
            combined = h_seq + mem_out + v * 0.1
            x_res = x + combined
            x_norm2 = _rms(x_res, norm2_scale)
            ffn = jax.nn.gelu(x_norm2 @ Wf1 + bf1) @ Wf2 + bf2
            return x_res + ffn
        return _forward(x, mem_k, mem_v, norm1_scale, norm2_scale, Wq, bq, Wk, bk, Wv, bv, Wz, bz, Wgz, bgz, Wgh, bgh, Wg1, bg1, Wg2, bg2, Wgc1, bgc1, Wgc2, bgc2, Awq, abq, Awk, abk, Awv, abv, Awo, abo, Wf1, bf1, Wf2, bf2)

    def _L1_xattn_ref(input_features, query_feature, norm1_w, norm1_b, norm2_w, norm2_b, norm3_w, norm3_b, gamma1, gamma2, fc1_w, fc1_b, fc2_w, fc2_b):
        import jax, jax.numpy as jnp
        import numpy as np
        EMBED_DIM = 256
        LN_EPS = 1e-05

        def _layernorm(x, w, b):
            m = jnp.mean(x, axis=-1, keepdims=True)
            v = jnp.mean(jnp.square(x - m), axis=-1, keepdims=True)
            return (x - m) * jax.lax.rsqrt(v + LN_EPS) * w + b

        def _attention(q, k, v, scale):
            scores = jnp.einsum('bqd,bkd->bqk', q, k) * scale
            probs = jax.nn.softmax(scores, axis=-1)
            return jnp.einsum('bqk,bkd->bqd', probs, v)
        scale = EMBED_DIM ** (-0.5)
        norm_X = _layernorm(input_features, norm1_w, norm1_b)
        norm_F_L = _layernorm(query_feature, norm2_w, norm2_b)
        attended = _attention(norm_F_L, norm_X, norm_X, scale)
        h = jax.nn.gelu(attended @ fc1_w.T + fc1_b, approximate=False)
        cross_attended = h @ fc2_w.T + fc2_b
        norm_cross = _layernorm(cross_attended, norm3_w, norm3_b)
        self_attended = _attention(norm_cross, norm_cross, norm_cross, scale)
        skip_connect = cross_attended + gamma1 * self_attended
        return norm_F_L + gamma2 * skip_connect

    def _L2_xattn_ref(query_seq, key_value_seq, Wq, bq, Wk, bk, Wv, bv, Wo, ln_gamma, ln_beta):
        import jax, jax.numpy as jnp
        import numpy as np
        HEAD_NUM = 16
        DIM = 256
        B, SQ, D = query_seq.shape
        H = HEAD_NUM
        hd = D // H
        Q = query_seq @ Wq + bq
        K = key_value_seq @ Wk + bk
        V = key_value_seq @ Wv + bv
        Q = Q.reshape(B, SQ, H, hd).transpose(0, 2, 1, 3)
        K = K.reshape(B, -1, H, hd).transpose(0, 2, 1, 3)
        V = V.reshape(B, -1, H, hd).transpose(0, 2, 1, 3)
        scores = jnp.einsum('bhqd,bhkd->bhqk', Q, K) / jnp.sqrt(jnp.float32(hd))
        attn = jax.nn.softmax(scores, axis=-1)
        ctx = jnp.einsum('bhqk,bhkd->bhqd', attn, V)
        ctx = ctx.transpose(0, 2, 1, 3).reshape(B, SQ, D)
        attended = ctx @ Wo
        x = query_seq + attended
        mu = jnp.mean(x, axis=-1, keepdims=True)
        var = jnp.var(x, axis=-1, keepdims=True)
        y = (x - mu) * jax.lax.rsqrt(var + 1e-05) * ln_gamma + ln_beta
        return y

    def _L3_xattn_ref(x, encoder_out, encoder_padding_mask, m_norm_w, in_proj_w, conv_w, conv_b, dt_bias, A_log, D_skip, gnorm_w, out_proj_w, ca_ln_w, ca_ln_b, Wq, Wk, Wv, Wo):
        import jax, jax.numpy as jnp
        import numpy as np
        D = 256
        D_STATE = 128
        N_HEADS = 8
        D_INNER = 2 * D
        HEADDIM = 64
        H_M = D_INNER // HEADDIM
        D_CONV = 4
        CONV_DIM = D_INNER + 2 * D_STATE
        D_IN_PROJ = 2 * D_INNER + 2 * D_STATE + H_M
        B = 1
        LQ = 256
        LK = 512
        EPS = 1e-05

        def _rms(x, w):
            return x * jax.lax.rsqrt(jnp.mean(x * x, axis=-1, keepdims=True) + EPS) * w

        def _ln(x, w, b):
            mu = jnp.mean(x, axis=-1, keepdims=True)
            v = jnp.mean((x - mu) ** 2, axis=-1, keepdims=True)
            return (x - mu) * jax.lax.rsqrt(v + EPS) * w + b

        def _mamba2_block(x, norm_w, in_proj_w, conv_w, conv_b, dt_bias, A_log, D_skip, gnorm_w, out_proj_w):
            b, L, _ = x.shape
            resid = x
            zxbcdt = _rms(x, norm_w) @ in_proj_w
            z = zxbcdt[..., :D_INNER]
            xBC = zxbcdt[..., D_INNER:D_INNER + CONV_DIM]
            dt = jax.nn.softplus(zxbcdt[..., -H_M:] + dt_bias)
            padded = jnp.pad(xBC, ((0, 0), (D_CONV - 1, 0), (0, 0)))
            conv = conv_b + sum((padded[:, k:k + L, :] * conv_w[:, k] for k in range(D_CONV)))
            xBC = jax.nn.silu(conv)
            xh = xBC[..., :D_INNER].reshape(b, L, H_M, HEADDIM)
            Bm = xBC[..., D_INNER:D_INNER + D_STATE]
            Cm = xBC[..., D_INNER + D_STATE:]
            A = -jnp.exp(A_log)
            decay = jnp.exp(dt * A)
            dbx = dt[..., None] * xh

            def step(h, inp):
                dec, u, bt, ct = inp
                h = h * dec[:, :, None, None] + u[..., None] * bt[:, None, None, :]
                y = jnp.einsum('bhpn,bn->bhp', h, ct)
                return (h, y)
            h0 = jnp.zeros((b, H_M, HEADDIM, D_STATE), x.dtype)
            xs = (decay.transpose(1, 0, 2), dbx.transpose(1, 0, 2, 3), Bm.transpose(1, 0, 2), Cm.transpose(1, 0, 2))
            _, ys = jax.lax.scan(step, h0, xs)
            y = ys.transpose(1, 0, 2, 3) + D_skip[None, None, :, None] * xh
            u = _rms(y.reshape(b, L, D_INNER) * jax.nn.silu(z), gnorm_w)
            return resid + u @ out_proj_w

        def _cross_attention(x, enc, pad_mask, ln_w, ln_b, Wq, Wk, Wv, Wo):
            b, Lq, _ = x.shape
            Lk = enc.shape[1]
            dh = D // N_HEADS
            resid = x
            xn = _ln(x, ln_w, ln_b)
            q = (xn @ Wq).reshape(b, Lq, N_HEADS, dh)
            k = (enc @ Wk).reshape(b, Lk, N_HEADS, dh)
            v = (enc @ Wv).reshape(b, Lk, N_HEADS, dh)
            scores = jnp.einsum('bqhd,bkhd->bhqk', q, k) * np.float32(1.0 / np.sqrt(dh))
            scores = jnp.where(pad_mask[:, None, None, :], jnp.float32(-1000000000.0), scores)
            p = jax.nn.softmax(scores, axis=-1)
            ctx = jnp.einsum('bhqk,bkhd->bqhd', p, v).reshape(b, Lq, D)
            return resid + ctx @ Wo
        h = _mamba2_block(x, m_norm_w, in_proj_w, conv_w, conv_b, dt_bias, A_log, D_skip, gnorm_w, out_proj_w)
        return _cross_attention(h, encoder_out, encoder_padding_mask, ca_ln_w, ca_ln_b, Wq, Wk, Wv, Wo)
    x = _L0_xattn_ref(x, ctx_1024, ctx_1024, L0_xattn_norm1_scale, L0_xattn_norm2_scale, L0_xattn_Wq, L0_xattn_bq, L0_xattn_Wk, L0_xattn_bk, L0_xattn_Wv, L0_xattn_bv, L0_xattn_Wz, L0_xattn_bz, L0_xattn_Wgz, L0_xattn_bgz, L0_xattn_Wgh, L0_xattn_bgh, L0_xattn_Wg1, L0_xattn_bg1, L0_xattn_Wg2, L0_xattn_bg2, L0_xattn_Wgc1, L0_xattn_bgc1, L0_xattn_Wgc2, L0_xattn_bgc2, L0_xattn_Awq, L0_xattn_abq, L0_xattn_Awk, L0_xattn_abk, L0_xattn_Awv, L0_xattn_abv, L0_xattn_Awo, L0_xattn_abo, L0_xattn_Wf1, L0_xattn_bf1, L0_xattn_Wf2, L0_xattn_bf2)
    x = _L1_xattn_ref(ctx_1024, x, L1_xattn_norm1_w, L1_xattn_norm1_b, L1_xattn_norm2_w, L1_xattn_norm2_b, L1_xattn_norm3_w, L1_xattn_norm3_b, L1_xattn_gamma1, L1_xattn_gamma2, L1_xattn_fc1_w, L1_xattn_fc1_b, L1_xattn_fc2_w, L1_xattn_fc2_b)
    x = _L2_xattn_ref(x, ctx_1024, L2_xattn_Wq, L2_xattn_bq, L2_xattn_Wk, L2_xattn_bk, L2_xattn_Wv, L2_xattn_bv, L2_xattn_Wo, L2_xattn_ln_gamma, L2_xattn_ln_beta)
    x = _L3_xattn_ref(x, ctx_1024, mask_1xS2_bf0, L3_xattn_m_norm_w, L3_xattn_in_proj_w, L3_xattn_conv_w, L3_xattn_conv_b, L3_xattn_dt_bias, L3_xattn_A_log, L3_xattn_D_skip, L3_xattn_gnorm_w, L3_xattn_out_proj_w, L3_xattn_ca_ln_w, L3_xattn_ca_ln_b, L3_xattn_Wq, L3_xattn_Wk, L3_xattn_Wv, L3_xattn_Wo)
    return x

_drawn_inputs = setup_inputs


def setup_inputs(seed=0):
    import zlib

    import numpy as np

    out = dict(_drawn_inputs(seed))
    spreads = {'L0_xattn_norm1_scale': (1.0, 0.2),
     'L0_xattn_norm2_scale': (1.0, 0.2),
     'L0_xattn_bq': (0.0, 0.1),
     'L0_xattn_bk': (0.0, 0.1),
     'L0_xattn_bv': (0.0, 0.1),
     'L0_xattn_bz': (0.0, 0.1),
     'L0_xattn_bgz': (0.0, 0.1),
     'L0_xattn_bgh': (0.0, 0.1),
     'L0_xattn_bg1': (0.0, 0.1),
     'L0_xattn_bg2': (0.0, 0.1),
     'L0_xattn_bgc1': (0.0, 0.1),
     'L0_xattn_bgc2': (0.0, 0.1),
     'L0_xattn_abq': (0.0, 0.1),
     'L0_xattn_abk': (0.0, 0.1),
     'L0_xattn_abv': (0.0, 0.1),
     'L0_xattn_abo': (0.0, 0.1),
     'L0_xattn_bf1': (0.0, 0.1),
     'L0_xattn_bf2': (0.0, 0.1),
     'L2_xattn_ln_gamma': (1.0, 0.2),
     'L2_xattn_ln_beta': (0.0, 0.1),
     'L3_xattn_m_norm_w': (1.0, 0.2),
     'L3_xattn_conv_b': (0.0, 0.1),
     'L3_xattn_dt_bias': (-4.600165843963623, 0.2),
     'L3_xattn_D_skip': (1.0, 0.2),
     'L3_xattn_gnorm_w': (1.0, 0.2),
     'L3_xattn_ca_ln_w': (1.0, 0.2),
     'L3_xattn_ca_ln_b': (0.0, 0.1)}
    factors = {}
    for name, (base, spread) in spreads.items():
        noise = np.random.default_rng([zlib.crc32(name.encode()), seed]).standard_normal(out[name].shape)
        drawn = base * np.exp(spread * noise) if base else spread * noise
        out[name] = jnp.asarray(drawn.astype(out[name].dtype))
    for name, factor in factors.items():
        out[name] = (out[name] * factor).astype(out[name].dtype)
    return out
```

```python
from contextlib import ExitStack

import numpy as np

import concourse.bass as bass
from concourse import mybir

F32 = mybir.dt.float32
BF16 = mybir.dt.bfloat16
I32 = mybir.dt.int32
U8 = mybir.dt.uint8
ALU = mybir.AluOpType
ACT = mybir.ActivationFunctionType
AX = mybir.AxisListType

P = 128
B, S, D, M = 2, 1024, 256, 77
DC = D // P
T = 512
J = S // T
SUB = T // P
MP = 96
SLOTS = 8
HALF = 4 * M
FF = 1024
DQ = D // 4
DI, DS, HM, PD = 512, 128, 8, 64
XBC = (DI + 2 * DS) // P
TAPS = 4
HEADS0, HEADS2, HEADS3 = 8, 16, 8
SWEEPS_BF, SWEEPS_F = 3, 3
FALLBACK_TEST = ALU.is_lt
TOL = 2.0 ** -19


def layout():
    vec, at = {}, 0
    for name, n in (("n1", 2), ("n2", 2), ("bq", 2), ("abq", 2), ("bk", 2), ("bz", 2), ("bv", 2), ("abo", 2),
                    ("bg1c", 1), ("bgz", 2), ("bgh", 2), ("bg2", 2), ("bgc2", 2), ("abk0", 2), ("abv0", 2),
                    ("bf1", 8), ("bf2", 2), ("l1w1", 2), ("l1b1", 2), ("l1w2", 2), ("l1b2", 2), ("fc1b", 1),
                    ("bq2", 2), ("bk2", 2), ("bv2", 2), ("lg2", 2), ("lb2", 2), ("mnw", 2), ("convw", 24),
                    ("convb", 6), ("dtb", 1), ("alog", 1), ("dskip", 8), ("gnw", 4), ("caw", 2), ("cab", 2)):
        vec[name] = (at, at + n)
        at += n
    mats = {}
    at0 = 0
    for name, n in (("Awk", 512), ("Awv", 512), ("WqT", 512), ("Awq", 512), ("WkT", 512), ("Wgc1", 128),
                    ("WzT", 512), ("Wg1", 128), ("Wz", 512), ("Wgz", 512), ("Wg2c", 256), ("Wgh", 512),
                    ("Wv", 512), ("Awo", 512), ("Wf1", 2048), ("Wf2", 2048)):
        mats[name] = (0, at0, at0 + n)
        at0 += n
    at1 = 0
    for name, n in (("Win", 2 * 1288), ("Wout", 1024), ("Wq3", 512), ("Wk3", 512), ("Wv3", 512), ("Wo3", 512)):
        mats[name] = (1, at1, at1 + n)
        at1 += n
    at2 = 0
    for name, n in (("Wq2", 512), ("Wk2", 512), ("Wv2", 512), ("Wo2", 512), ("fc1T", 8)):
        mats[name] = (2, at2, at2 + n)
        at2 += n
    return vec, at, mats, (at0, at1, at2)


CONST = {"ident": (0, 128), "mean": (128, 256), "last": (256, 384), "m32": (384, 388), "m16": (388, 396),
         "future": (396, 524), "ones": (524, 652), "eps6": (652, 653), "eps5": (653, 654), "den": (654, 660)}
NCONST = 660


def constants():
    c = np.zeros((P, NCONST), np.float32)
    p = np.arange(P)

    def put(name, v):
        c[:, CONST[name][0]:CONST[name][1]] = v

    put("ident", np.eye(P))
    put("mean", 1.0 / D)
    put("last", (p == P - 1)[:, None] * np.ones(P))
    put("m32", (p[:, None] // 32 == np.arange(4)) * 32 ** -0.5)
    put("m16", (p[:, None] // 16 == np.arange(8)) * 16 ** -0.5)
    put("future", np.where(p[:, None] > p[None, :], -1e30, 0.0))
    put("ones", 1.0)
    put("eps6", 1e-6)
    put("eps5", 1e-5)
    put("den", (p == 5)[:, None] * np.ones(6))
    rows = np.zeros((8, HM * P + T), np.float32)
    rows[:, :HM * P] = np.repeat(np.eye(8), P, axis=1)
    rows[:, HM * P:] = np.arange(T) % P != 0
    return c, rows


def xattn_stack_kernel(nc, xT, ctxT, mask, vecs, m0, m1, m2, rows6, consts, rowconsts, outT):
    vcol, nvec, mats, sizes = layout()
    with ExitStack() as ctx:
        def sb(name, shape, dt=F32):
            return ctx.enter_context(nc.sbuf_tensor(name, shape, dt))

        sems = {}

        SHARED = (
            (("count", 1), ("s_mm", 2), ("mr_mm", B), ("q3b_mm", 1)),
            (("g_mm", B * J), ("xr_mm", 4 * J), ("b1_sc", B * J), ("den_mm", 2 * B), ("o2_mm", 4 * J), ("dt_mm", B * J), ("y_mm3", 4 * J)),
            (("z_mm", 4 * J), ("q0_mm", 4 * J), ("b1_tr", B * J), ("o6_mm", 2 * B), ("q2_mm", 4 * J), ("z3_mm", 8 * J), ("q3_mm", 4 * J)),
            (("zg_mm", 4 * J), ("f1_mm", 16 * J), ("h4_mm", B * J), ("p1", 8 * J), ("x2_mm", 8), ("xtk_mm", 8 * J)),
            (("gam_mm", 8 * J), ("f2_mm", B * J), ("wu_mm", B * J), ("p2", 16 * J), ("bt_mm", 8 * J)),
            (("hm", 8 * (SWEEPS_BF + SWEEPS_F + 2)), ("var_mm", B * J), ("een_mm", 8 * J)),
            (("pw", 5), ("y_mm", B * J), ("dmm", 8 * J)),
            (("g6_mm", 2), ("ut_mm", B * J), ("y2_mm", 8 * J)),
            (("nf_mm", 1), ("s_new", 8 * J)),
            (("gg", B * J), ("b1_ex", B * J), ("p2e", 16 * J), ("et", B * J)),
            (("gam", 8 * J), ("ff", 16 * J), ("b1_pt", B * J), ("l1p", B * J)),
            (("g", 8 * (SWEEPS_BF + SWEEPS_F + 2)), ("rm", B * J), ("zs", 8 * J)),
            (("z", 4 * J), ("h4", B * J), ("xs", B * J)),
            (("zg", 4 * J), ("b1_sh", B * J), ("dt1", B * J)),
            (("u", 8 * (SWEEPS_BF + SWEEPS_F + 2)), ("b1_ri", B * J), ("dms", 8 * J)),
        )
        before, home = {}, {}
        for group in SHARED:
            n = 0
            for name, comes in group:
                before[name], home[name] = n, "_".join(g[0] for g in group)
                n += comes
        STARTED = {"vector": ("opg", "x1", "utok", "x3", "x4", "y", "xh"), "scalar": ("yy",), "gpsimd": ("u5x", "u6x", "wx")}
        for names in STARTED.values():
            for name in names:
                before[name] = 1

        def begin(eng, engine):
            for name in STARTED[engine]:
                eng.sem_inc(sem(name), 1)

        def sem(name):
            name = home.get(name, name)
            if name not in sems:
                sems[name] = ctx.enter_context(nc.semaphore(name))
            return sems[name]

        def after(name, n):
            return sem(name), n + before.get(name, 0)

        X = sb("X", [P, DC, B, S])
        CX = sb("CX", [P, DC, B * M])
        CN = sb("CN", [P, NCONST])
        RC = sb("RC", [8, HM * P + T])
        VC = sb("VC", [P, nvec])
        WA = sb("WA", [P, sizes[0]])
        WB = sb("WB", [P, sizes[2]])
        R6 = WA[0:6, sizes[1]:sizes[1] + 5 * D].rearrange("p (a n) -> p a n", a=5)
        KB = sb("KB", [P, B, 2, 2 * HALF])
        VB = sb("VB", [P, B, 2, 6, P])
        VS = sb("VS", [M, B, D])
        CB = sb("CB", [P, 32])
        MX = sb("MX", [P, B, 2, SLOTS])
        RS = sb("RS", [P, B, 2, SLOTS])
        ARENA = 26640
        AR = sb("AR", [P, ARENA])
        ps = ctx.enter_context(nc.psum_tensor("ps", [P, 8, 512], F32))

        def cn(name, rows=P):
            return CN[0:rows, CONST[name][0]:CONST[name][1]]

        def v(name, k=0):
            return VC[:, vcol[name][0] + k:vcol[name][0] + k + 1]

        def w(name, chunks):
            which, lo, hi = mats[name]
            return (WA, WA, WB)[which][:, lo:hi].rearrange("p (c n) -> p c n", c=chunks)

        class Carver:

            def __init__(self, at=0):
                self.at = at

            def take(self, *shape, parts=P):
                n = int(np.prod(shape))
                a = AR[0:parts, self.at:self.at + n]
                self.at += n
                assert self.at <= ARENA, self.at
                if len(shape) == 1:
                    return a
                names = "abcdef"[:len(shape)]
                pat = "p (" + " ".join(names) + ") -> p " + " ".join(names)
                return a.rearrange(pat, **{k: s for k, s in zip(names[:-1], shape[:-1])})

        c1 = Carver()
        XN = c1.take(DC, B, S)
        H = c1.take(DC, B, J, T + 1)
        lower = c1.at
        Z = c1.take(DC, B, S)
        ZG = c1.take(DC, B, S)
        OPG = c1.take(DC, B, S)
        sweeps_at = c1.at
        UG = [[c1.take(T) for _ in range(DC)] for _ in range(B)]
        GZ = [[c1.take(T) for _ in range(DC)] for _ in range(B)]
        AA = [[c1.take(T) for _ in range(DC)] for _ in range(B)]
        HB = VB[:, :, :, :, :].rearrange("p a b c d -> p (a b c d)")[:, 0:DC * B * J * (T + 2) // 2].bitcast(BF16).rearrange(
            "p (c b j s) -> p c b j s", c=DC, b=B, j=J)
        WGB = KB[:, :, :, :].rearrange("p a b c -> p (a b c)")[:, 0:DC * D // 2].bitcast(BF16).rearrange(
            "p (c n) -> p c n", c=DC)
        OKC = sb("OKC", [P, 8])
        TOT = sb("TOT", [1, 4])
        FLAG = sb("FLAG", [1, 4], I32)
        UX = sb("UX", [P, 4, DC, B])
        c1b = Carver(sweeps_at)
        SQ = [c1b.take(DC, T) for _ in range(B)]
        RT = [c1b.take(T) for _ in range(B)]
        GG = [c1b.take(T) for _ in range(B)]
        c1c = Carver(DC * B * S)
        GB = [c1c.take(DC, T) for _ in range(B)]
        assert c1c.at <= lower
        c3 = Carver(lower)
        QS = [c3.take(DC, T) for _ in range(B)]
        PT = [c3.take(6, T) for _ in range(B)]
        ST = [c3.take(DC, T) for _ in range(B)]
        PR = [[c3.take(SLOTS, MP) for _ in range(2)] for _ in range(B)]
        XC = [c3.take(DC, T) for _ in range(B)]
        RTB = [c3.take(T) for _ in range(B)]
        FH = [[QS[b][:, k, :] if k < 2 else PT[b][:, k - 2, :] for k in range(8)] for b in range(B)]
        c4 = Carver(c3.at)
        NX = c4.take(DC, B * M)
        NXS = c4.take(DC, B * M)
        NF = c4.take(B, 4)
        FT6 = c4.take(DC, 6)
        ET6 = c4.take(DC, 6)
        UT = c4.take(B, SUB * J, 8)
        MN = c4.take(B, SUB * J)
        c4r = Carver(0)
        F6C = c4r.take(D)
        E6 = c4r.take(D)
        E1 = c4r.take(D)
        C1 = c4r.take(D)
        G6 = c4r.take(64)
        GS = c4r.take(64)
        U5 = c4r.take(B, S)
        UU = c4r.take(B, S)
        YY = c4r.take(B, S)
        assert c4r.at <= lower
        PE1 = [[PT[b][:, k, :] for k in range(4)] for b in range(B)]
        U5S = [PT[b][:, 4, :] for b in range(B)]
        U6S = [PT[b][:, 5, :] for b in range(B)]
        WU = [ST[b][:, 0, :] for b in range(B)]
        RM = [ST[b][:, 1, :] for b in range(B)]
        c7 = Carver(0)
        XBW = XBC * (T + TAPS - 1)
        xb = [c7.take(XBW) for _ in range(B)]
        XB = [a.rearrange("p (c n) -> p c n", c=XBC) for a in xb]
        CV = [c7.take(XBC, T) for _ in range(B)]
        ZS = [c7.take(SUB, DI) for _ in range(B)]
        LAM = [c7.take(T) for _ in range(B)]
        ROWS = [c7.take(T) for _ in range(B)]
        LNG = [c7.take(T) for _ in range(B)]
        RB = [c7.take(HM, P) for _ in range(B)]
        BT = [c7.take(224) for _ in range(B)]
        STATE = [c7.take(DI) for _ in range(B)]
        HIST = [c7.take(XBC, TAPS - 1) for _ in range(B)]
        XN3 = [c7.take(DC, T) for _ in range(B)]
        SSQ = c7.take(B, SUB)
        SSR = c7.take(B, SUB)
        EEN = c7.take(B, HM)
        SQ7 = [CV[b][:, 0:2, :] for b in range(B)]
        RT7 = [CV[b][:, 2, :] for b in range(B)]
        ET = [ZS[b][:, 0, :] for b in range(B)]
        DTV = [ZS[b][:, 1, :] for b in range(B)]
        DM = [xb[b][:, 0:1024].rearrange("p (h n) -> p h n", h=HM) for b in range(B)]
        XTK = [xb[b][:, 1024:1536] for b in range(B)]
        DTX = [xb[b][:, 1536:2048] for b in range(B)]
        WX = [xb[b][:, 2048:2560] for b in range(B)]
        SE = [xb[b][:, 2560:3072] for b in range(B)]
        TOT6 = sb("TOT6", [6, 2])
        MKU = sb("MKU", [P, -(-M // 4)], I32)
        KEEP = sb("KEEP", [P, M])
        NEG = sb("NEG", [P, M])

        class Chain:
            PER = 160

            def __init__(self, eng, name):
                self.eng, self.sem, self.base, self.n, self.j = eng, sem(name), 0, 0, 0

            def link(self, ins):
                self.n += 1
                ins.then_inc(self.sem, 1)
                self.eng.wait_ge(self.sem, self.j * self.PER + (self.base + self.n))

            def enter(self, j):
                self.base += self.n
                self.n, self.j = 0, j

            def turn(self):
                assert self.n < self.PER, self.n
                self.eng.sem_inc(self.sem, self.PER - self.n)

            def leave(self, trips):
                self.base += self.PER * trips
                self.n, self.j = 0, 0

        def mm(out, lhsT, rhs, first=True, last=True):
            return nc.tensor.matmul(out, lhsT, rhs, start=first, stop=last)

        def nk(j, per, k):
            return j * per + (k + 1)

        def n2(j, b):
            return nk(j, B, b)

        def tj(j):
            return bass.ds(j * T, T)

        def feat(w_, c, mo):
            return w_[:, c, mo * P:(mo + 1) * P]

        def bc(a, n, axis):
            a = a.unsqueeze(axis)
            shape = list(a.shape)
            shape[axis] = n
            return a.broadcast_to(shape)

        def bank(b, k):
            return ps[:, 4 * b + k, :]

        BS = range(B)
        vidx = {"CQb": 0, "gcb": 2, "zgb": 3, "xob": 5, "q3b": 7, "A": 9}

        def cb(name, k=0):
            return CB[:, vidx[name] + k:vidx[name] + k + 1]

        CQ = w("WqT", 2)
        CG = w("WkT", 2)

        NORMS = {"r1": 0, "r2": B * J, "cn": 2 * B * J, "l1": 2 * B * J + 1, "x3": 3 * B * J + 1, "r3": 4 * B * J + 1, "l3": 5 * B * J + 1}
        CENTRED = {"cn": 0, "l1": 1, "x3": B * J + 1, "l3": 2 * B * J + 1}
        LAYER = {"a0": 0, "a2": 1, "a3": 2}
        STEPS = {"a0": 0, "a2": 8 * J, "a3": 24 * J}
        CHUNKS = {"a0": 0, "a2": 4 * J, "a3": 8 * J}

        def norm_pe(pe, p, j, src, sq, mean, width=T, bs=BS):
            if mean:
                for b in bs:
                    pe.wait_ge(*after("norm_sum", CENTRED[p] + nk(j, len(bs), b)))
                    mm(bank(b, 0)[:, 0:width], cn("mean"), sq[b][:, 0, 0:width]).then_inc(sem("norm_mean"), 1)
            for b in bs:
                pe.wait_ge(*after("norm_sqs", NORMS[p] + nk(j, len(bs), b)))
                mm(bank(b, 1)[:, 0:width], cn("mean"), sq[b][:, 0, 0:width]).then_inc(sem("norm_ms"), 1)

        def norm_act(act, p, j, src, sq, rt, eps, mean, xc=None, width=T, bs=BS):
            for b in bs:
                if mean:
                    act.wait_ge(*after("norm_xc", CENTRED[p] + nk(j, len(bs), b)))
                nc.scalar.activation(sq[b][:, :, 0:width], xc[b][:, :, 0:width] if mean else src(b), ACT.Square).then_inc(sem("norm_sq"), 1)
            for b in bs:
                act.wait_ge(*after("norm_ms", NORMS[p] + nk(j, len(bs), b)))
                nc.scalar.activation(rt[b][:, 0:width], bank(b, 1)[:, 0:width], ACT.Sqrt, bias=cn(eps)).then_inc(sem("norm_rt"), 1)

        def norm_dve(dve, ch, p, j, src, sq, rt, out, mean, xc=None, width=T, bs=BS):
            if mean:
                for b in bs:
                    nc.vector.tensor_tensor(sq[b][:, 0, 0:width], src(b)[:, 0], src(b)[:, 1], ALU.add).then_inc(sem("norm_sum"), 1)
                for b in bs:
                    dve.wait_ge(*after("norm_mean", CENTRED[p] + nk(j, len(bs), b)))
                    nc.vector.tensor_tensor(xc[b][:, :, 0:width], src(b), bc(bank(b, 0)[:, 0:width], DC, 1), ALU.subtract).then_inc(sem("norm_xc"), 1)
            for b in bs:
                dve.wait_ge(*after("norm_sq", NORMS[p] + nk(j, len(bs), b)))
                nc.vector.tensor_tensor(sq[b][:, 0, 0:width], sq[b][:, 0, 0:width], sq[b][:, 1, 0:width], ALU.add).then_inc(sem("norm_sqs"), 1)
            for b in bs:
                dve.wait_ge(*after("norm_rt", NORMS[p] + nk(j, len(bs), b)))
                ch.link(nc.vector.reciprocal(rt[b][:, 0:width], rt[b][:, 0:width]))
                nc.vector.tensor_tensor(out(b), xc[b][:, :, 0:width] if mean else src(b), bc(rt[b][:, 0:width], DC, 1), ALU.mult).then_inc(sem("norm_xn"), 1)

        def prep_pe(pe, p, wk, wv):
            for g in range(2):
                for c in range(DC):
                    last = mm(ps[:, g, 0:B * M], feat(wk, c, g), CX[:, c, :], c == 0, c == DC - 1)
                last.then_inc(sem("kv_kp"), 1)
            for b in BS:
                for c in range(DC):
                    last = mm(ps[0:M, 2, b * D:(b + 1) * D], CX[:, c, b * M:(b + 1) * M], wv[:, c, :], c == 0, c == DC - 1)
            last.then_inc(sem("kv_vp"), 1)

        def prep_act(act, p):
            act.wait_ge(*after("kv_vp", LAYER[p] + 1))
            nc.scalar.activation(VS[:, :, :].rearrange("m b n -> m (b n)"), ps[0:M, 2, :], ACT.Copy).then_inc(sem("kv_vs"), 1)

        def prep_dve(dve, ch, p, bias, hg, masked=False):
            for g in range(2):
                dve.wait_ge(*after("kv_kp", 2 * LAYER[p] + g + 1))
                for b in BS:
                    out = KB[:, b, g, 0:hg * M].rearrange("p (h m) -> p h m", h=hg)
                    ins = nc.vector.scalar_tensor_tensor(out=out, in0=bc(ps[:, g, b * M:(b + 1) * M], hg, 1), scalar=v(bias, g) if bias else 0.0,
                                                         in1=bc(cn("m32" if hg == 4 else "m16"), M, 2), op0=ALU.add, op1=ALU.mult)
                    if masked:
                        ch.link(ins)
                        ins = nc.vector.tensor_tensor(out, out, bc(KEEP[:, :], hg, 1), ALU.mult)
                    ins.then_inc(sem("kv_kb"), 1)

        def prep_sp(sp, p, hg):
            sp.wait_ge(*after("kv_vz", LAYER[p] + 1))
            sp.wait_ge(*after("kv_vs", LAYER[p] + 1))
            width, n = P // hg, 0
            for h in range(hg):
                m = 0
                while m < M:
                    chunk, part = divmod(MP * h + m, P)
                    k = min(M - m, P - part)
                    for b in BS:
                        sp.dma_start(VB[part:part + k, b, :, chunk, h * width:(h + 1) * width],
                                     VS[m:m + k, b, :].rearrange("m (g n) -> m g n", g=2)[:, :, h * width:(h + 1) * width]
                                     ).then_inc(sem("kv_vb"), 16)
                        n += 1
                    m += k
            return n

        def pieces(hg):
            return B * sum(1 + ((MP * h) // P != (MP * h + M - 1) // P) for h in range(hg))

        def steps(units):
            return [(u, s, b) for u in range(units) for s in range(SUB) for b in BS]

        def attn_pe(pe, p, j, units):
            seq = steps(units)
            per = len(seq)
            pe.wait_ge(*after("kv_kb", 4 * (LAYER[p] + 1)))
            pe.wait_ge(*after("kv_vb", 16 * sum(pieces(h) for h in (4, 8, 4)[:LAYER[p] + 1])))
            done = [0, 0]
            for n in range(per + 2):
                if n < per:
                    u, s, b = seq[n]
                    pe.wait_ge(*after("att_q", CHUNKS[p] + nk(j, 4, 2 * b + 1)))
                    if n >= 2:
                        pe.wait_ge(*after("att_sh", STEPS[p] + nk(j, per, n - 2)))
                    for half in range(2):
                        chunk = half if units == 1 else u
                        cols = slice(0, HALF) if units == 1 else slice(half * HALF, (half + 1) * HALF)
                        last = mm(bank(b, half)[:, 0:HALF], QS[b][:, chunk, s * P:(s + 1) * P], KB[:, b, chunk, cols])
                    last.then_inc(sem("att_sc"), 1)
                if n >= 2:
                    u, s, b = seq[n - 2]
                    pe.wait_ge(*after("att_pn", STEPS[p] + nk(j, per, n - 2)))
                    if n >= 4:
                        pe.wait_ge(*after("att_ta", STEPS[p] + nk(j, per, n - 4)))
                        pe.wait_ge(*after("att_td", STEPS[p] + nk(j, per, n - 4)))
                    if done[b]:
                        pe.wait_ge(*after("att_ctx", CHUNKS[p] + nk(j, 4, ctx_at(units, done[b] - 1, b))))
                    flat = PR[b][((n - 2) // 2) % 2].rearrange("p h m -> p (h m)")
                    for k in range(6):
                        last = nc.tensor.transpose(bank(b, 2 + k // 4)[:, (k % 4) * P:(k % 4 + 1) * P], flat[:, k * P:(k + 1) * P], cn("ident"))
                    last.then_inc(sem("att_tr"), 1)
                    if s == SUB - 1:
                        pe.wait_ge(*after("att_ta", STEPS[p] + nk(j, per, n - 2)))
                        pe.wait_ge(*after("att_td", STEPS[p] + nk(j, per, n - 2)))
                        for g in range(2 if units == 1 else 1):
                            chunks = range(3) if units == 1 else range(6)
                            for k in chunks:
                                last = mm(bank(b, 2 + g), VB[:, b, g if units == 1 else u, k, :], PT[b][:, 3 * g + k, :], k == 0, k == chunks[-1])
                            last.then_inc(sem("att_pv"), 1)
                            done[b] += 1

        def ctx_at(units, k, b):
            return 2 * b + k if units == 1 else 2 * k + b

        def attn_act(act, p, j, units, bias):
            seq = steps(units)
            per = len(seq)
            done = [0, 0]
            for n in range(per + 2):
                if n < per:
                    u, s, b = seq[n]
                    pr = PR[b][(n // 2) % 2][:, :, 0:M]
                    act.wait_ge(*after("att_sh", STEPS[p] + nk(j, per, n)))
                    nc.scalar.activation(pr, pr, ACT.Exp).then_inc(sem("att_ex"), 1)
                if n >= 2:
                    u, s, b = seq[n - 2]
                    act.wait_ge(*after("att_tr", STEPS[p] + nk(j, per, n - 2)))
                    nc.scalar.activation(PT[b][:, 0:4, s * P:(s + 1) * P], bank(b, 2).rearrange("p (k t) -> p k t", k=4), ACT.Copy).then_inc(sem("att_ta"), 1)
                    if s == SUB - 1:
                        for g in range(2 if units == 1 else 1):
                            at = ctx_at(units, done[b], b)
                            act.wait_ge(*after("att_pv", CHUNKS[p] + nk(j, 4, at)))
                            if bias:
                                nc.scalar.activation(ST[b][:, done[b], :], bank(b, 2 + g), ACT.Identity, bias=v(bias, done[b])).then_inc(sem("att_ctx"), 1)
                            else:
                                nc.scalar.activation(ST[b][:, done[b], :], bank(b, 2 + g), ACT.Copy).then_inc(sem("att_ctx"), 1)
                            done[b] += 1

        def attn_dve(dve, ch, p, j, units, masked=False):
            seq = steps(units)
            per = len(seq)
            for n in range(per + 2):
                if n < per:
                    u, s, b = seq[n]
                    k = (n // 2) % 2
                    pr = PR[b][k]
                    sc = ps[:, 4 * b:4 * b + 2, 0:HALF].rearrange("p g (h m) -> p g h m", h=4)
                    pr4 = pr.rearrange("p (g h) m -> p g h m", g=2)[:, :, :, 0:M]
                    mx = MX[:, b, k, :].rearrange("p (g h) -> p g h", g=2)
                    dve.wait_ge(*after("att_sc", STEPS[p] + nk(j, per, n)))
                    if masked:
                        for g in range(2):
                            ins = nc.vector.tensor_tensor(pr4[:, g], sc[:, g], bc(NEG[:, :], 4, 1), ALU.add)
                        ch.link(ins)
                        sc = pr4
                    ch.link(nc.vector.tensor_reduce(mx, sc, AX.X, ALU.max, negate=True))
                    for g in range(2):
                        ins = nc.vector.tensor_tensor(pr4[:, g], sc[:, g], bc(mx[:, g], M, 2), ALU.add)
                    ins.then_inc(sem("att_sh"), 1)
                if 1 <= n <= per:
                    b = seq[n - 1][2]
                    k = ((n - 1) // 2) % 2
                    dve.wait_ge(*after("att_ex", STEPS[p] + nk(j, per, n - 1)))
                    ch.link(nc.vector.tensor_reduce(RS[:, b, k, :], PR[b][k][:, :, 0:M], AX.X, ALU.add))
                    nc.vector.reciprocal(RS[:, b, k, :], RS[:, b, k, :]).then_inc(sem("att_ri"), 1)
                if n >= 2:
                    u, s, b = seq[n - 2]
                    dve.wait_ge(*after("att_tr", STEPS[p] + nk(j, per, n - 2)))
                    nc.vector.tensor_copy(PT[b][:, 4:6, s * P:(s + 1) * P], bank(b, 3)[:, 0:2 * P].rearrange("p (k t) -> p k t", k=2)).then_inc(sem("att_td"), 1)

        def attn_pool(pool, p, j, units):
            seq = steps(units)
            per = len(seq)
            for n, (u, s, b) in enumerate(seq):
                k = (n // 2) % 2
                pr = PR[b][k][:, :, 0:M]
                pool.wait_ge(*after("att_ri", STEPS[p] + nk(j, per, n)))
                nc.gpsimd.tensor_tensor(pr, pr, bc(RS[:, b, k, :], M, 2), ALU.mult).then_inc(sem("att_pn"), 1)

        def lin_pe(pe, sig, j, wname_or_ap, rhs, order, ready=None):
            for b in BS:
                if ready is not None:
                    ready(b)
                for mo in range(DC):
                    for c in range(DC):
                        last = mm(bank(b, order[mo]), feat(wname_or_ap, c, mo), rhs(b, c), c == 0, c == DC - 1)
                    last.then_inc(sem(sig), 1)

        block = ctx.enter_context(nc.Block())

        def xs(b, j):
            return X[:, :, b, tj(j)]

        def cx_src(b):
            return CX[:, :, :]

        @block.sync
        def _(sp):
            sp.dma_start(VC[:, :], vecs).then_inc(sem("ld_vec"), 16)
            sp.dma_start(CN[:, :], consts).then_inc(sem("ld_cn"), 16)
            sp.dma_start(CX[:, :, :].rearrange("p c n -> p (c n)"), ctxT).then_inc(sem("ld_cx"), 16)
            a, z_ = mats["WqT"][1], mats["Awo"][2]
            sp.dma_start(WA[:, a:z_], m0[:, a:z_]).then_inc(sem("ld_w0"), 16)
            sp.dma_start(WA[:, 0:a], m0[:, 0:a]).then_inc(sem("ld_kv0"), 16)
            sp.dma_start(WA[:, z_:sizes[0]], m0[:, z_:sizes[0]]).then_inc(sem("ld_ffn"), 16)
            sp.dma_start(RC[:, :], rowconsts).then_inc(sem("ld_rc"), 16)
            sp.dma_start(WB[:, :], m2).then_inc(sem("ld_w12"), 16)
            sp.dma_start(MKU[:, :], mask.broadcast_to([P, -(-M // 4)])).then_inc(sem("ld_mask"), 16)
            prep_sp(sp, "a0", 4)
            sp.wait_ge(*after("x1", B * J))
            sp.dma_start(WA[0:6, sizes[1]:sizes[1] + 5 * D], rows6).then_inc(sem("ld_r6"), 16)
            sp.dma_start(WA[:, 0:sizes[1]], m1).then_inc(sem("ld_w3"), 16)
            prep_sp(sp, "a2", 8)
            prep_sp(sp, "a3", 4)
            with sp.Fori(0, J) as j:
                for b in BS:
                    sp.wait_ge(*after("y", n2(j, b)))
                    sp.dma_start(outT[:, :, b, tj(j)], X[:, :, b, tj(j)]).then_inc(sem("st"), 16)
            sp.wait_ge(*after("st", 16 * B * J))

        @block.gpsimd
        def _(pool):
            begin(pool, "gpsimd")
            nc.gpsimd.dma_start(X[:, :, :, :].rearrange("p c b s -> p (c b s)"), xT).then_inc(sem("ld_x"), 16)
            def products(j):
                for q in range(2 * B):
                    jj, b = q // B, q % B
                    for mo in range(DC):
                        pool.wait_ge(*after("g", nk(j, 8, 2 * q + mo)))
                        nc.gpsimd.tensor_tensor(GZ[b][mo], UG[b][mo], Z[:, mo, b, jj * T:(jj + 1) * T], ALU.mult).then_inc(sem("gz"), 1)
            with pool.Fori(0, SWEEPS_BF + SWEEPS_F + 2) as j:
                products(j)
            pool.wait_ge(*after("h", 8 * (SWEEPS_BF + SWEEPS_F + 2)))
            pool.wait_ge(*after("decided", 1))
            nc.gpsimd.memset(VB[:, :, :, :, :].rearrange("p a b c d -> p (a b c d)"), 0.0).then_inc(sem("kv_vz"), 1)
            for b in BS:
                for k in range(2):
                    nc.gpsimd.memset(PR[b][k].rearrange("p h m -> p (h m)"), 0.0).then_inc(sem("pr0"), 1)
            with pool.Fori(0, J) as j:
                attn_pool(pool, "a0", j, 1)
            pool.wait_ge(*after("x1", B * J))
            nc.gpsimd.memset(VB[:, :, :, :, :].rearrange("p a b c d -> p (a b c d)"), 0.0).then_inc(sem("kv_vz"), 1)
            for t in (UU, YY):
                nc.gpsimd.memset(t[0:33].rearrange("p b s -> p (b s)"), 0.0).then_inc(sem("uy0"), 1)
            for t in (G6, GS):
                nc.gpsimd.memset(t[0:6], 0.0).then_inc(sem("g60"), 1)
            pool.wait_ge(*after("uy0", 2))
            pool.wait_ge(*after("g60", 2))
            nc.gpsimd.memset(YY[32:33].rearrange("p b s -> p (b s)"), 1.0).then_inc(sem("y1s"), 1)
            for b in BS:
                nc.gpsimd.memset(U5S[b][0:6], 1.0).then_inc(sem("us1"), 1)
                nc.gpsimd.memset(U6S[b][0:6], 1.0).then_inc(sem("us1"), 1)
            pool.wait_ge(*after("y1s", 1))
            pool.wait_ge(*after("us1", 4))
            with pool.Fori(0, J) as j:
                for b in BS:
                    pool.wait_ge(*after("f", nk(j, 4, 2 * b + 1)))
                    pool.wait_ge(*after("ld_x", 16))
                    nc.gpsimd.tensor_copy(X[:, :, b, tj(j)], QS[b]).then_inc(sem("fx"), 1)
                for b in BS:
                    pool.wait_ge(*after("b1_ri", n2(j, b)))
                    pr = PR[b][0][:, 0:4, 0:M]
                    nc.gpsimd.tensor_tensor(pr, pr, bc(RS[:, b, 0, 0:4], M, 2), ALU.mult).then_inc(sem("b1_pn"), 1)
                for b in BS:
                    pool.wait_ge(*after("h4", n2(j, b)))
                    pool.wait_ge(*after("ld_x", 16))
                    nc.gpsimd.tensor_copy(U5[0:6, b, tj(j)], U5S[b][0:6]).then_inc(sem("u5x"), 1)
                for b in BS:
                    pool.wait_ge(*after("u6", n2(j, b)))
                    pool.wait_ge(*after("ld_x", 16))
                    nc.gpsimd.tensor_copy(UU[0:6, b, tj(j)], U6S[b][0:6]).then_inc(sem("u6x"), 1)
            pool.wait_ge(*after("x2", 4 * B))
            with pool.Fori(0, J) as j:
                attn_pool(pool, "a2", j, 2)
            pool.wait_ge(*after("x3", 4 * J))
            for b in BS:
                nc.gpsimd.memset(HIST[b].rearrange("p c n -> p (c n)"), 0.0).then_inc(sem("m0"), 1)
                nc.gpsimd.memset(STATE[b], 0.0).then_inc(sem("m0"), 1)
                nc.gpsimd.memset(ROWS[b][0:96], 0.0).then_inc(sem("m0"), 1)
                nc.gpsimd.memset(LNG[b][0:40], 0.0).then_inc(sem("m0"), 1)
                nc.gpsimd.memset(RB[b][0:40].rearrange("p h n -> p (h n)"), 0.0).then_inc(sem("m0"), 1)
            nc.gpsimd.memset(VB[:, :, :, :, :].rearrange("p a b c d -> p (a b c d)"), 0.0).then_inc(sem("kv_vz"), 1)
            pool.wait_ge(*after("m0", 10))
            pool.wait_ge(*after("kv_vz", 3))
            pool.wait_ge(*after("ld_rc", 16))
            for b in BS:
                nc.gpsimd.memset(LNG[b][32:40], 1.0).then_inc(sem("m1"), 1)
                nc.gpsimd.tensor_copy(RB[b][0:8].rearrange("p h n -> p (h n)"), RC[:, 0:HM * P]).then_inc(sem("m1"), 1)
            with pool.Fori(0, J) as j:
                for s in range(SUB):
                    for b in BS:
                        k = 2 * s + b
                        if s == 0:
                            pool.wait_ge(*after("lam", n2(j, b)))
                        else:
                            pool.wait_ge(*after("dmm", nk(j, 8, k - 2)))
                        pool.wait_ge(*after("wx", j * 8 + k))
                        nc.gpsimd.tensor_tensor(RB[b][32:40], bc(LAM[b][0:8, s * P:(s + 1) * P], HM, 1),
                                                RC[:, 0:HM * P].rearrange("p (h n) -> p h n", h=HM), ALU.mult).then_inc(sem("rb"), 1)
                        pool.wait_ge(*after("rb", nk(j, 8, k)))
                        pool.wait_ge(*after("xtk", nk(j, 8, k)))
                        pool.wait_ge(*after("bt", nk(j, 8, k)))
                        x3 = XTK[b].rearrange("p (h n) -> p h n", h=HM)
                        nc.gpsimd.tensor_tensor(WX[b].rearrange("p (h n) -> p h n", h=HM), x3, bc(BT[b][:, P + 64:P + 72], PD, 2), ALU.mult).then_inc(sem("wx"), 1)
            pool.wait_ge(*after("x4", B * J))
            for b in BS:
                for k in range(2):
                    nc.gpsimd.memset(PR[b][k].rearrange("p h m -> p (h m)"), 0.0).then_inc(sem("pr0"), 1)
            with pool.Fori(0, J) as j:
                attn_pool(pool, "a3", j, 1)

        @block.tensor
        def _(pe):
            pe.wait_ge(*after("ld_cn", 16))
            pe.wait_ge(*after("ld_vec", 16))
            pe.wait_ge(*after("ld_w0", 16))
            wq, wk_, wz = w("WqT", 2), w("WkT", 2), w("WzT", 2)
            for m in range(DC):
                for c in range(DC):
                    last = mm(ps[:, m, 0:D], wq[:, c, m * P:(m + 1) * P], w("Awq", 2)[:, c, :], c == 0, c == DC - 1)
                last.then_inc(sem("pw"), 1)
            for m in range(DC):
                for c in range(DC):
                    mm(ps[:, 2 + m, 0:64], wz[:, c, m * P:(m + 1) * P], w("Wg1", 2)[:, c, :], c == 0, c == DC - 1)
                for c in range(DC):
                    last = mm(ps[:, 2 + m, 64:128], wk_[:, c, m * P:(m + 1) * P], w("Wgc1", 2)[:, c, :], c == 0, c == DC - 1)
                last.then_inc(sem("pw"), 1)
            for mo in range(DC):
                for c in range(DC):
                    last = mm(ps[:, 4, mo:mo + 1], feat(w("Awq", 2), c, mo), v("bq", c), c == 0, c == DC - 1)
            for c in range(DC):
                mm(ps[0:64, 5, 0:1], w("Wg1", 2)[:, c, :], v("bz", c), c == 0, c == DC - 1)
            for c in range(DC):
                last = mm(ps[64:128, 5, 0:1], w("Wgc1", 2)[:, c, :], v("bk", c), c == 0, c == DC - 1)
            last.then_inc(sem("pw"), 1)
            pe.wait_ge(*after("wready", 1))
            with pe.Fori(0, J) as j:
                pe.wait_ge(*after("opg", j * B))
                norm_pe(pe, "r1", j, None, SQ, False)
                lin_pe(pe, "z_mm", j, w("Wz", 2), lambda b, c: XN[:, c, b, tj(j)], (2, 3), lambda b: pe.wait_ge(*after("norm_xn", NORMS["r1"] + n2(j, b))))
                for b in BS:
                    for c in range(DC):
                        last = mm(bank(b, 1), CG[:, c, 0:P], XN[:, c, b, tj(j)], c == 0, c == DC - 1)
                    last.then_inc(sem("g_mm"), 1)
                for b in BS:
                    pe.wait_ge(*after("z", nk(j, 4, 2 * b + 1)))
                    for mo in range(DC):
                        for c in range(DC):
                            last = mm(bank(b, 2 * mo), feat(w("Wgz", 2), c, mo), Z[:, c, b, tj(j)], c == 0, c == DC - 1)
                        last.then_inc(sem("zg_mm"), 1)
                for b in BS:
                    pe.wait_ge(*after("gg", n2(j, b)))
                    for k, (lo, mo, to) in enumerate(((0, 0, 3), (0, 1, 1), (64, 0, 0), (64, 1, 2))):
                        if k == 2:
                            pe.wait_ge(*after("zg", nk(j, 4, 2 * b + 1)))
                        mm(bank(b, to), WA[lo:lo + 64, mats["Wg2c"][1] + mo * P:mats["Wg2c"][1] + (mo + 1) * P], GG[b][lo:lo + 64, :]).then_inc(sem("gam_mm"), 1)

            pe.wait_ge(*after("opg", B * J))

            def sweep(j, hin, wgt):
                for q in range(2 * B):
                    jj, b = q // B, q % B
                    pe.wait_ge(*after("h", nk(j, 8, 2 * q + 1)))
                    for mo in range(DC):
                        for c in range(DC):
                            last = mm(bank(b, 2 * jj + mo), wgt[:, c, mo * P:(mo + 1) * P], hin[:, c, b, jj, 0:T], c == 0, c == DC - 1)
                        last.then_inc(sem("hm"), 1)

            with pe.Fori(0, SWEEPS_BF) as j:
                sweep(j, HB, WGB)
            sweep(SWEEPS_BF, HB, WGB)
            with pe.Fori(0, SWEEPS_F) as j:
                sweep(j + (SWEEPS_BF + 1), H, w("Wgh", 2))
            sweep(SWEEPS_BF + SWEEPS_F + 1, H, w("Wgh", 2))
            pe.wait_ge(*after("okc", 8))
            mm(ps[0:1, 0, 0:8], cn("ones")[:, 0:1], OKC[:, :]).then_inc(sem("count"), 1)
            pe.wait_ge(*after("flag", 1))
            need = pe.value_load(FLAG[0:1, 0:1], min_val=0, max_val=1)
            with pe.If(need == 1):
                for jj in range(J):
                    with pe.Fori(0, T) as t:
                        pe.wait_ge(*after("xh", t + jj * (T + 1)))
                        for mo in range(DC):
                            for c in range(DC):
                                last = mm(ps[:, 1, mo * B:(mo + 1) * B], feat(w("Wgh", 2), c, mo), H[:, c, :, jj, bass.ds(t, 1)].rearrange("p b s -> p (b s)"), c == 0, c == DC - 1)
                        last.then_inc(sem("xm"), 1)

            pe.wait_ge(*after("decided", 1))
            pe.wait_ge(*after("ld_kv0", 16))
            pe.wait_ge(*after("ld_cx", 16))
            pe.wait_ge(*after("ld_ffn", 16))
            prep_pe(pe, "a0", w("Awk", 2), w("Awv", 2))
            pe.wait_ge(*after("kv_kb", 4 * (LAYER["a0"] + 1)))
            pe.wait_ge(*after("kv_vs", LAYER["a0"] + 1))
            with pe.Fori(0, J) as j:
                pe.wait_ge(*after("x1", j * B))
                lin_pe(pe, "q0_mm", j, CQ, lambda b, c: XN[:, c, b, tj(j)], (0, 1))
                attn_pe(pe, "a0", j, 1)
                for b in BS:
                    pe.wait_ge(*after("att_ctx", CHUNKS["a0"] + nk(j, 4, 2 * b + 1)))
                    for mo in range(DC):
                        for c in range(DC):
                            mm(bank(b, mo), feat(w("Awo", 2), c, mo), ST[b][:, c, :], c == 0, False)
                        for c in range(DC):
                            last = mm(bank(b, mo), feat(w("Wv", 2), c, mo), XN[:, c, b, tj(j)], False, c == DC - 1)
                        last.then_inc(sem("xr_mm"), 1)
                for b in BS:
                    pe.wait_ge(*after("xr", n2(j, b)))
                norm_pe(pe, "r2", j, None, ST, False)
                for k in range(9):
                    for b in BS:
                        if k < 8:
                            if k == 0:
                                pe.wait_ge(*after("norm_xn", NORMS["r2"] + n2(j, b)))
                            if k >= 2:
                                pe.wait_ge(*after("ff", nk(j, 16, 2 * (k - 2) + b)))
                            for c in range(DC):
                                last = mm(bank(b, k % 2), feat(w("Wf1", 2), c, k), XC[b][:, c, :], c == 0, c == DC - 1)
                            last.then_inc(sem("f1_mm"), 1)
                        if k >= 1:
                            pe.wait_ge(*after("ff", nk(j, 16, 2 * (k - 1) + b)))
                            for mo in range(DC):
                                last = mm(bank(b, 2 + mo), feat(w("Wf2", 8), k - 1, mo), FH[b][k - 1], k == 1, k == 8)
                            if k == 8:
                                last.then_inc(sem("f2_mm"), 1)

            pe.wait_ge(*after("x1", B * J))
            norm_pe(pe, "cn", 0, None, [ST[0]], True, B * M, [0])
            pe.wait_ge(*after("f6", 1))
            for c in range(DC):
                last = nc.tensor.transpose(ps[:, 2, 8 * c:8 * c + 6], F6C[0:6, c * P:(c + 1) * P], cn("ident", 6)[:, 0:6])
            last.then_inc(sem("s_mm"), 1)
            pe.wait_ge(*after("e6", 1))
            for c in range(DC):
                last = nc.tensor.transpose(ps[:, 3, 8 * c:8 * c + 6], E6[0:6, c * P:(c + 1) * P], cn("ident", 6)[:, 0:6])
            last.then_inc(sem("s_mm"), 1)
            pe.wait_ge(*after("ft6", 2))
            for t, to in ((FT6, 4), (ET6, 5)):
                for c in range(DC):
                    last = mm(ps[0:6, to, 0:6], t[:, c, :], t[:, c, :], c == 0, c == DC - 1)
                last.then_inc(sem("g6_mm"), 1)
            pe.wait_ge(*after("nxs", 1))
            pe.wait_ge(*after("nx", 2))
            pe.wait_ge(*after("ld_w12", 16))
            for b in BS:
                for c in range(DC):
                    last = mm(ps[0:M, 6, 8 * b:8 * b + 4], NX[:, c, b * M:(b + 1) * M], w("fc1T", 2)[:, c, :], c == 0, c == DC - 1)
            last.then_inc(sem("nf_mm"), 1)
            pe.wait_ge(*after("g6", 2))
            pe.wait_ge(*after("nf", 1))
            with pe.Fori(0, J) as j:
                pe.wait_ge(*after("utok", j * 8))
                pe.wait_ge(*after("yy", j * B))
                norm_pe(pe, "l1", j, None, ST, True)
                for b in BS:
                    pe.wait_ge(*after("f", nk(j, 4, 2 * b + 1)))
                    for s in range(SUB):
                        for c in range(DC):
                            last = mm(bank(b, 2)[:, s * M:(s + 1) * M], QS[b][:, c, s * P:(s + 1) * P], NXS[:, c, b * M:(b + 1) * M], c == 0, c == DC - 1)
                    last.then_inc(sem("b1_sc"), 1)
                for b in BS:
                    pe.wait_ge(*after("b1_pn", n2(j, b)))
                    for s in range(SUB):
                        last = nc.tensor.transpose(bank(b, 3)[0:M, s * P:(s + 1) * P], PR[b][0][:, s, 0:M], cn("ident"))
                    last.then_inc(sem("b1_tr"), 1)
                for b in BS:
                    pe.wait_ge(*after("b1_pt", n2(j, b)))
                    mm(bank(b, 0)[0:4, :], NF[0:M, b, :], PT[b][0:M, 0, :]).then_inc(sem("h4_mm"), 1)
                for b in BS:
                    pe.wait_ge(*after("h4", n2(j, b)))
                    pe.wait_ge(*after("ld_cn", 16))
                    mm(bank(b, 1)[0:64, :], G6[0:6, :], U5S[b][0:6, :]).then_inc(sem("wu_mm"), 1)
                for b in BS:
                    pe.wait_ge(*after("wu", n2(j, b)))
                    pe.wait_ge(*after("ld_cn", 16))
                    mm(bank(b, 2)[0:64, :], cn("ones", 6)[:, 0:64], WU[b][0:6, :]).then_inc(sem("var_mm"), 1)
                for b in BS:
                    pe.wait_ge(*after("u6", n2(j, b)))
                    pe.wait_ge(*after("ld_cn", 16))
                    mm(bank(b, 3)[0:64, :], GS[0:6, :], U6S[b][0:6, :]).then_inc(sem("y_mm"), 1)
                    for s in range(SUB):
                        last = nc.tensor.transpose(bank(b, 0)[:, 8 * s:8 * s + 6], U6S[b][0:6, s * P:(s + 1) * P], cn("ident", 6)[:, 0:6])
                    last.then_inc(sem("ut_mm"), 1)
            pe.wait_ge(*after("u6x", B * J))
            pe.wait_ge(*after("yy", B * J))
            pe.wait_ge(*after("utok", 8 * J))
            for t in range(SUB * J):
                for b in BS:
                    if t >= 2:
                        pe.wait_ge(*after("mn", 2 * (t - 2) + b + 1))
                    for half in range(2):
                        last = mm(bank(b, 2 * (t % 2) + half), UU[0:6, b, t * P:(t + 1) * P], YY[0:6, b, half * T:(half + 1) * T])
                    last.then_inc(sem("p1"), 1)
            for b in BS:
                pe.wait_ge(*after("mn", 2 * (SUB * J - 1) + b + 1))
                for t in range(SUB * J):
                    last = nc.tensor.transpose(bank(b, t // 4)[0:1, (t % 4) * P:(t % 4 + 1) * P], MN[:, b, t:t + 1], cn("ident"))
                last.then_inc(sem("mr_mm"), 1)
            for half in range(2):
                for k in range(SUB * J + 1):
                    for b in BS:
                        n = (half * 8 + k) * 2 + b
                        if k < 8:
                            if k == 0 and half == 0:
                                pe.wait_ge(*after("mrow", b + 1))
                                pe.wait_ge(*after("y1s", 1))
                            if n >= 4:
                                pe.wait_ge(*after("p2e", n - 4 + 1))
                            mm(bank(b, k % 2), YY[0:33, b, k * P:(k + 1) * P], UU[0:33, b, half * T:(half + 1) * T]).then_inc(sem("p2"), 1)
                        if k >= 1:
                            pe.wait_ge(*after("p2e", n - 2 + 1))
                            if k == 1 and half == 1:
                                pe.wait_ge(*after("o6", b + 1))
                            last = mm(bank(b, 2)[0:6, :], UT[:, b, k - 1, 0:6], PE1[b][(k - 1) % 4], k == 1, k == 8)
                            if k == 8:
                                last.then_inc(sem("o6_mm"), 1)
                for b in BS:
                    pe.wait_ge(*after("o6", 2 * half + b + 1))
                    mm(bank(b, 3)[0:6, :], cn("den", 6), RM[b][0:6, :]).then_inc(sem("den_mm"), 1)
                for b in BS:
                    pe.wait_ge(*after("oo", 2 * half + b + 1))
                    for mo in range(DC):
                        if mo == 1:
                            pe.wait_ge(*after("x2", 4 * half + 2 * b + 1))
                        mm(bank(b, 3), E1[0:6, mo * P:(mo + 1) * P], WU[b][0:6, :], True, False)
                        mm(bank(b, 3), C1[0:6, mo * P:(mo + 1) * P], U5[0:6, b, half * T:(half + 1) * T], False, True).then_inc(sem("x2_mm"), 1)

            pe.wait_ge(*after("x2", 4 * B))
            prep_pe(pe, "a2", w("Wk2", 2), w("Wv2", 2))
            pe.wait_ge(*after("kv_kb", 4 * (LAYER["a2"] + 1)))
            pe.wait_ge(*after("kv_vs", LAYER["a2"] + 1))
            with pe.Fori(0, J) as j:
                pe.wait_ge(*after("x3", j * 4))
                lin_pe(pe, "q2_mm", j, w("Wq2", 2), lambda b, c: X[:, c, b, tj(j)], (0, 1))
                attn_pe(pe, "a2", j, 2)
                for b in BS:
                    pe.wait_ge(*after("att_ctx", CHUNKS["a2"] + nk(j, 4, 2 + b)))
                    for mo in range(DC):
                        for c in range(DC):
                            last = mm(bank(b, mo), feat(w("Wo2", 2), c, mo), ST[b][:, c, :], c == 0, c == DC - 1)
                        last.then_inc(sem("o2_mm"), 1)
                for b in BS:
                    pe.wait_ge(*after("o2", nk(j, 4, 2 * b + 1)))
                norm_pe(pe, "x3", j, None, ST, True)

            pe.wait_ge(*after("x3", 4 * J))
            pe.wait_ge(*after("w3ready", 1))
            win = w("Win", 2)
            prep_pe(pe, "a3", w("Wk3", 2), w("Wv3", 2))
            for mo in range(DC):
                for c in range(DC):
                    last = mm(ps[:, 3, mo:mo + 1], feat(w("Wq3", 2), c, mo), v("cab", c), c == 0, c == DC - 1)
            last.then_inc(sem("q3b_mm"), 1)
            pe.wait_ge(*after("q3w", 1))
            pe.wait_ge(*after("kv_kb", 4 * (LAYER["a3"] + 1)))
            pe.wait_ge(*after("kv_vs", LAYER["a3"] + 1))
            with pe.Fori(0, J) as j:
                pe.wait_ge(*after("x4", j * B))
                norm_pe(pe, "r3", j, None, SQ7, False)
                for b in BS:
                    for k in range(XBC):
                        if k == 0:
                            pe.wait_ge(*after("norm_xn", NORMS["r3"] + n2(j, b)))
                        if k >= 4:
                            pe.wait_ge(*after("xbc", nk(j, 12, XBC * b + k - 4)))
                        for c in range(DC):
                            last = mm(bank(b, k % 4), win[:, c, DI + k * P:DI + (k + 1) * P], XN3[b][:, c, :], c == 0, c == DC - 1)
                        last.then_inc(sem("xbc_mm"), 1)
                for b in BS:
                    pe.wait_ge(*after("xbc", nk(j, 12, XBC * b + 2)))
                    for c in range(DC):
                        last = mm(bank(b, 2)[0:8, :], win[:, c, 1280:1288], XN3[b][:, c, :], c == 0, c == DC - 1)
                    last.then_inc(sem("dt_mm"), 1)
                for s in range(SUB):
                    for b in BS:
                        k = 2 * s + b
                        to = (3, 0)[s % 2]
                        if s == 0:
                            pe.wait_ge(*after("lam", n2(j, b)))
                        if s == 1:
                            pe.wait_ge(*after("xbc", nk(j, 12, XBC * b + 5)))
                        if s >= 2:
                            pe.wait_ge(*after("zs", nk(j, 8, k - 4)))
                        for c in range(DC):
                            last = mm(bank(b, to), XN3[b][:, c, s * P:(s + 1) * P], win[:, c, 0:DI], c == 0, c == DC - 1)
                        last.then_inc(sem("z3_mm"), 1)
                for s in range(SUB):
                    for b in BS:
                        k = 2 * s + b
                        sub = slice(s * P, (s + 1) * P)
                        if s == 0:
                            pe.wait_ge(*after("xs", n2(j, b)))
                            pe.wait_ge(*after("rows", n2(j, b)))
                            pe.wait_ge(*after("zs", nk(j, 8, 6 + b)))
                        else:
                            pe.wait_ge(*after("y7", nk(j, 8, k - 2)))
                            pe.wait_ge(*after("s7", nk(j, 8, k - 2)))
                        for c in range(4):
                            last = nc.tensor.transpose(bank(b, 0)[:, c * P:(c + 1) * P], CV[b][:, c, sub], cn("ident"))
                        last.then_inc(sem("xtk_mm"), 1)
                        nc.tensor.transpose(bank(b, 1)[:, 0:P], CV[b][:, 4, sub], cn("ident"))
                        nc.tensor.transpose(bank(b, 1)[:, P:P + 96], ROWS[b][0:96, sub], cn("ident", 96)[:, 0:96])
                        mm(bank(b, 1)[:, 256:384], CV[b][:, 4, sub], CV[b][:, 5, sub]).then_inc(sem("bt_mm"), 1)
                        pe.wait_ge(*after("rb", nk(j, 8, k)))
                        for half in range(2):
                            last = mm(bank(b, 2 + half), LNG[b][0:40, sub], RB[b][0:40, 4 * half:4 * half + 4, :].rearrange("p h n -> p (h n)"))
                        last.then_inc(sem("dmm"), 1)
                        pe.wait_ge(*after("bt", nk(j, 8, k)))
                        mm(bank(b, 1)[:, 384:392], cn("last"), BT[b][:, P + 32:P + 40]).then_inc(sem("een_mm"), 1)
                    for b in BS:
                        k = 2 * s + b
                        sub = slice(s * P, (s + 1) * P)
                        pe.wait_ge(*after("dm", nk(j, 8, k)))
                        pe.wait_ge(*after("dtx", nk(j, 8, k)))
                        for h in range(HM):
                            last = mm(bank(b, 2)[:, h * PD:(h + 1) * PD], DM[b][:, h, :], DTX[b][:, h * PD:(h + 1) * PD])
                        last.then_inc(sem("y1_mm"), 1)
                        if s == 0:
                            pe.wait_ge(*after("m0", 10))
                        else:
                            pe.wait_ge(*after("s7", nk(j, 8, k - 2)))
                        mm(bank(b, 3), CV[b][:, 5, sub], STATE[b]).then_inc(sem("y2_mm"), 1)
                        pe.wait_ge(*after("wx", nk(j, 8, k)))
                        pe.wait_ge(*after("xtk", nk(j, 8, k)))
                        mm(bank(b, 0), BT[b][:, 0:P], WX[b]).then_inc(sem("s_new"), 1)
                for b in BS:
                    for s in range(SUB):
                        if s == 0:
                            pe.wait_ge(*after("yn", n2(j, b)))
                            pe.wait_ge(*after("s7", nk(j, 8, 6 + b)))
                        if s >= 2:
                            pe.wait_ge(*after("ut", nk(j, 8, 4 * b + s - 2)))
                        for c in range(4):
                            last = nc.tensor.transpose(bank(b, s % 2)[:, c * P:(c + 1) * P], ZS[b][:, s, :][:, c * P:(c + 1) * P], cn("ident"))
                        last.then_inc(sem("ut7_mm"), 1)
                for b in BS:
                    pe.wait_ge(*after("ut", nk(j, 8, 4 * b + 3)))
                    for mo in range(DC):
                        for c in range(4):
                            last = mm(bank(b, 2 + mo), feat(w("Wout", 4), c, mo), CV[b][:, c, :], c == 0, c == 3)
                        last.then_inc(sem("x4_mm"), 1)

            pe.wait_ge(*after("x4", B * J))
            with pe.Fori(0, J) as j:
                pe.wait_ge(*after("y", j * B))
                norm_pe(pe, "l3", j, None, ST, True)
                lin_pe(pe, "q3_mm", j, w("Wq3", 2), lambda b, c: XC[b][:, c, :], (2, 3), lambda b: pe.wait_ge(*after("norm_xn", NORMS["l3"] + n2(j, b))))
                for b in BS:
                    pe.wait_ge(*after("att_q", CHUNKS["a3"] + nk(j, 4, 2 * b + 1)))
                attn_pe(pe, "a3", j, 1)
                for b in BS:
                    pe.wait_ge(*after("att_ctx", CHUNKS["a3"] + nk(j, 4, 2 * b + 1)))
                    for mo in range(DC):
                        for c in range(DC):
                            last = mm(bank(b, mo), feat(w("Wo3", 2), c, mo), ST[b][:, c, :], c == 0, c == DC - 1)
                        last.then_inc(sem("y_mm3"), 1)

        @block.scalar
        def _(act):
            begin(act, "scalar")
            act.wait_ge(*after("ld_cn", 16))
            act.wait_ge(*after("ld_vec", 16))
            act.wait_ge(*after("ld_x", 16))
            with act.Fori(0, J) as j:
                act.wait_ge(*after("opg", j * B))
                norm_act(act, "r1", j, lambda b: xs(b, j), SQ, RT, "eps6", False)
                for b in BS:
                    for mo in range(DC):
                        act.wait_ge(*after("z_mm", nk(j, 4, 2 * b + mo)))
                        nc.scalar.activation(Z[:, mo, b, tj(j)], bank(b, 2 + mo), ACT.Identity, bias=v("bz", mo)).then_inc(sem("z"), 1)
                act.wait_ge(*after("wready", 1))
                for b in BS:
                    act.wait_ge(*after("g_mm", n2(j, b)))
                    nc.scalar.activation(GG[b], bank(b, 1), ACT.Gelu_apprx_tanh, bias=cb("gcb")).then_inc(sem("gg"), 1)
                for b in BS:
                    for k, (dst, bias, to) in enumerate(((GB[b][:, 0], v("bg2", 0), 3), (GB[b][:, 1], v("bg2", 1), 1),
                                                         (SQ[b][:, 0], v("bgc2", 0), 0), (SQ[b][:, 1], v("bgc2", 1), 2))):
                        act.wait_ge(*after("gam_mm", nk(j, 8, 4 * b + k)))
                        nc.scalar.activation(dst, bank(b, to), ACT.Sigmoid, bias=bias).then_inc(sem("gam"), 1)

            def gates(j):
                for q in range(2 * B):
                    for mo in range(DC):
                        act.wait_ge(*after("u", nk(j, 8, 2 * q + mo)))
                        nc.scalar.activation(UG[q % B][mo], UG[q % B][mo], ACT.Sigmoid).then_inc(sem("g"), 1)

            with act.Fori(0, SWEEPS_BF + SWEEPS_F + 1) as j:
                gates(j)
            n = SWEEPS_BF + SWEEPS_F + 1
            for q in range(2 * B + 1):
                jj, b = q // B, q % B
                for mo in range(DC):
                    if q < 2 * B:
                        act.wait_ge(*after("u", nk(n, 8, 2 * q + mo)))
                        nc.scalar.activation(UG[b][mo], UG[b][mo], ACT.Sigmoid).then_inc(sem("g"), 1)
                if q >= 1:
                    jj, b = (q - 1) // B, (q - 1) % B
                    for mo in range(DC):
                        act.wait_ge(*after("dd", 2 * (q - 1) + mo + 1))
                        nc.scalar.activation(GZ[b][mo], GZ[b][mo], ACT.Abs).then_inc(sem("ad"), 1)
                        nc.scalar.activation(AA[b][mo], H[:, mo, b, jj, 1:T + 1], ACT.Abs, scale=TOL).then_inc(sem("ad"), 1)
            act.wait_ge(*after("flag", 1))
            need = act.value_load(FLAG[0:1, 0:1], min_val=0, max_val=1)
            with act.If(need == 1):
                with act.Fori(0, S) as t:
                    act.wait_ge(*after("xu", t + 1))
                    nc.scalar.activation(UX[:, 0], UX[:, 0], ACT.Sigmoid).then_inc(sem("xg"), 1)

            prep_act(act, "a0")
            with act.Fori(0, J) as j:
                act.wait_ge(*after("x1", j * B))
                for b in BS:
                    for mo in range(DC):
                        act.wait_ge(*after("q0_mm", nk(j, 4, 2 * b + mo)))
                        nc.scalar.activation(QS[b][:, mo, :], bank(b, mo), ACT.Identity, bias=cb("CQb", mo)).then_inc(sem("att_q"), 1)
                attn_act(act, "a0", j, 1, "abv0")
                for b in BS:
                    act.wait_ge(*after("xr", n2(j, b)))
                norm_act(act, "r2", j, lambda b: xs(b, j), ST, RTB, "eps6", False)
                for k in range(8):
                    for b in BS:
                        act.wait_ge(*after("f1_mm", nk(j, 16, 2 * k + b)))
                        nc.scalar.activation(FH[b][k], bank(b, k % 2), ACT.Gelu_apprx_tanh, bias=v("bf1", k)).then_inc(sem("ff"), 1)

            norm_act(act, "cn", 0, None, [ST[0]], [RTB[0]], "eps5", True, [XC[0]], B * M, [0])
            for t, k in ((FT6, 2), (ET6, 3)):
                act.wait_ge(*after("s_mm", k - 1))
                nc.scalar.activation(t[:, :, :], ps[:, k, 0:16].rearrange("p (c n) -> p c n", c=DC)[:, :, 0:6], ACT.Copy).then_inc(sem("ft6"), 1)
            act.wait_ge(*after("g6_mm", 2))
            act.wait_ge(*after("g60", 2))
            nc.scalar.activation(G6[0:6, 0:6], ps[0:6, 4, 0:6], ACT.Copy, scale=1.0 / D).then_inc(sem("g6"), 1)
            nc.scalar.activation(GS[0:6, 0:6], ps[0:6, 5, 0:6], ACT.Copy, scale=D ** -0.5).then_inc(sem("g6"), 1)
            act.wait_ge(*after("nf_mm", 1))
            nc.scalar.activation(NF[0:M, :, :], ps[0:M, 6, 0:16].rearrange("p (b n) -> p b n", b=B)[:, :, 0:4], ACT.Copy).then_inc(sem("nf"), 1)
            with act.Fori(0, J) as j:
                act.wait_ge(*after("utok", j * 8))
                norm_act(act, "l1", j, None, ST, RTB, "eps5", True, XC)
                for b in BS:
                    act.wait_ge(*after("b1_sh", n2(j, b)))
                    pr = PR[b][0][:, 0:4, 0:M]
                    nc.scalar.activation(pr, pr, ACT.Exp).then_inc(sem("b1_ex"), 1)
                for b in BS:
                    act.wait_ge(*after("b1_tr", n2(j, b)))
                    nc.scalar.activation(PT[b][0:M, 0, :], bank(b, 3)[0:M, :], ACT.Copy).then_inc(sem("b1_pt"), 1)
                act.wait_ge(*after("us1", 4))
                for b in BS:
                    act.wait_ge(*after("h4_mm", n2(j, b)))
                    if j is not None:
                        act.wait_ge(*after("u5x", j * B))
                    nc.scalar.activation(U5S[b][0:4, :], bank(b, 0)[0:4, :], ACT.Gelu, bias=v("fc1b")[0:4]).then_inc(sem("h4"), 1)
                for b in BS:
                    act.wait_ge(*after("var_mm", n2(j, b)))
                    nc.scalar.activation(RM[b][0:6, :], bank(b, 2)[0:6, :], ACT.Sqrt, bias=cn("eps5", 6)).then_inc(sem("rm"), 1)
                act.wait_ge(*after("uy0", 2))
                for b in BS:
                    act.wait_ge(*after("y_mm", n2(j, b)))
                    nc.scalar.activation(YY[0:6, b, tj(j)], bank(b, 3)[0:6, :], ACT.Copy).then_inc(sem("yy"), 1)
            for b in BS:
                act.wait_ge(*after("mr_mm", b + 1))
                act.wait_ge(*after("uy0", 2))
                nc.scalar.activation(UU[32:33, b, :], ps[0:1, 4 * b:4 * b + 2, :].rearrange("p k n -> p (k n)"), ACT.Copy).then_inc(sem("mrow"), 1)
            for half in range(2):
                for k in range(SUB * J):
                    for b in BS:
                        n = (half * 8 + k) * 2 + b
                        act.wait_ge(*after("p2", n + 1))
                        nc.scalar.activation(PE1[b][k % 4], bank(b, k % 2), ACT.Exp).then_inc(sem("p2e"), 1)

            prep_act(act, "a2")
            with act.Fori(0, J) as j:
                act.wait_ge(*after("x3", j * 4))
                for b in BS:
                    for mo in range(DC):
                        act.wait_ge(*after("q2_mm", nk(j, 4, 2 * b + mo)))
                        nc.scalar.activation(QS[b][:, mo, :], bank(b, mo), ACT.Identity, bias=v("bq2", mo)).then_inc(sem("att_q"), 1)
                attn_act(act, "a2", j, 2, "bv2")
                norm_act(act, "x3", j, None, ST, RTB, "eps5", True, XC)

            prep_act(act, "a3")
            nc.scalar.activation(cb("A")[0:8], v("alog")[0:8], ACT.Exp).then_inc(sem("expa"), 1)
            with act.Fori(0, J) as j:
                act.wait_ge(*after("x4", j * B))
                if True:
                    act.wait_ge(*after("x3", 4 * J))
                norm_act(act, "r3", j, lambda b: xs(b, j), SQ7, RT7, "eps5", False)
                for b in BS:
                    act.wait_ge(*after("hx", n2(j, b)))
                    for k in range(XBC):
                        act.wait_ge(*after("xbc_mm", nk(j, 12, XBC * b + k)))
                        nc.scalar.activation(XB[b][:, k, TAPS - 1:], bank(b, k % 4), ACT.Copy).then_inc(sem("xbc"), 1)
                    for k in range(XBC):
                        act.wait_ge(*after("xbc", nk(j, 12, XBC * b + k)))
                        act.wait_ge(*after("norm_xn", NORMS["r3"] + n2(j, b)))
                        nc.scalar.activation(CV[b][:, k, :], XB[b][:, k, 0:T], ACT.Identity, bias=v("convb", k), scale=v("convw", 4 * k)).then_inc(sem("cv0"), 1)
                for b in BS:
                    act.wait_ge(*after("dt1", n2(j, b)))
                    nc.scalar.activation(ET[b][0:8], ET[b][0:8], ACT.Exp, scale=-1.0).then_inc(sem("et"), 1)
                for b in BS:
                    act.wait_ge(*after("et", n2(j, b)))
                    nc.scalar.activation(ET[b][0:8], ET[b][0:8], ACT.Ln, bias=cn("ones", 8)[:, 0:1]).then_inc(sem("l1p"), 1)
                for b in BS:
                    act.wait_ge(*after("lam", n2(j, b)))
                    act.wait_ge(*after("m0", 10))
                    nc.scalar.activation(ROWS[b][32:40], LAM[b][0:8], ACT.Exp).then_inc(sem("el"), 1)
                    act.wait_ge(*after("led", n2(j, b)))
                    nc.scalar.activation(ROWS[b][64:72], ROWS[b][64:72], ACT.Exp).then_inc(sem("ew"), 1)
                for s in range(SUB):
                    for b in BS:
                        k = 2 * s + b
                        act.wait_ge(*after("z3_mm", nk(j, 8, k)))
                        act.wait_ge(*after("rows", n2(j, b)))
                        nc.scalar.activation(ZS[b][:, s, :], bank(b, (3, 0)[s % 2]), ACT.Silu).then_inc(sem("zs"), 1)
                for b in BS:
                    act.wait_ge(*after("cv", nk(j, 12, XBC * b + 5)))
                    nc.scalar.activation(CV[b][:, :, :], CV[b][:, :, :], ACT.Silu).then_inc(sem("xs"), 1)
                for s in range(SUB):
                    for b in BS:
                        k = 2 * s + b
                        act.wait_ge(*after("xtk_mm", nk(j, 8, k)))
                        act.wait_ge(*after("hist", n2(j, b)))
                        nc.scalar.activation(XTK[b], bank(b, 0), ACT.Copy).then_inc(sem("xtk"), 1)
                        act.wait_ge(*after("bt_mm", nk(j, 8, k)))
                        nc.scalar.activation(BT[b], bank(b, 1)[:, 0:224], ACT.Copy).then_inc(sem("bt"), 1)
                    for b in BS:
                        k = 2 * s + b
                        act.wait_ge(*after("dms", nk(j, 8, k)))
                        nc.scalar.activation(DM[b], DM[b], ACT.Exp).then_inc(sem("dme"), 1)
                for b in BS:
                    for s in range(SUB):
                        act.wait_ge(*after("y7", nk(j, 8, 6 + b)))
                        nc.scalar.activation((DTX, XTK, WX, SE)[s][b], ZS[b][:, s, :], ACT.Square, accum_out=SSQ[:, b, s:s + 1]).then_inc(sem("ssq"), 1)
                    act.wait_ge(*after("ssq", nk(j, 8, 4 * b + 3)))
                    nc.scalar.activation(SSR[:, b, :], SSQ[:, b, :], ACT.Sqrt, scale=1.0 / DI, bias=cn("eps5")).then_inc(sem("ssr"), 1)
                for b in BS:
                    for s in range(SUB):
                        act.wait_ge(*after("ut7_mm", nk(j, 8, 4 * b + s)))
                        nc.scalar.activation(CV[b][:, 0:4, s * P:(s + 1) * P], bank(b, s % 2).rearrange("p (c n) -> p c n", c=4), ACT.Copy).then_inc(sem("ut"), 1)
            with act.Fori(0, J) as j:
                act.wait_ge(*after("x4", B * J))
                act.wait_ge(*after("y", j * B))
                norm_act(act, "l3", j, None, ST, RTB, "eps5", True, XC)
                for b in BS:
                    for mo in range(DC):
                        act.wait_ge(*after("q3_mm", nk(j, 4, 2 * b + mo)))
                        nc.scalar.activation(QS[b][:, mo, :], bank(b, 2 + mo), ACT.Identity, bias=cb("q3b", mo)).then_inc(sem("att_q"), 1)
                attn_act(act, "a3", j, 1, None)

        @block.vector
        def _(dve):
            begin(dve, "vector")
            ch = Chain(dve, "dve_step")
            dve.wait_ge(*after("ld_vec", 16))
            dve.wait_ge(*after("ld_w0", 16))
            dve.wait_ge(*after("ld_x", 16))
            dve.wait_ge(*after("ld_cn", 16))
            TT, TS, STT = nc.vector.tensor_tensor, nc.vector.tensor_scalar, nc.vector.scalar_tensor_tensor
            TT(cb("zgb"), v("bgz", 0), v("bgh", 0), ALU.add)
            TT(cb("zgb", 1), v("bgz", 1), v("bgh", 1), ALU.add)
            for k in range(2):
                STT(out=cb("xob", k), in0=v("bv", k), scalar=0.1, in1=v("abo", k), op0=ALU.mult, op1=ALU.add)
                TS(w("Wz", 2)[:, k, :], w("Wz", 2)[:, k, :], v("n1", k), None, ALU.mult)
                TS(w("Wv", 2)[:, k, :], w("Wv", 2)[:, k, :], v("n1", k), 0.1, ALU.mult, ALU.mult)
                nc.vector.tensor_copy(WGB[:, k, :], w("Wgh", 2)[:, k, :])
            dve.wait_ge(*after("pw", 5))
            for k in range(2):
                TS(CQ[:, k, :], ps[:, k, 0:D], v("n1", k), None, ALU.mult)
                TS(CG[:, k, 0:P], ps[:, 2 + k, 0:P], v("n1", k), None, ALU.mult)
            TT(CB[:, 0:2], ps[:, 4, 0:2], VC[:, vcol["abq"][0]:vcol["abq"][1]], ALU.add)
            ch.link(TT(cb("gcb"), ps[:, 5, 0:1], v("bg1c"), ALU.add))
            dve.sem_inc(sem("wready"), 1)
            with dve.Fori(0, J) as j:
                ch.enter(j)
                norm_dve(dve, ch, "r1", j, lambda b: xs(b, j), SQ, RT, lambda b: XN[:, :, b, tj(j)], False)
                for b in BS:
                    for mo in range(DC):
                        dve.wait_ge(*after("zg_mm", nk(j, 4, 2 * b + mo)))
                        TS(ZG[:, mo, b, tj(j)], bank(b, 2 * mo), cb("zgb", mo), None, ALU.add).then_inc(sem("zg"), 1)
                for b in BS:
                    dve.wait_ge(*after("gam", nk(j, 8, 4 * b + 3)))
                    ch.link(TT(GB[b], GB[b], SQ[b], ALU.mult))
                    ch.link(TS(GB[b], GB[b], 1e-6, 1.0 - 1e-6, ALU.max, ALU.min))
                    TS(OPG[:, :, b, tj(j)], GB[b], 1.0, None, ALU.add).then_inc(sem("opg"), 1)
                ch.turn()
            ch.leave(J)

            dve.wait_ge(*after("opg", B * J))
            nc.vector.memset(HB[:, :, :, :, :].rearrange("p c b j s -> p (c b j s)"), 0.0)
            ch.link(nc.vector.memset(H[:, :, :, :, :].rearrange("p c b j s -> p (c b j s)"), 0.0))
            dve.sem_inc(sem("h"), 8)

            def sweep(j, dst, checking=False):
                for q in range(2 * B + 1):
                    jj, b = q // B, q % B
                    if q < 2 * B:
                        for mo in range(DC):
                            dve.wait_ge(*after("hm", nk(j, 8, 2 * q + mo)))
                            TT(UG[b][mo], bank(b, 2 * jj + mo), ZG[:, mo, b, jj * T:(jj + 1) * T], ALU.add).then_inc(sem("u"), 1)
                    if q >= 1:
                        jj, b = (q - 1) // B, (q - 1) % B
                        span = slice(1, T + 1)
                        if jj == 1 and not checking:
                            nc.vector.tensor_copy(dst[:, :, b, 1, 0:1], dst[:, :, b, 0, T:T + 1])
                        for mo in range(DC):
                            k = 2 * (q - 1) + mo
                            dve.wait_ge(*after("g", nk(j, 8, k)))
                            ch.link(TT(AA[b][mo], OPG[:, mo, b, jj * T:(jj + 1) * T], UG[b][mo], ALU.subtract))
                            dve.wait_ge(*after("gz", nk(j, 8, k)))
                            first = dst[:, mo, b, 0, T * jj:T * jj + 1]
                            scan = nc.vector.tensor_tensor_scan(UG[b][mo] if checking else dst[:, mo, b, jj, span], AA[b][mo], GZ[b][mo],
                                                                first, ALU.mult, ALU.add)
                            if not checking:
                                scan.then_inc(sem("h"), 1)
                                continue
                            ch.link(scan)
                            TT(GZ[b][mo], UG[b][mo], H[:, mo, b, jj, span], ALU.subtract).then_inc(sem("dd"), 1)
                        if checking:
                            for mo in range(DC):
                                k = 2 * (q - 1) + mo
                                dve.wait_ge(*after("ad", 2 * k + 2))
                                STT(out=UG[b][mo], in0=GZ[b][mo], scalar=-TOL, in1=AA[b][mo], op0=ALU.add, op1=ALU.is_le,
                                    accum_out=OKC[:, k:k + 1]).then_inc(sem("okc"), 1)
                                dve.wait_ge(*after("okc", k + 1))

            with dve.Fori(0, SWEEPS_BF) as j:
                ch.enter(j)
                sweep(j, HB)
                ch.turn()
            ch.leave(SWEEPS_BF)
            sweep(SWEEPS_BF, H)
            with dve.Fori(0, SWEEPS_F) as j:
                ch.enter(j)
                sweep(j + (SWEEPS_BF + 1), H)
                ch.turn()
            ch.leave(SWEEPS_F)
            sweep(SWEEPS_BF + SWEEPS_F + 1, H, checking=True)
            dve.wait_ge(*after("count", 1))
            ch.link(nc.vector.tensor_reduce(TOT[:, 0:1], ps[0:1, 0, 0:8], AX.X, ALU.add))
            nc.vector.tensor_scalar(FLAG[:, 0:1], TOT[:, 0:1], float(D * B * S) - 0.5, None, FALLBACK_TEST).then_inc(sem("flag"), 1)
            dve.wait_ge(*after("flag", 1))
            need = dve.value_load(FLAG[0:1, 0:1], min_val=0, max_val=1)
            with dve.If(need == 1):
                cx = Chain(dve, "exact_step")
                for jj in range(J):
                    if jj:
                        nc.vector.tensor_copy(H[:, :, :, jj, 0:1], H[:, :, :, jj - 1, T:T + 1]).then_inc(sem("xh"), 1)
                        dve.wait_ge(*after("xh", jj * (T + 1)))
                    with dve.Fori(0, T) as t:
                        cx.enter(t)
                        at, now = bass.ds(t, 1), bass.ds(t + jj * T, 1)
                        dve.wait_ge(*after("xm", t + (jj * T + 1)))
                        TT(UX[:, 0], ps[:, 1, 0:2 * B].rearrange("p (c b) -> p c b", c=DC), ZG[:, :, :, now].rearrange("p c b s -> p c (b s)"), ALU.add).then_inc(sem("xu"), 1)
                        dve.wait_ge(*after("xg", t + (jj * T + 1)))
                        TT(UX[:, 1], UX[:, 0], Z[:, :, :, now].rearrange("p c b s -> p c (b s)"), ALU.mult)
                        cx.link(TT(UX[:, 2], OPG[:, :, :, now].rearrange("p c b s -> p c (b s)"), UX[:, 0], ALU.subtract))
                        cx.link(TT(UX[:, 3], UX[:, 2], H[:, :, :, jj, at].rearrange("p c b s -> p c (b s)"), ALU.mult))
                        TT(H[:, :, :, jj, bass.ds(t + 1, 1)].rearrange("p c b s -> p c (b s)"), UX[:, 3], UX[:, 1], ALU.add).then_inc(sem("xh"), 1)
                        cx.turn()
                    cx.leave(T)
                    dve.wait_ge(*after("xh", jj * (T + 1) + T))
            dve.sem_inc(sem("decided"), 1)

            dve.wait_ge(*after("ld_ffn", 16))
            for c in range(DC):
                ins = TS(w("Wf1", 2)[:, c, :], w("Wf1", 2)[:, c, :], v("n2", c), None, ALU.mult)
            prep_dve(dve, ch, "a0", "abk0", 4)
            dve.wait_ge(*after("pr0", 4))
            with dve.Fori(0, J) as j:
                ch.enter(j)
                attn_dve(dve, ch, "a0", j, 1)
                for b in BS:
                    for mo in range(DC):
                        xd = X[:, mo, b, tj(j)]
                        dve.wait_ge(*after("xr_mm", nk(j, 4, 2 * b + mo)))
                        ch.link(STT(out=xd, in0=bank(b, mo), scalar=cb("xob", mo), in1=xd, op0=ALU.add, op1=ALU.add))
                        ins = TT(xd, xd, H[:, mo, b, bass.ds(j, 1), 1:T + 1].rearrange("p a n -> p (a n)"), ALU.add)
                    ins.then_inc(sem("xr"), 1)
                for b in BS:
                    dve.wait_ge(*after("xr", n2(j, b)))
                norm_dve(dve, ch, "r2", j, lambda b: xs(b, j), ST, RTB, lambda b: XC[b], False)
                for b in BS:
                    dve.wait_ge(*after("f2_mm", n2(j, b)))
                    for mo in range(DC):
                        xd = X[:, mo, b, tj(j)]
                        ins = STT(out=xd, in0=bank(b, 2 + mo), scalar=v("bf2", mo), in1=xd, op0=ALU.add, op1=ALU.add)
                    ins.then_inc(sem("x1"), 1)
                ch.turn()
            ch.leave(J)

            dve.wait_ge(*after("x1", B * J))
            dve.wait_ge(*after("ld_r6", 16))
            norm_dve(dve, ch, "cn", 0, cx_src, [ST[0]], [RTB[0]], lambda b: XC[0][:, :, 0:B * M], True, [XC[0]], B * M, [0])
            dve.wait_ge(*after("norm_xn", NORMS["cn"] + 1))
            for c in range(DC):
                TS(NX[:, c, :], XC[0][:, c, 0:B * M], v("l1w1", c), v("l1b1", c), ALU.mult, ALU.add).then_inc(sem("nx"), 1)
            dve.wait_ge(*after("nx", 2))
            TS(NXS[:, :, :], NX[:, :, :], D ** -0.5, None, ALU.mult).then_inc(sem("nxs"), 1)
            ch.link(nc.vector.tensor_reduce(TOT6[:, 0:1], R6[:, 0, :], AX.X, ALU.add))
            ch.link(TS(TOT6[:, 1:2], TOT6[:, 0:1], 1.0 / D, None, ALU.mult))
            TS(F6C[0:6], R6[:, 0, :], TOT6[:, 1:2], None, ALU.subtract).then_inc(sem("f6"), 1)
            dve.wait_ge(*after("f6", 1))
            ch.link(TT(E6[0:6], F6C[0:6], R6[:, 1, :], ALU.mult))
            TT(E6[0:6], E6[0:6], R6[:, 2, :], ALU.add).then_inc(sem("e6"), 1)
            dve.wait_ge(*after("e6", 1))
            ch.link(TT(E1[0:6], E6[0:6], R6[:, 3, :], ALU.mult))
            TT(E1[0:6], E1[0:6], R6[:, 4, :], ALU.mult)
            ch.link(TT(C1[0:6], R6[:, 0, :], R6[:, 4, :], ALU.mult))
            dve.sem_inc(sem("e1"), 1)
            with dve.Fori(0, J) as j:
                ch.enter(j)
                norm_dve(dve, ch, "l1", j, lambda b: xs(b, j), ST, RTB, lambda b: XC[b], True, XC)
                for b in BS:
                    dve.wait_ge(*after("norm_xn", NORMS["l1"] + n2(j, b)))
                    for c in range(DC):
                        TS(QS[b][:, c, :], XC[b][:, c, :], v("l1w2", c), v("l1b2", c), ALU.mult, ALU.add).then_inc(sem("f"), 1)
                for b in BS:
                    dve.wait_ge(*after("b1_sc", n2(j, b)))
                    sc = bank(b, 2)[:, 0:HALF].rearrange("p (h m) -> p h m", h=4)
                    ch.link(nc.vector.tensor_reduce(MX[:, b, 0, 0:4], sc, AX.X, ALU.max, negate=True))
                    TT(PR[b][0][:, 0:4, 0:M], sc, bc(MX[:, b, 0, 0:4], M, 2), ALU.add).then_inc(sem("b1_sh"), 1)
                for b in BS:
                    dve.wait_ge(*after("b1_ex", n2(j, b)))
                    ch.link(nc.vector.tensor_reduce(RS[:, b, 0, 0:4], PR[b][0][:, 0:4, 0:M], AX.X, ALU.add))
                    nc.vector.reciprocal(RS[:, b, 0, 0:4], RS[:, b, 0, 0:4]).then_inc(sem("b1_ri"), 1)
                for b in BS:
                    dve.wait_ge(*after("h4", n2(j, b)))
                    dve.wait_ge(*after("wu_mm", n2(j, b)))
                    TT(WU[b][0:6, :], bank(b, 1)[0:6, :], U5S[b][0:6, :], ALU.mult).then_inc(sem("wu"), 1)
                for b in BS:
                    dve.wait_ge(*after("rm", n2(j, b)))
                    dve.wait_ge(*after("us1", 4))
                    dve.wait_ge(*after("u6x", j * B))
                    ch.link(nc.vector.reciprocal(RM[b][0:6, :], RM[b][0:6, :]))
                    TT(U6S[b][0:5, :], U5S[b][0:5, :], RM[b][0:5, :], ALU.mult).then_inc(sem("u6"), 1)
                for b in BS:
                    dve.wait_ge(*after("ut_mm", n2(j, b)))
                    for s in range(SUB):
                        nc.vector.tensor_copy(UT[:, b, bass.ds(j * SUB + s, 1), 0:6].rearrange("p a n -> p (a n)"), bank(b, 0)[:, 8 * s:8 * s + 6]).then_inc(sem("utok"), 1)
                ch.turn()
            ch.leave(J)
            for t in range(SUB * J):
                for b in BS:
                    k = 2 * (t % 2)
                    dve.wait_ge(*after("p1", 2 * t + b + 1))
                    nc.vector.tensor_reduce(MN[:, b, t:t + 1], ps[:, 4 * b + k:4 * b + k + 2, :].rearrange("p k n -> p (k n)"), AX.X, ALU.max, negate=True).then_inc(sem("mn"), 1)
            dve.wait_ge(*after("fx", B * J))
            for half in range(2):
                for b in BS:
                    dve.wait_ge(*after("o6_mm", 2 * half + b + 1))
                    nc.vector.tensor_copy(RM[b][0:6, :], bank(b, 2)[0:6, :]).then_inc(sem("o6"), 1)
                for b in BS:
                    dve.wait_ge(*after("den_mm", 2 * half + b + 1))
                    ch.link(nc.vector.reciprocal(WU[b][0:6, :], bank(b, 3)[0:6, :]))
                    TT(WU[b][0:6, :], WU[b][0:6, :], RM[b][0:6, :], ALU.mult).then_inc(sem("oo"), 1)
                for b in BS:
                    for mo in range(DC):
                        xd = X[:, mo, b, half * T:(half + 1) * T]
                        dve.wait_ge(*after("x2_mm", 4 * half + 2 * b + mo + 1))
                        TT(xd, bank(b, 3), xd, ALU.add).then_inc(sem("x2"), 1)

            dve.wait_ge(*after("x2", 4 * B))
            prep_dve(dve, ch, "a2", "bk2", 8)
            with dve.Fori(0, J) as j:
                ch.enter(j)
                attn_dve(dve, ch, "a2", j, 2)
                for b in BS:
                    for mo in range(DC):
                        xd = X[:, mo, b, tj(j)]
                        dve.wait_ge(*after("o2_mm", nk(j, 4, 2 * b + mo)))
                        TT(xd, bank(b, mo), xd, ALU.add).then_inc(sem("o2"), 1)
                dve.wait_ge(*after("o2", nk(j, 4, 3)))
                norm_dve(dve, ch, "x3", j, lambda b: xs(b, j), ST, RTB, lambda b: XC[b], True, XC)
                for b in BS:
                    dve.wait_ge(*after("norm_xn", NORMS["x3"] + n2(j, b)))
                    for c in range(DC):
                        TS(X[:, c, b, tj(j)], XC[b][:, c, :], v("lg2", c), v("lb2", c), ALU.mult, ALU.add).then_inc(sem("x3"), 1)
                ch.turn()
            ch.leave(J)

            dve.wait_ge(*after("ld_w3", 16))
            dve.wait_ge(*after("x3", 4 * J))
            dve.wait_ge(*after("ld_mask", 16))
            ch.link(nc.vector.tensor_copy(NEG[:, :], MKU[:, :].bitcast(U8)[:, 0:M]))
            TS(KEEP[:, :], NEG[:, :], -1.0, 1.0, ALU.mult, ALU.add)
            for c in range(DC):
                TS(w("Win", 2)[:, c, :], w("Win", 2)[:, c, :], v("mnw", c), None, ALU.mult)
            ch.link(TS(NEG[:, :], NEG[:, :], -1e9, None, ALU.mult))
            dve.sem_inc(sem("w3ready"), 1)
            for c in range(4):
                TS(w("Wout", 4)[:, c, :], w("Wout", 4)[:, c, :], v("gnw", c), None, ALU.mult)
            dve.wait_ge(*after("q3b_mm", 1))
            for c in range(DC):
                TS(w("Wq3", 2)[:, c, :], w("Wq3", 2)[:, c, :], v("caw", c), None, ALU.mult)
            ch.link(nc.vector.tensor_copy(CB[:, 7:9], ps[:, 3, 0:2]))
            dve.sem_inc(sem("q3w"), 1)
            prep_dve(dve, ch, "a3", None, 4, masked=True)
            ET_A = cb("A")[0:8]
            dve.wait_ge(*after("expa", 1))
            ch.link(TS(ET_A, ET_A, -1.0, None, ALU.mult))
            dve.wait_ge(*after("m0", 10))
            dve.wait_ge(*after("m1", 4))
            reset = RC[:, HM * P:HM * P + T]
            with dve.Fori(0, J) as j:
                ch.enter(j)
                dve.wait_ge(*after("x4", j * B))
                for b in BS:
                    nc.vector.tensor_copy(XB[b][:, :, 0:TAPS - 1], HIST[b]).then_inc(sem("hx"), 1)
                norm_dve(dve, ch, "r3", j, lambda b: xs(b, j), SQ7, RT7, lambda b: XN3[b], False)
                for b in BS:
                    for k in range(XBC):
                        dve.wait_ge(*after("cv0", nk(j, 12, XBC * b + k)))
                        for tap in range(1, TAPS):
                            ins = STT(out=CV[b][:, k, :], in0=XB[b][:, k, tap:tap + T], scalar=v("convw", 4 * k + tap), in1=CV[b][:, k, :],
                                      op0=ALU.mult, op1=ALU.add)
                            if tap < TAPS - 1:
                                ch.link(ins)
                        ins.then_inc(sem("cv"), 1)
                for b in BS:
                    dve.wait_ge(*after("hx", n2(j, b)))
                    nc.vector.tensor_copy(HIST[b], XB[b][:, :, T:T + TAPS - 1]).then_inc(sem("hist"), 1)
                for b in BS:
                    dve.wait_ge(*after("dt_mm", n2(j, b)))
                    ch.link(TS(DTV[b][0:8], bank(b, 2)[0:8, :], v("dtb")[0:8], None, ALU.add))
                    STT(out=ET[b][0:8], in0=DTV[b][0:8], scalar=-1.0, in1=DTV[b][0:8], op0=ALU.mult, op1=ALU.max).then_inc(sem("dt1"), 1)
                for b in BS:
                    dve.wait_ge(*after("l1p", n2(j, b)))
                    ch.link(STT(out=ROWS[b][0:8], in0=DTV[b][0:8], scalar=0.0, in1=ET[b][0:8], op0=ALU.max, op1=ALU.add))
                    ch.link(TS(DTV[b][0:8], ROWS[b][0:8], ET_A, None, ALU.mult))
                    ch.link(nc.vector.tensor_tensor_scan(LAM[b][0:8], reset, DTV[b][0:8], 0.0, ALU.mult, ALU.add))
                    TS(LNG[b][0:8], LAM[b][0:8], -1.0, None, ALU.mult).then_inc(sem("lam"), 1)
                    lam = LAM[b][0:8].rearrange("p (s n) -> p s n", s=SUB)
                    TT(ROWS[b][64:72].rearrange("p (s n) -> p s n", s=SUB), lam[:, :, P - 1:P].broadcast_to([8, SUB, P]), lam, ALU.subtract).then_inc(sem("led"), 1)
                for b in BS:
                    dve.wait_ge(*after("ew", n2(j, b)))
                    ch.link(nc.vector.tensor_copy(ET[b][64:72], ROWS[b][0:8]))
                    TT(ROWS[b][64:72], ROWS[b][64:72], ET[b][64:72], ALU.mult).then_inc(sem("rows"), 1)
                for s in range(SUB):
                    for b in BS:
                        k = 2 * s + b
                        dve.wait_ge(*after("dmm", nk(j, 8, k)))
                        dve.wait_ge(*after("hist", n2(j, b)))
                        dve.wait_ge(*after("cv", nk(j, 12, 11)))
                        TT(DM[b], ps[:, 4 * b + 2:4 * b + 4, :].rearrange("p k (h n) -> p (k h) n", h=4), bc(cn("future"), HM, 1), ALU.add).then_inc(sem("dms"), 1)
                        dve.wait_ge(*after("xtk", nk(j, 8, k)))
                        dve.wait_ge(*after("bt", nk(j, 8, k)))
                        TT(DTX[b].rearrange("p (h n) -> p h n", h=HM), XTK[b].rearrange("p (h n) -> p h n", h=HM), bc(BT[b][:, P:P + 8], PD, 2), ALU.mult).then_inc(sem("dtx"), 1)
                        dve.wait_ge(*after("een_mm", nk(j, 8, k)))
                        nc.vector.tensor_copy(EEN[:, b, :], bank(b, 1)[:, 384:392]).then_inc(sem("een"), 1)
                    for b in BS:
                        k = 2 * s + b
                        dve.wait_ge(*after("dme", nk(j, 8, k)))
                        TT(DM[b], DM[b], bc(bank(b, 1)[:, 256:384], HM, 1), ALU.mult).then_inc(sem("dm"), 1)
                        dve.wait_ge(*after("een", nk(j, 8, k)))
                        h3 = lambda a: a.rearrange("p (h n) -> p h n", h=HM)
                        TT(h3(SE[b]), h3(STATE[b]), bc(EEN[:, b, :], PD, 2), ALU.mult)
                        dve.wait_ge(*after("y2_mm", nk(j, 8, k)))
                        ch.link(TT(h3(DTX[b]), h3(bank(b, 3)), bc(BT[b][:, P + 32:P + 40], PD, 2), ALU.mult))
                        ch.link(TT(DTX[b], DTX[b], bank(b, 2), ALU.add))
                        dve.wait_ge(*after("s_new", nk(j, 8, k)))
                        TT(STATE[b], SE[b], bank(b, 0), ALU.add).then_inc(sem("s7"), 1)
                        ch.link(TT(h3(XTK[b]), h3(XTK[b]), bc(VC[:, vcol["dskip"][0]:vcol["dskip"][1]], PD, 2), ALU.mult))
                        ch.link(TT(DTX[b], DTX[b], XTK[b], ALU.add))
                        TT(ZS[b][:, s, :], ZS[b][:, s, :], DTX[b], ALU.mult).then_inc(sem("y7"), 1)
                for b in BS:
                    dve.wait_ge(*after("ssr", n2(j, b)))
                    ch.link(nc.vector.reciprocal(SSR[:, b, :], SSR[:, b, :]))
                    ins = TT(ZS[b][:, :, :], ZS[b][:, :, :], bc(SSR[:, b, :], DI, 2), ALU.mult)
                    ins.then_inc(sem("yn"), 1)
                for b in BS:
                    for mo in range(DC):
                        xd = X[:, mo, b, tj(j)]
                        dve.wait_ge(*after("x4_mm", nk(j, 4, 2 * b + mo)))
                        ins = TT(xd, bank(b, 2 + mo), xd, ALU.add)
                    ins.then_inc(sem("x4"), 1)
                ch.turn()
            ch.leave(J)
            dve.wait_ge(*after("pr0", 8))
            dve.wait_ge(*after("x4", B * J))
            with dve.Fori(0, J) as j:
                ch.enter(j)
                norm_dve(dve, ch, "l3", j, lambda b: xs(b, j), ST, RTB, lambda b: XC[b], True, XC)
                attn_dve(dve, ch, "a3", j, 1, masked=True)
                for b in BS:
                    for mo in range(DC):
                        xd = X[:, mo, b, tj(j)]
                        dve.wait_ge(*after("y_mm3", nk(j, 4, 2 * b + mo)))
                        ins = TT(xd, bank(b, mo), xd, ALU.add)
                    ins.then_inc(sem("y"), 1)
                ch.turn()
            ch.leave(J)


def pack_cols(a, n):
    out = np.zeros((n * P,), np.float32)
    a = np.asarray(a).reshape(-1)
    out[:a.size] = a
    return out.reshape(n, P).T


def kernel(**inputs):
    import concourse.bacc as bacc
    from concourse.bass_utils import run_bass_kernel_spmd

    i = {k: np.asarray(a) for k, a in inputs.items()}
    g0, g1, g2, g3 = (lambda n, k=k: i[f"L{k}_xattn_{n}"] for k in range(4))
    vcol, nvec, mats, sizes = layout()
    f = np.float32

    def chunks(a):
        k, n = a.shape
        return a.reshape(k // P, P, n).transpose(1, 0, 2).reshape(P, -1)

    vecs = np.zeros((P, nvec), f)

    def put(name, a, n):
        vecs[:, vcol[name][0]:vcol[name][1]] = pack_cols(a, n)

    for name, a in (("n1", g0("norm1_scale")), ("n2", g0("norm2_scale")), ("bq", g0("bq")), ("abq", g0("abq")),
                    ("bk", g0("bk")), ("bz", g0("bz")), ("bv", g0("bv")), ("abo", g0("abo")), ("bgz", g0("bgz")),
                    ("bgh", g0("bgh")), ("bg2", g0("bg2")), ("bgc2", g0("bgc2")), ("abk0", g0("abk")),
                    ("abv0", g0("abv")), ("bf2", g0("bf2")), ("l1w1", g1("norm1_w")), ("l1b1", g1("norm1_b")),
                    ("l1w2", g1("norm2_w")), ("l1b2", g1("norm2_b")), ("bq2", g2("bq")), ("bk2", g2("bk")),
                    ("bv2", g2("bv")), ("lg2", g2("ln_gamma")), ("lb2", g2("ln_beta")), ("mnw", g3("m_norm_w")),
                    ("caw", g3("ca_ln_w")), ("cab", g3("ca_ln_b"))):
        put(name, a, 2)
    put("bg1c", np.concatenate([g0("bg1"), g0("bgc1")]), 1)
    put("bf1", g0("bf1"), 8)
    put("fc1b", g1("fc1_b"), 1)
    put("convb", g3("conv_b"), XBC)
    vecs[:, vcol["convw"][0]:vcol["convw"][1]] = g3("conv_w").reshape(XBC, P, TAPS).transpose(1, 0, 2).reshape(P, -1)
    put("dtb", g3("dt_bias"), 1)
    put("alog", g3("A_log"), 1)
    vecs[:, vcol["dskip"][0]:vcol["dskip"][1]] = g3("D_skip")[None, :]
    put("gnw", g3("gnorm_w"), 4)

    packs = [np.zeros((P, n), f) for n in sizes]

    def putm(name, a):
        which, lo, hi = mats[name]
        packs[which][:, lo:hi] = a

    for name, a in (("Awk", g0("Awk")), ("Awv", g0("Awv")), ("WqT", g0("Wq").T), ("Awq", g0("Awq")), ("WkT", g0("Wk").T),
                    ("Wgc1", g0("Wgc1")), ("WzT", g0("Wz").T), ("Wg1", g0("Wg1")), ("Wz", g0("Wz")), ("Wgz", g0("Wgz")),
                    ("Wgh", g0("Wgh")), ("Wv", g0("Wv")), ("Awo", g0("Awo")), ("Wf1", g0("Wf1")), ("Wf2", g0("Wf2")),
                    ("Win", g3("in_proj_w")), ("Wout", g3("out_proj_w")), ("Wq3", g3("Wq")), ("Wk3", g3("Wk")),
                    ("Wv3", g3("Wv")), ("Wo3", g3("Wo")), ("Wq2", g2("Wq")), ("Wk2", g2("Wk")), ("Wv2", g2("Wv")),
                    ("Wo2", g2("Wo")), ("fc1T", g1("fc1_w").T)):
        putm(name, chunks(a))
    putm("Wg2c", np.concatenate([g0("Wg2"), g0("Wgc2")], 0))
    rows6 = np.zeros((6, 5, D), f)
    rows6[0:4, 0] = g1("fc2_w").T
    rows6[4, 0] = g1("fc2_b")
    rows6[0:5, 1] = g1("norm3_w")
    rows6[5, 2] = g1("norm3_b")
    rows6[:, 3] = g1("gamma1")
    rows6[:, 4] = g1("gamma2")
    cst, rowc = constants()
    mask = np.zeros((1, 4 * -(-M // 4)), np.uint8)
    mask[:, 0:M] = i["mask_1xS2_bf0"].view(np.uint8)
    xT = i["x"].transpose(2, 0, 1).reshape(DC, P, B, S).transpose(1, 0, 2, 3).reshape(P, -1)
    cT = i["ctx_1024"].transpose(2, 0, 1).reshape(DC, P, B * M).transpose(1, 0, 2).reshape(P, -1)
    arrays = {"xT": xT, "ctxT": cT, "mask": mask.view(np.int32), "vecs": vecs, "m0": packs[0], "m1": packs[1],
              "m2": packs[2], "rows6": rows6.reshape(6, -1), "consts": cst, "rowconsts": rowc}
    arrays = {k: np.ascontiguousarray(a) for k, a in arrays.items()}
    nc = bacc.Bacc("TRN2", target_bir_lowering=False, num_devices=1)
    args = [nc.dram_tensor(f"in_{k}", a.shape, mybir.dt.from_np(a.dtype), kind="ExternalInput").ap() for k, a in arrays.items()]
    out = nc.dram_tensor("out", (P, DC, B, S), F32, kind="ExternalOutput").ap()
    xattn_stack_kernel(nc, *args, out)
    r = run_bass_kernel_spmd(nc, [{f"in_{k}": a for k, a in arrays.items()}], core_ids=[0])
    got = r.results[0]["out"].reshape(P, DC, B, S)
    return np.ascontiguousarray(got.transpose(2, 3, 1, 0).reshape(B, S, D))
```

```python
from contextlib import ExitStack

import numpy as np

import concourse.bass as bass
from concourse import mybir

F32 = mybir.dt.float32
BF16 = mybir.dt.bfloat16
I32 = mybir.dt.int32
U8 = mybir.dt.uint8
ALU = mybir.AluOpType
ACT = mybir.ActivationFunctionType
AX = mybir.AxisListType

P = 128
B, S, D, M = 2, 1024, 256, 77
DC = D // P
T = 512
J = S // T
SUB = T // P
SLOTS = 8
ROWC = -(-SLOTS * M // P)
HALF = 4 * M
DI, DS, HM, PD = 512, 128, 8, 64
XBC = (DI + 2 * DS) // P
TAPS = 4
SWEEPS_BF, SWEEPS_F = 2, 3
FALLBACK_TEST = ALU.is_lt
TOL = 2.0 ** -20


def layout():
    vec, at = {}, 0
    for name, n in (("n1", 2), ("n2", 2), ("bq", 2), ("abq", 2), ("bk", 2), ("bz", 2), ("bv", 2), ("abo", 2),
                    ("bg1c", 1), ("bgz", 2), ("bgh", 2), ("bg2", 2), ("bgc2", 2), ("abk0", 2), ("abv0", 2),
                    ("bf1", 8), ("bf2", 2), ("l1w1", 2), ("l1b1", 2), ("l1w2", 2), ("l1b2", 2), ("fc1b", 1),
                    ("bq2", 2), ("bk2", 2), ("bv2", 2), ("lg2", 2), ("lb2", 2), ("mnw", 2), ("convw", 24),
                    ("convb", 6), ("dtb", 1), ("alog", 1), ("dskip", 8), ("gnw", 4), ("caw", 2), ("cab", 2)):
        vec[name] = (at, at + n)
        at += n
    mats = {}
    at0 = 0
    for name, n in (("Awk", 512), ("Awv", 512), ("WqT", 512), ("Awq", 512), ("WkT", 512), ("Wgc1", 128),
                    ("WzT", 512), ("Wg1", 128), ("Wz", 512), ("Wgz", 512), ("Wg2c", 256), ("Wgh", 512),
                    ("Wv", 512), ("Awo", 512), ("Wf1", 2048), ("Wf2", 2048)):
        mats[name] = (0, at0, at0 + n)
        at0 += n
    at1 = 0
    for name, n in (("Win", 2 * 1288), ("Wout", 1024), ("Wq3", 512), ("Wk3", 512), ("Wv3", 512), ("Wo3", 512)):
        mats[name] = (1, at1, at1 + n)
        at1 += n
    at2 = 0
    for name, n in (("Wq2", 512), ("Wk2", 512), ("Wv2", 512), ("Wo2", 512), ("fc1T", 8)):
        mats[name] = (2, at2, at2 + n)
        at2 += n
    return vec, at, mats, (at0, at1, at2)


CONST = {"ident": (0, 128), "mean": (128, 256), "last": (256, 384), "m32": (384, 388), "m16": (388, 396),
         "future": (396, 524), "ones": (524, 652), "eps6": (652, 653), "eps5": (653, 654), "den": (654, 660), "neg": (660, 661)}
NCONST = 661


def constants():
    c = np.zeros((P, NCONST), np.float32)
    p = np.arange(P)

    def put(name, v):
        c[:, CONST[name][0]:CONST[name][1]] = v

    put("ident", np.eye(P))
    put("mean", 1.0 / D)
    put("last", (p == P - 1)[:, None] * np.ones(P))
    put("m32", (p[:, None] // 32 == np.arange(4)) * 32 ** -0.5)
    put("m16", (p[:, None] // 16 == np.arange(8)) * 16 ** -0.5)
    put("future", np.where(p[:, None] > p[None, :], -1e30, 0.0))
    put("ones", 1.0)
    put("eps6", 1e-6)
    put("eps5", 1e-5)
    rest = np.float32(-1e9)
    for k in range(3):
        unit = 2.0 ** (np.floor(np.log2(abs(rest))) - 7)
        part = np.float32(np.trunc(rest / unit) * unit)
        c[k, CONST["neg"][0]] = part
        rest = np.float32(rest - part)
    put("den", (p == 5)[:, None] * np.ones(6))
    rows = np.zeros((8, HM * P + T), np.float32)
    rows[:, :HM * P] = np.repeat(np.eye(8), P, axis=1)
    rows[:, HM * P:] = np.arange(T) % P != 0
    return c, rows


def xattn_stack_kernel(nc, xT, ctxT, mask, vecs, m0, m1, m2, rows6, consts, rowconsts, outT):
    vcol, nvec, mats, sizes = layout()
    with ExitStack() as ctx:
        def sb(name, shape, dt=F32):
            return ctx.enter_context(nc.sbuf_tensor(name, shape, dt))

        sems = {}

        SHARED = (
            (("count", 1), ("s_mm", 2), ("mr_mm", B), ("q3b_mm", 1)),
            (("g_mm", B * J), ("xr_mm", 4 * J), ("b1_sc", B * J), ("den_mm", 2 * B), ("o2_mm", 4 * J), ("dt_mm", B * J), ("y_mm3", 4 * J)),
            (("z_mm", 4 * J), ("q0_mm", 4 * J), ("b1_tr", B * J), ("o6_mm", 2 * B), ("q2_mm", 4 * J), ("z3_mm", 8 * J), ("q3_mm", 4 * J)),
            (("zg_mm", 4 * J), ("f1_mm", 16 * J), ("h4_mm", B * J), ("p1", 8 * J), ("x2_mm", 8), ("xtk_mm", 8 * J)),
            (("gam_mm", 8 * J), ("f2_mm", B * J), ("wu_mm", B * J), ("p2", 16 * J), ("bt_mm", 8 * J)),
            (("hm", 8 * (SWEEPS_BF + SWEEPS_F + 2)), ("var_mm", B * J), ("een_mm", 8 * J)),
            (("pw", 5), ("y_mm", B * J), ("dmm", 8 * J)),
            (("g6_mm", 2), ("ut_mm", B * J), ("y2_mm", 8 * J)),
            (("nf_mm", 1), ("s_new", 8 * J)),
            (("gg", B * J), ("b1_ex", B * J), ("p2e", 16 * J), ("et", B * J)),
            (("gam", 8 * J), ("ff", 16 * J), ("b1_pt", B * J), ("l1p", B * J)),
            (("g", 8 * (SWEEPS_BF + SWEEPS_F + 2)), ("rm", B * J), ("zs", 8 * J)),
            (("z", 4 * J), ("h4", B * J), ("xs", B * J)),
            (("zg", 4 * J), ("b1_sh", B * J), ("dt1", B * J)),
            (("u", 8 * (SWEEPS_F + 1)), ("b1_ri", B * J)),
        )
        before, home = {}, {}
        for group in SHARED:
            n = 0
            for name, comes in group:
                before[name], home[name] = n, "_".join(g[0] for g in group)
                n += comes
        STARTED = {"vector": ("opg", "x1", "x3", "x4", "y", "xh"), "gpsimd": ("dx",)}
        for names in STARTED.values():
            for name in names:
                before[name] = 1

        def begin(eng, engine):
            for name in STARTED[engine]:
                eng.sem_inc(sem(name), 1)

        def sem(name):
            name = home.get(name, name)
            if name not in sems:
                sems[name] = ctx.enter_context(nc.semaphore(name))
            return sems[name]

        def after(name, n):
            return sem(name), n + before.get(name, 0)

        X = sb("X", [P, DC, B, S])
        CX = sb("CX", [P, DC, B * M])
        CN = sb("CN", [P, NCONST])
        RC = sb("RC", [8, HM * P + T])
        VC = sb("VC", [P, nvec])
        WA = sb("WA", [P, sizes[0]])
        WB = sb("WB", [P, sizes[2]])
        R6 = WA[0:6, sizes[1]:sizes[1] + 5 * D].rearrange("p (a n) -> p a n", a=5)
        KB = sb("KB", [P, B, 2, 2 * HALF])
        VB = sb("VB", [P, B, 2, 6, P])
        VS = sb("VS", [M, B, D])
        CB = sb("CB", [P, 32])
        MX = sb("MX", [P, B, 2, SLOTS])
        IR = sb("IR", [P, B * J, SUB])
        RS = sb("RS", [P, B, 2, SLOTS])
        ARENA = 26640
        AR = sb("AR", [P, ARENA])
        ps = ctx.enter_context(nc.psum_tensor("ps", [P, 8, 512], F32))

        def cn(name, rows=P):
            return CN[0:rows, CONST[name][0]:CONST[name][1]]

        def v(name, k=0):
            return VC[:, vcol[name][0] + k:vcol[name][0] + k + 1]

        def w(name, chunks):
            which, lo, hi = mats[name]
            return (WA, WA, WB)[which][:, lo:hi].rearrange("p (c n) -> p c n", c=chunks)

        class Carver:

            def __init__(self, at=0):
                self.at = at

            def take(self, *shape, parts=P):
                n = int(np.prod(shape))
                a = AR[0:parts, self.at:self.at + n]
                self.at += n
                assert self.at <= ARENA, self.at
                if len(shape) == 1:
                    return a
                names = "abcdef"[:len(shape)]
                pat = "p (" + " ".join(names) + ") -> p " + " ".join(names)
                return a.rearrange(pat, **{k: s for k, s in zip(names[:-1], shape[:-1])})

        c1 = Carver()
        XN = c1.take(DC, B, S)
        H = c1.take(DC, B, J, T + 1)
        lower = c1.at
        Z = c1.take(DC, B, S)
        ZG = c1.take(DC, B, S)
        OPG = c1.take(DC, B, S)
        sweeps_at = c1.at
        UG = [[c1.take(T) for _ in range(DC)] for _ in range(B)]
        GZ = [[c1.take(T) for _ in range(DC)] for _ in range(B)]
        AA = [[c1.take(T) for _ in range(DC)] for _ in range(B)]
        HB = VB[:, :, :, :, :].rearrange("p a b c d -> p (a b c d)")[:, 0:DC * B * J * (T + 2) // 2].bitcast(BF16).rearrange(
            "p (c b j s) -> p c b j s", c=DC, b=B, j=J)
        WGB = KB[:, :, :, :].rearrange("p a b c -> p (a b c)")[:, 0:DC * D // 2].bitcast(BF16).rearrange(
            "p (c n) -> p c n", c=DC)
        OKC = sb("OKC", [P, 8])
        TOT = sb("TOT", [1, 4])
        FLAG = sb("FLAG", [1, 4], I32)
        UX = sb("UX", [P, 4, DC, B])
        c1b = Carver(sweeps_at)
        SQ = [c1b.take(DC, T) for _ in range(B)]
        RT = [c1b.take(T) for _ in range(B)]
        GG = [c1b.take(T) for _ in range(B)]
        UNITS = range(B * J)
        SQR1 = SQ + [c1b.take(DC, T) for _ in range(B)]
        RTR1 = RT + GG
        c1c = Carver(DC * B * S)
        GB = [c1c.take(DC, T) for _ in range(B)]
        assert c1c.at <= lower
        c3 = Carver(lower)
        QS = [c3.take(DC, T) for _ in range(B)]
        PT = [c3.take(6, T) for _ in range(B)]
        ST = [c3.take(DC, T) for _ in range(B)]
        PF = [[c3.take(ROWC * P) for _ in range(2)] for _ in range(B)]
        PR = [[PF[b][k][:, 0:SLOTS * M].rearrange("p (h m) -> p h m", h=SLOTS) for k in range(2)] for b in range(B)]
        XC = [c3.take(DC, T) for _ in range(B)]
        RTB = [c3.take(T) for _ in range(B)]
        FH = [[QS[b][:, k, :] if k < 2 else PT[b][:, k - 2, :] for k in range(8)] for b in range(B)]
        c4 = Carver(c3.at)
        NX = c4.take(DC, B * M)
        NXS = c4.take(DC, B * M)
        NF = c4.take(B, 4)
        FT6 = c4.take(DC, 6)
        ET6 = c4.take(DC, 6)
        UT = c4.take(B, SUB * J, 8)
        MN = c4.take(B, SUB * J, 4)
        MB = c4.take(B * SUB * J * 2).bitcast(BF16).rearrange("p (b t k) -> p b t k", b=B, t=SUB * J)
        MR = c4.take(B, SUB * J)
        c4r = Carver(0)
        F6C = c4r.take(D)
        E6 = c4r.take(D)
        E1 = c4r.take(D)
        EC = c4r.take(D)
        G6 = c4r.take(8)
        GS = c4r.take(8)
        U5 = c4r.take(B, S)
        UP = c4r.take(3 * B * S // 2).bitcast(BF16).rearrange("p (k b s) -> p k b s", k=3, b=B)
        ROWS1 = 9 * 6
        flat = VB[:, :, :, :, :].rearrange("p a b c d -> p (a b c d)")
        YP = flat[:, 0:3 * B * S // 2].bitcast(BF16).rearrange("p (k b s) -> p k b s", k=3, b=B)
        flat = KB[:, :, :, :].rearrange("p a b c -> p (a b c)")
        US = flat[:, 0:B * S // 2].bitcast(BF16).rearrange("p (b s) -> p b s", b=B)
        YS = flat[:, B * S // 2:B * S].bitcast(BF16).rearrange("p (b s) -> p b s", b=B)
        MP3 = c4r.take(B * S // 2).bitcast(BF16).rearrange("p (b s) -> p b s", b=B)
        assert c4r.at <= lower
        PE1 = [[PT[b][:, k, :] for k in range(4)] for b in range(B)]
        XC1, SQ1 = XC + QS, ST + [PT[b][:, 0:2] for b in range(B)]
        RT1 = RTB + [PT[b][:, 2] for b in range(B)]
        PT1 = [a[0:M, 0, :] for a in XC1]
        U6S = [PT[q % B][:, 4 + q // B, :] for q in UNITS]
        WU1, YR = [a[:, 0, :] for a in SQ1], [a[:, 1, :] for a in SQ1]
        UR = WU1
        RM = [ST[b][:, 1, :] for b in range(B)]
        c7 = Carver(0)
        XBW = XBC * (T + TAPS - 1)
        xb = [c7.take(XBW) for _ in range(B)]
        XB = [a.rearrange("p (c n) -> p c n", c=XBC) for a in xb]
        CV = [c7.take(XBC, T) for _ in range(B)]
        ZS = [c7.take(SUB, DI) for _ in range(B)]
        LAM = [c7.take(T) for _ in range(B)]
        ROWS = [c7.take(T) for _ in range(B)]
        LNG = [c7.take(T) for _ in range(B)]
        RB = [c7.take(HM, P) for _ in range(B)]
        BT = [c7.take(224) for _ in range(B)]
        STATE = [c7.take(DI) for _ in range(B)]
        HIST = [c7.take(XBC, TAPS - 1) for _ in range(B)]
        XN3 = [c7.take(DC, T) for _ in range(B)]
        YT = [c7.take(DI) for _ in range(B)]
        IDB = c7.take(P // 2).bitcast(BF16)
        FUTB = c7.take(P // 2).bitcast(BF16)
        SSQ = c7.take(B, SUB)
        SSR = c7.take(B, SUB)
        EEN = c7.take(B, HM)
        SQ7 = [CV[b][:, 0:2, :] for b in range(B)]
        RT7 = [CV[b][:, 2, :] for b in range(B)]
        ET = YT
        DM = [xb[b][:, 0:1024].rearrange("p (h n) -> p h n", h=HM) for b in range(B)]
        XTK = [xb[b][:, 1024:1536] for b in range(B)]
        DTX = [xb[b][:, 1536:2048] for b in range(B)]
        WX = [xb[b][:, 2048:2560] for b in range(B)]
        SE = [xb[b][:, 2560:3072] for b in range(B)]
        TOT6 = sb("TOT6", [6, 2])
        MKU = sb("MKU", [P, -(-M // 4)], I32)
        KEEP = sb("KEEP", [P, M])
        NEG3 = sb("NEG3", [3, HALF], BF16)
        ONESB = sb("ONESB", [3, P], BF16)

        class Chain:
            PER = 160

            def __init__(self, eng, name):
                self.eng, self.sem, self.base, self.n, self.j = eng, sem(name), 0, 0, 0

            def link(self, ins):
                self.n += 1
                ins.then_inc(self.sem, 1)
                self.eng.wait_ge(self.sem, self.j * self.PER + (self.base + self.n))

            def enter(self, j):
                self.base += self.n
                self.n, self.j = 0, j

            def turn(self):
                assert self.n < self.PER, self.n
                self.eng.sem_inc(self.sem, self.PER - self.n)

            def leave(self, trips):
                self.base += self.PER * trips
                self.n, self.j = 0, 0

        def mm(out, lhsT, rhs, first=True, last=True):
            return nc.tensor.matmul(out, lhsT, rhs, start=first, stop=last)

        def nk(j, per, k):
            return j * per + (k + 1)

        def n2(j, b):
            return nk(j, B, b)

        def tj(j):
            return bass.ds(j * T, T)

        def feat(w_, c, mo):
            return w_[:, c, mo * P:(mo + 1) * P]

        def bc(a, n, axis):
            a = a.unsqueeze(axis)
            shape = list(a.shape)
            shape[axis] = n
            return a.broadcast_to(shape)

        def bank(b, k):
            return ps[:, 4 * b + k, :]

        def bank1(q, k):
            return ps[:, 2 * q + k, :]

        def part_of(q):
            return q % B, slice(q // B * T, (q // B + 1) * T)

        BS = range(B)
        vidx = {"CQb": 0, "gcb": 2, "zgb": 3, "xob": 5, "q3b": 7, "A": 9}

        def cb(name, k=0):
            return CB[:, vidx[name] + k:vidx[name] + k + 1]

        CQ = w("WqT", 2)
        CG = w("WkT", 2)

        NORMS = {"r1": 0, "r2": B * J, "l1": 2 * B * J, "x3": 3 * B * J, "r3": 4 * B * J, "l3": 5 * B * J}
        CENTRED = {"l1": 0, "x3": B * J, "l3": 2 * B * J}
        DIAGS = {"r1": 0, "r2": B * J, "l1": 2 * B * J, "den": 4 * B * J, "x3": 4 * B * J + 2 * B, "r3": 5 * B * J + 2 * B, "l3": 6 * B * J + 2 * B}
        RT_OF = {"r1": RTR1, "r2": RTB, "l1": RT1, "x3": RTB, "r3": RT7, "l3": RTB}
        LAYER = {"a0": 0, "a2": 1, "a3": 2}
        STEPS = {"a0": 0, "a2": 8 * J, "a3": 24 * J}
        CHUNKS = {"a0": 0, "a2": 4 * J, "a3": 8 * J}

        def spread_pe(to, diag, width=T, rows=P):
            return mm(to[0:rows, 0:width], cn("ones")[:, 0:rows], diag[:, 0:width])

        def diagonal(diag, col):
            nc.vector.tensor_tensor(diag.rearrange("p (k n) -> p k n", k=SUB), bc(cn("ident"), SUB, 1), bc(col, P, 2), ALU.mult).then_inc(sem("diag"), 1)

        def norm_pe(pe, p, j, sq, mean, units=BS, at=bank, meanwhile=None):
            if mean:
                for b in units:
                    pe.wait_ge(*after("norm_sum", CENTRED[p] + n2(j, b)))
                    mm(at(b, 0), cn("mean"), sq[b][:, 0, :]).then_inc(sem("norm_mean"), 1)
            if meanwhile:
                meanwhile(0)
            for b in units:
                pe.wait_ge(*after("norm_sqs", NORMS[p] + n2(j, b)))
                for k in range(SUB):
                    last = mm(at(b, 1)[:, k:k + 1], sq[b][:, 0, k * P:(k + 1) * P], cn("mean")[:, 0:1])
                last.then_inc(sem("norm_ms"), 1)
            if meanwhile:
                meanwhile(1)
            for b in units:
                pe.wait_ge(*after("diag", DIAGS[p] + n2(j, b)))
                spread_pe(at(b, 1), RT_OF[p][b]).then_inc(sem("norm_r"), 1)

        def norm_act(act, p, j, src, sq, eps, mean, xc=None, units=BS, at=bank):
            for b in units:
                if mean:
                    act.wait_ge(*after("norm_xc", CENTRED[p] + n2(j, b)))
                nc.scalar.activation(sq[b][:, :, :], xc[b] if mean else src(b), ACT.Square).then_inc(sem("norm_sq"), 1)
            for b in units:
                act.wait_ge(*after("norm_ms", NORMS[p] + n2(j, b)))
                nc.scalar.activation(IR[:, b, :], at(b, 1)[:, 0:SUB], ACT.Sqrt, bias=cn(eps)).then_inc(sem("norm_rt"), 1)

        def norm_dve(dve, ch, p, j, src, rt, out, mean, xc=None, sq=None, units=BS, at=bank):
            if mean:
                for b in units:
                    nc.vector.tensor_tensor(sq[b][:, 0, :], src(b)[:, 0], src(b)[:, 1], ALU.add).then_inc(sem("norm_sum"), 1)
                for b in units:
                    dve.wait_ge(*after("norm_mean", CENTRED[p] + n2(j, b)))
                    nc.vector.tensor_tensor(xc[b], src(b), bc(at(b, 0), DC, 1), ALU.subtract).then_inc(sem("norm_xc"), 1)
            for b in units:
                dve.wait_ge(*after("norm_sq", NORMS[p] + n2(j, b)))
                nc.vector.tensor_tensor(sq[b][:, 0], sq[b][:, 0], sq[b][:, 1], ALU.add).then_inc(sem("norm_sqs"), 1)
            for b in units:
                dve.wait_ge(*after("norm_rt", NORMS[p] + n2(j, b)))
                ch.link(nc.vector.reciprocal(IR[:, b, :], IR[:, b, :]))
                diagonal(rt[b], IR[:, b, :])
            for b in units:
                dve.wait_ge(*after("norm_r", NORMS[p] + n2(j, b)))
                nc.vector.tensor_tensor(out(b), xc[b] if mean else src(b), bc(at(b, 1), DC, 1), ALU.mult).then_inc(sem("norm_xn"), 1)

        K_BANK, V_BANK = {"a0": 2, "a2": 0, "a3": 0}, {"a0": 6, "a2": 2, "a3": 2}

        def keys_pe(pe, p, wk):
            for g in range(2):
                for c in range(DC):
                    last = mm(ps[:, K_BANK[p] + g, 0:B * M], feat(wk, c, g), CX[:, c, :], c == 0, c == DC - 1)
                last.then_inc(sem("kv_kp"), 1)

        def values_pe(pe, p, wv):
            for b in BS:
                for c in range(DC):
                    last = mm(ps[0:M, V_BANK[p], b * D:(b + 1) * D], CX[:, c, b * M:(b + 1) * M], wv[:, c, :], c == 0, c == DC - 1)
            last.then_inc(sem("kv_vp"), 1)

        def prep_act(act, p):
            act.wait_ge(*after("kv_vp", LAYER[p] + 1))
            nc.scalar.activation(VS[:, :, :].rearrange("m b n -> m (b n)"), ps[0:M, V_BANK[p], :], ACT.Copy).then_inc(sem("kv_vs"), 1)

        def prep_dve(dve, ch, p, bias, hg, masked=False):
            for g in range(2):
                dve.wait_ge(*after("kv_kp", 2 * LAYER[p] + g + 1))
                for b in BS:
                    out = KB[:, b, g, 0:hg * M].rearrange("p (h m) -> p h m", h=hg)
                    ins = nc.vector.scalar_tensor_tensor(out=out, in0=bc(ps[:, K_BANK[p] + g, b * M:(b + 1) * M], hg, 1), scalar=v(bias, g) if bias else 0.0,
                                                         in1=bc(cn("m32" if hg == 4 else "m16"), M, 2), op0=ALU.add, op1=ALU.mult)
                    if masked:
                        ch.link(ins)
                        ins = nc.vector.tensor_tensor(out, out, bc(KEEP[:, :], hg, 1), ALU.mult)
                    ins.then_inc(sem("kv_kb"), 1)

        def prep_sp(sp, p, hg):
            sp.wait_ge(*after("kv_vz", LAYER[p] + 1))
            sp.wait_ge(*after("kv_vs", LAYER[p] + 1))
            width = P // hg
            for head, m, k, chunk, part in pieces(hg):
                g = head // hg
                for b in BS:
                    sp.dma_start(VB[part:part + k, b, g, chunk, head % hg * width:(head % hg + 1) * width],
                                 VS[m:m + k, b, head * width:(head + 1) * width]).then_inc(sem("kv_vb"), 16)

        def pieces(hg):
            out = []
            for head in range(2 * hg):
                m = 0
                while m < M:
                    chunk, part = divmod(M * (head % SLOTS) + m, P)
                    k = min(M - m, P - part)
                    out.append((head, m, k, chunk, part))
                    m += k
            return out

        def steps(units):
            return [(u, s, b) for u in range(units) for s in range(SUB) for b in BS]

        def attn_pe(pe, p, j, units, masked=False):
            seq = steps(units)
            per = len(seq)
            pe.wait_ge(*after("kv_kb", 4 * (LAYER[p] + 1)))
            for n in range(per + 3):
                if n < per:
                    u, s, b = seq[n]
                    pe.wait_ge(*after("att_q", CHUNKS[p] + nk(j, 4, 2 * b + 1)))
                    if n >= 2:
                        pe.wait_ge(*after("att_ex", STEPS[p] + nk(j, per, n - 2)))
                    for half in range(2):
                        chunk = half if units == 1 else u
                        cols = slice(0, HALF) if units == 1 else slice(half * HALF, (half + 1) * HALF)
                        last = mm(bank(b, half)[:, 0:HALF], QS[b][:, chunk, s * P:(s + 1) * P], KB[:, b, chunk, cols], True, not masked)
                        if masked:
                            last = mm(bank(b, half)[:, 0:HALF], ONESB[0:3, :], NEG3[0:3, :], False, True)
                    last.then_inc(sem("att_sc"), 1)
                if 2 <= n < per + 2:
                    u, s, b = seq[n - 2]
                    pe.wait_ge(*after("att_pn", STEPS[p] + nk(j, per, n - 2)))
                    if n >= 4:
                        pe.wait_ge(*after("att_ctx", STEPS[p] + nk(j, per, n - 4)))
                    flat = PF[b][((n - 2) // 2) % 2]
                    for k in range(ROWC):
                        last = nc.tensor.transpose(bank(b, 2 + k // 4)[:, (k % 4) * P:(k % 4 + 1) * P], flat[:, k * P:(k + 1) * P], cn("ident"))
                    last.then_inc(sem("att_tr"), 1)
                if n >= 3:
                    u, s, b = seq[n - 3]
                    if n == 3:
                        pe.wait_ge(*after("kv_vb", 16 * sum(B * len(pieces(h)) for h in (4, 8, 4)[:LAYER[p] + 1])))
                    pe.wait_ge(*after("att_ta", STEPS[p] + nk(j, per, n - 3)))
                    for g in range(2 if units == 1 else 1):
                        chunks = range(HALF * g // P, (HALF * (g + 1) - 1) // P + 1) if units == 1 else range(ROWC)
                        for k in chunks:
                            last = mm(bank(b, 3)[:, (1 + g) * P:(2 + g) * P], VB[:, b, g if units == 1 else u, k, :], PT[b][:, k, s * P:(s + 1) * P],
                                      k == chunks[0], k == chunks[-1])
                    last.then_inc(sem("att_pv"), 1)

        def attn_act(act, p, j, units):
            seq = steps(units)
            per = len(seq)
            for n in range(per + 2):
                if n < per:
                    u, s, b = seq[n]
                    k = (n // 2) % 2
                    pr = PR[b][k]
                    act.wait_ge(*after("att_mx", STEPS[p] + nk(j, per, n)))
                    for h in range(4, SLOTS):
                        nc.scalar.activation(pr[:, h, 0:M], bank(b, 1)[:, (h - 4) * M:(h - 3) * M], ACT.Exp, bias=MX[:, b, k, h:h + 1],
                                             accum_out=RS[:, b, k, h:h + 1])
                    act.wait_ge(*after("att_sh", STEPS[p] + nk(j, per, n)))
                    nc.scalar.activation(pr[:, 0:4, 0:M], pr[:, 0:4, 0:M], ACT.Exp).then_inc(sem("att_ex"), 1)
                if n >= 2:
                    u, s, b = seq[n - 2]
                    act.wait_ge(*after("att_tr", STEPS[p] + nk(j, per, n - 2)))
                    tr = ps[:, 4 * b + 2:4 * b + 4, :].rearrange("p g (k t) -> p (g k) t", k=4)
                    nc.scalar.activation(PT[b][:, 0:ROWC, s * P:(s + 1) * P], tr[:, 0:ROWC, :], ACT.Copy).then_inc(sem("att_ta"), 1)

        def attn_dve(dve, ch, p, j, units, bias):
            seq = steps(units)
            per = len(seq)
            for n in range(per + 4):
                if n >= 4:
                    u, s, b = seq[n - 4]
                    dve.wait_ge(*after("att_pv", STEPS[p] + nk(j, per, n - 4)))
                    if bias is None:
                        ins = nc.vector.tensor_copy(ST[b][:, :, s * P:(s + 1) * P], bank(b, 3)[:, P:3 * P].rearrange("p (g t) -> p g t", g=2))
                    for g in range(2 if units == 1 else 1) if bias else ():
                        c = g if units == 1 else u
                        ins = nc.vector.tensor_scalar(ST[b][:, c, s * P:(s + 1) * P], bank(b, 3)[:, (1 + g) * P:(2 + g) * P], v(bias, c), None, ALU.add)
                    ins.then_inc(sem("att_ctx"), 1)
                if n < per:
                    u, s, b = seq[n]
                    k = (n // 2) % 2
                    pr = PR[b][k]
                    sc = ps[:, 4 * b:4 * b + 2, 0:HALF].rearrange("p g (h m) -> p g h m", h=4)
                    pr4 = pr.rearrange("p (g h) m -> p g h m", g=2)[:, :, :, 0:M]
                    mx = MX[:, b, k, :].rearrange("p (g h) -> p g h", g=2)
                    dve.wait_ge(*after("att_sc", STEPS[p] + nk(j, per, n)))
                    nc.vector.tensor_reduce(mx, sc, AX.X, ALU.max, negate=True).then_inc(sem("att_mx"), 1)
                    dve.wait_ge(*after("att_mx", STEPS[p] + nk(j, per, n)))
                    nc.vector.tensor_tensor(pr4[:, 0], sc[:, 0], bc(mx[:, 0], M, 2), ALU.add).then_inc(sem("att_sh"), 1)
                if 1 <= n <= per:
                    b = seq[n - 1][2]
                    k = ((n - 1) // 2) % 2
                    dve.wait_ge(*after("att_ex", STEPS[p] + nk(j, per, n - 1)))
                    ch.link(nc.vector.tensor_reduce(RS[:, b, k, 0:4], PR[b][k][:, 0:4, 0:M], AX.X, ALU.add))
                    nc.vector.reciprocal(RS[:, b, k, :], RS[:, b, k, :]).then_inc(sem("att_ri"), 1)

        def attn_pool(pool, p, j, units):
            seq = steps(units)
            per = len(seq)
            for n, (u, s, b) in enumerate(seq):
                k = (n // 2) % 2
                pr = PR[b][k][:, :, 0:M]
                pool.wait_ge(*after("att_ri", STEPS[p] + nk(j, per, n)))
                nc.gpsimd.tensor_tensor(pr, pr, bc(RS[:, b, k, :], M, 2), ALU.mult).then_inc(sem("att_pn"), 1)

        def pool_takes(q, mo):
            return q % 2 == 1 and mo == 1

        def lin_pe(pe, sig, j, wname_or_ap, rhs, order, ready=None, batches=BS):
            for b in batches:
                if ready is not None:
                    ready(b)
                for mo in range(DC):
                    for c in range(DC):
                        last = mm(bank(b, order[mo]), feat(wname_or_ap, c, mo), rhs(b, c), c == 0, c == DC - 1)
                    last.then_inc(sem(sig), 1)

        block = ctx.enter_context(nc.Block())

        def xs(b, j):
            return X[:, :, b, tj(j)]

        @block.sync
        def _(sp):
            sp.dma_start(VC[:, :], vecs).then_inc(sem("ld_vec"), 16)
            sp.dma_start(CN[:, :], consts).then_inc(sem("ld_cn"), 16)
            sp.dma_start(CX[:, :, :].rearrange("p c n -> p (c n)"), ctxT).then_inc(sem("ld_cx"), 16)
            a, z_ = mats["WqT"][1], mats["Awo"][2]
            sp.dma_start(WA[:, a:z_], m0[:, a:z_]).then_inc(sem("ld_w0"), 16)
            sp.dma_start(WA[:, 0:a], m0[:, 0:a]).then_inc(sem("ld_kv0"), 16)
            sp.dma_start(WA[:, z_:sizes[0]], m0[:, z_:sizes[0]]).then_inc(sem("ld_ffn"), 16)
            sp.dma_start(RC[:, :], rowconsts).then_inc(sem("ld_rc"), 16)
            sp.dma_start(WB[:, :], m2).then_inc(sem("ld_w12"), 16)
            sp.dma_start(MKU[:, :], mask.broadcast_to([P, -(-M // 4)])).then_inc(sem("ld_mask"), 16)
            prep_sp(sp, "a0", 4)
            sp.wait_ge(*after("x1", B * J))
            sp.dma_start(WA[0:6, sizes[1]:sizes[1] + 5 * D], rows6).then_inc(sem("ld_r6"), 16)
            sp.dma_start(WA[:, 0:sizes[1]], m1).then_inc(sem("ld_w3"), 16)
            sp.wait_ge(*after("y1s", 1))
            for part in range(3):
                sp.wait_ge(*(after("u_parts", (part + 1) * B * J) if part < 2 else after("u_low", B * J)))
                for k in range(3):
                    sp.dma_start(US[6 * (3 * part + k):6 * (3 * part + k) + 6], UP[0:6, part]).then_inc(sem("pairs"), 16)
                sp.wait_ge(*(after("y_parts", (part + 1) * B * J) if part < 2 else after("y_low", B * J)))
                for k in range(3):
                    sp.dma_start(YS[6 * (3 * k + part):6 * (3 * k + part) + 6], YP[0:6, part]).then_inc(sem("pairs"), 16)
            sp.wait_ge(*after("mrow", B))
            sp.dma_start(US[ROWS1:ROWS1 + 3], MP3[0:3]).then_inc(sem("pairs"), 16)
            prep_sp(sp, "a2", 8)
            prep_sp(sp, "a3", 4)
            with sp.Fori(0, J) as j:
                for b in BS:
                    sp.wait_ge(*after("y", n2(j, b)))
                    sp.dma_start(outT[:, :, b, tj(j)], X[:, :, b, tj(j)]).then_inc(sem("st"), 16)
            sp.wait_ge(*after("st", 16 * B * J))

        @block.gpsimd
        def _(pool):
            begin(pool, "gpsimd")
            nc.gpsimd.dma_start(X[:, :, :, :].rearrange("p c b s -> p (c b s)"), xT).then_inc(sem("ld_x"), 16)
            def products(j, factors):
                for q in range(2 * B):
                    jj, b = q // B, q % B
                    for mo in range(DC):
                        pool.wait_ge(*after("g", nk(j, 8, 2 * q + mo)))
                        if factors and pool_takes(q, mo):
                            pool.wait_ge(*after("h", nk(j, 8, 4 + 2 * q + mo)))
                            nc.gpsimd.tensor_tensor(AA[b][mo], OPG[:, mo, b, jj * T:(jj + 1) * T], UG[b][mo], ALU.subtract)
                        nc.gpsimd.tensor_tensor(GZ[b][mo], UG[b][mo], Z[:, mo, b, jj * T:(jj + 1) * T], ALU.mult).then_inc(sem("gz"), 1)
            with pool.Fori(0, SWEEPS_BF + 1) as j:
                products(j, False)
            with pool.Fori(SWEEPS_BF + 1, SWEEPS_BF + SWEEPS_F + 1) as j:
                products(j, True)
            products(SWEEPS_BF + SWEEPS_F + 1, False)
            pool.wait_ge(*after("ld_ffn", 16))
            pool.wait_ge(*after("h", 8 * (SWEEPS_BF + SWEEPS_F + 2)))
            for c in range(DC):
                nc.gpsimd.tensor_scalar(w("Wf1", 2)[:, c, :], w("Wf1", 2)[:, c, :], v("n2", c), None, ALU.mult).then_inc(sem("wf1"), 1)
            nc.gpsimd.memset(VB[:, :, :, :, :].rearrange("p a b c d -> p (a b c d)"), 0.0).then_inc(sem("kv_vz"), 1)
            pool.wait_ge(*after("decided", 1))
            for b in BS:
                for k in range(2):
                    nc.gpsimd.memset(PF[b][k][:, SLOTS * M:], 0.0).then_inc(sem("pr0"), 1)
            with pool.Fori(0, J) as j:
                attn_pool(pool, "a0", j, 1)
            pool.wait_ge(*after("x1", B * J))
            nc.gpsimd.memset(YS[0:ROWS1 + 3].rearrange("p b s -> p (b s)"), 1.0).then_inc(sem("y1s"), 1)
            nc.gpsimd.memset(U5[0:32].rearrange("p b s -> p (b s)"), 1.0).then_inc(sem("us1"), 1)
            for q in UNITS:
                nc.gpsimd.memset(U6S[q][0:6], 1.0).then_inc(sem("us1"), 1)
            pool.wait_ge(*after("y1s", 1))
            pool.wait_ge(*after("us1", 1 + B * J))
            for q in UNITS:
                pool.wait_ge(*after("b1_ri", q + 1))
                pr = PR[q % B][q // B][:, 0:4, 0:M]
                nc.gpsimd.tensor_tensor(pr, pr, bc(RS[:, q % B, q // B, 0:4], M, 2), ALU.mult).then_inc(sem("b1_pn"), 1)
            pool.wait_ge(*after("pairs", 16 * 18))
            nc.gpsimd.memset(VB[:, :, :, :, :].rearrange("p a b c d -> p (a b c d)"), 0.0).then_inc(sem("kv_vz"), 1)
            pool.wait_ge(*after("x2", 4 * B))
            with pool.Fori(0, J) as j:
                attn_pool(pool, "a2", j, 2)
            pool.wait_ge(*after("x3", 4 * J))
            for b in BS:
                nc.gpsimd.memset(HIST[b].rearrange("p c n -> p (c n)"), 0.0).then_inc(sem("m0"), 1)
            for b in BS:
                nc.gpsimd.memset(STATE[b], 0.0).then_inc(sem("m0"), 1)
                nc.gpsimd.memset(ROWS[b][0:96], 0.0).then_inc(sem("m0"), 1)
                nc.gpsimd.memset(LNG[b][0:40], 0.0).then_inc(sem("m0"), 1)
                nc.gpsimd.memset(RB[b][0:40].rearrange("p h n -> p (h n)"), 0.0).then_inc(sem("m0"), 1)
            nc.gpsimd.memset(VB[:, :, :, :, :].rearrange("p a b c d -> p (a b c d)"), 0.0).then_inc(sem("kv_vz"), 1)
            pool.wait_ge(*after("m0", 10))
            pool.wait_ge(*after("kv_vz", 3))
            pool.wait_ge(*after("ld_rc", 16))
            for b in BS:
                nc.gpsimd.memset(LNG[b][32:40], 1.0).then_inc(sem("m1"), 1)
                nc.gpsimd.tensor_copy(RB[b][0:8].rearrange("p h n -> p (h n)"), RC[:, 0:HM * P]).then_inc(sem("m1"), 1)
            with pool.Fori(0, J) as j:
                for s in range(SUB):
                    for b in BS:
                        k = 2 * s + b
                        if s == 0:
                            pool.wait_ge(*after("lam", n2(j, b)))
                        else:
                            pool.wait_ge(*after("dmm", nk(j, 8, k - 2)))
                        pool.wait_ge(*after("dx", j * 8 + k))
                        nc.gpsimd.tensor_tensor(RB[b][32:40], bc(LAM[b][0:8, s * P:(s + 1) * P], HM, 1),
                                                RC[:, 0:HM * P].rearrange("p (h n) -> p h n", h=HM), ALU.mult).then_inc(sem("rb"), 1)
                        pool.wait_ge(*after("rb", nk(j, 8, k)))
                        pool.wait_ge(*after("xtk", nk(j, 8, k)))
                        pool.wait_ge(*after("bt", nk(j, 8, k)))
                        x3 = XTK[b].rearrange("p (h n) -> p h n", h=HM)
                        nc.gpsimd.tensor_tensor(WX[b].rearrange("p (h n) -> p h n", h=HM), x3, bc(BT[b][:, P + 64:P + 72], PD, 2), ALU.mult).then_inc(sem("wx"), 1)
                        pool.wait_ge(*after("dtx", nk(j, 8, k)))
                        pool.wait_ge(*after("wx", nk(j, 8, k)))
                        nc.gpsimd.tensor_tensor(x3, x3, bc(VC[:, vcol["dskip"][0]:vcol["dskip"][1]], PD, 2), ALU.mult).then_inc(sem("dx"), 1)
            pool.wait_ge(*after("x4", B * J))
            for b in BS:
                for k in range(2):
                    nc.gpsimd.memset(PF[b][k][:, SLOTS * M:], 0.0).then_inc(sem("pr0"), 1)
            with pool.Fori(0, J) as j:
                attn_pool(pool, "a3", j, 1)

        @block.tensor
        def _(pe):
            pe.wait_ge(*after("ld_cn", 16))
            pe.wait_ge(*after("ld_vec", 16))
            norm_pe(pe, "r1", 0, SQR1, False, UNITS, lambda q, k: ps[:, q, :])
            pe.wait_ge(*after("ld_w0", 16))
            wq, wk_, wz = w("WqT", 2), w("WkT", 2), w("WzT", 2)
            for m in range(DC):
                for c in range(DC):
                    last = mm(ps[:, 4, m * D:(m + 1) * D], wq[:, c, m * P:(m + 1) * P], w("Awq", 2)[:, c, :], c == 0, c == DC - 1)
                last.then_inc(sem("pw"), 1)
            for m in range(DC):
                for c in range(DC):
                    mm(ps[:, 5, m * P:m * P + 64], wz[:, c, m * P:(m + 1) * P], w("Wg1", 2)[:, c, :], c == 0, c == DC - 1)
                for c in range(DC):
                    last = mm(ps[:, 5, m * P + 64:(m + 1) * P], wk_[:, c, m * P:(m + 1) * P], w("Wgc1", 2)[:, c, :], c == 0, c == DC - 1)
                last.then_inc(sem("pw"), 1)
            for mo in range(DC):
                for c in range(DC):
                    last = mm(ps[:, 6, mo:mo + 1], feat(w("Awq", 2), c, mo), v("bq", c), c == 0, c == DC - 1)
            for c in range(DC):
                mm(ps[0:64, 7, 0:1], w("Wg1", 2)[:, c, :], v("bz", c), c == 0, c == DC - 1)
            for c in range(DC):
                last = mm(ps[64:128, 7, 0:1], w("Wgc1", 2)[:, c, :], v("bk", c), c == 0, c == DC - 1)
            last.then_inc(sem("pw"), 1)
            pe.wait_ge(*after("wready", 1))
            with pe.Fori(0, J) as j:
                pe.wait_ge(*after("opg", j * B))
                pe.wait_ge(*after("norm_xn", NORMS["r1"] + B * J))
                lin_pe(pe, "z_mm", j, w("Wz", 2), lambda b, c: XN[:, c, b, tj(j)], (2, 3))
                for b in BS:
                    for c in range(DC):
                        last = mm(bank(b, 1), CG[:, c, 0:P], XN[:, c, b, tj(j)], c == 0, c == DC - 1)
                    last.then_inc(sem("g_mm"), 1)
                for b in BS:
                    pe.wait_ge(*after("z", nk(j, 4, 2 * b + 1)))
                    for mo in range(DC):
                        for c in range(DC):
                            last = mm(bank(b, 2 * mo), feat(w("Wgz", 2), c, mo), Z[:, c, b, tj(j)], c == 0, c == DC - 1)
                        last.then_inc(sem("zg_mm"), 1)
                for b in BS:
                    pe.wait_ge(*after("gg", n2(j, b)))
                    for k, (lo, mo, to) in enumerate(((0, 0, 3), (0, 1, 1), (64, 0, 0), (64, 1, 2))):
                        if k == 2:
                            pe.wait_ge(*after("zg", nk(j, 4, 2 * b + 1)))
                        mm(bank(b, to), WA[lo:lo + 64, mats["Wg2c"][1] + mo * P:mats["Wg2c"][1] + (mo + 1) * P], GG[b][lo:lo + 64, :]).then_inc(sem("gam_mm"), 1)

            pe.wait_ge(*after("opg", B * J))

            def sweep(j, hin, wgt, rough=False):
                for q in range(2 * B):
                    jj, b = q // B, q % B
                    pe.wait_ge(*after("h", nk(j, 8, 2 * q + 1)))
                    for mo in range(DC):
                        for c in range(DC):
                            last = mm(bank(b, 2 * jj + mo), wgt[:, c, mo * P:(mo + 1) * P], hin[:, c, b, jj, 0:T], c == 0, c == DC - 1 and not rough)
                        if rough:
                            last = mm(bank(b, 2 * jj + mo), cn("ident"), ZG[:, mo, b, jj * T:(jj + 1) * T], False, True)
                        last.then_inc(sem("hm"), 1)

            with pe.Fori(0, SWEEPS_BF) as j:
                sweep(j, HB, WGB, rough=True)
            sweep(SWEEPS_BF, HB, WGB, rough=True)
            with pe.Fori(0, SWEEPS_F) as j:
                sweep(j + (SWEEPS_BF + 1), H, w("Wgh", 2))
            sweep(SWEEPS_BF + SWEEPS_F + 1, H, w("Wgh", 2))
            pe.wait_ge(*after("u", 8 * (SWEEPS_F + 1)))
            pe.wait_ge(*after("ld_kv0", 16))
            pe.wait_ge(*after("ld_cx", 16))
            keys_pe(pe, "a0", w("Awk", 2))
            values_pe(pe, "a0", w("Awv", 2))

            def queries(j):
                lin_pe(pe, "q0_mm", j, CQ, lambda b, c: XN[:, c, b, tj(j)], (0, 1))

            queries(0)
            pe.wait_ge(*after("okc", 8))
            mm(ps[0:1, 7, 0:8], cn("ones")[:, 0:1], OKC[:, :]).then_inc(sem("count"), 1)
            pe.wait_ge(*after("flag", 1))
            need = pe.value_load(FLAG[0:1, 0:1], min_val=0, max_val=1)
            with pe.If(need == 1):
                for jj in range(J):
                    with pe.Fori(0, T) as t:
                        pe.wait_ge(*after("xh", t + jj * (T + 1)))
                        for mo in range(DC):
                            for c in range(DC):
                                last = mm(ps[:, 7, mo * B:(mo + 1) * B], feat(w("Wgh", 2), c, mo), H[:, c, :, jj, bass.ds(t, 1)].rearrange("p b s -> p (b s)"), c == 0, c == DC - 1)
                        last.then_inc(sem("xm"), 1)

            pe.wait_ge(*after("decided", 1))
            pe.wait_ge(*after("ld_ffn", 16))
            pe.wait_ge(*after("kv_kb", 4 * (LAYER["a0"] + 1)))
            pe.wait_ge(*after("kv_vs", LAYER["a0"] + 1))

            def half_of_layer0(j):
                pe.wait_ge(*after("x1", j * B))
                attn_pe(pe, "a0", j, 1)
                for b in BS:
                    pe.wait_ge(*after("att_ctx", STEPS["a0"] + nk(j, 8, 6 + b)))
                    for mo in range(DC):
                        for c in range(DC):
                            mm(bank(b, mo), feat(w("Awo", 2), c, mo), ST[b][:, c, :], c == 0, False)
                        for c in range(DC):
                            last = mm(bank(b, mo), feat(w("Wv", 2), c, mo), XN[:, c, b, tj(j)], False, c == DC - 1)
                        last.then_inc(sem("xr_mm"), 1)
                for b in BS:
                    pe.wait_ge(*after("xr", n2(j, b)))
                norm_pe(pe, "r2", j, ST, False)
                for k in range(9):
                    for b in BS:
                        if k < 8:
                            if k == 0:
                                pe.wait_ge(*after("norm_xn", NORMS["r2"] + n2(j, b)))
                            if k >= 2:
                                pe.wait_ge(*after("ff", nk(j, 16, 2 * (k - 2) + b)))
                            for c in range(DC):
                                last = mm(bank(b, k % 2), feat(w("Wf1", 2), c, k), XC[b][:, c, :], c == 0, c == DC - 1)
                            last.then_inc(sem("f1_mm"), 1)
                        if k >= 1:
                            pe.wait_ge(*after("ff", nk(j, 16, 2 * (k - 1) + b)))
                            for mo in range(DC):
                                last = mm(bank(b, 2 + mo), feat(w("Wf2", 8), k - 1, mo), FH[b][k - 1], k == 1, k == 8)
                            if k == 8:
                                last.then_inc(sem("f2_mm"), 1)

            with pe.Fori(0, J - 1) as j:
                half_of_layer0(j)
                queries(j + 1)
            half_of_layer0(J - 1)

            pe.wait_ge(*after("x1", B * J))
            for c in range(DC):
                last = mm(bank(0, 0)[:, 0:B * M], cn("mean"), CX[:, c, :], c == 0, c == DC - 1)
            last.then_inc(sem("cn_mean"), 1)
            pe.wait_ge(*after("cn_sq", 1))
            for c in range(DC):
                last = mm(bank(0, 1)[:, 0:B * M], cn("mean"), ST[0][:, c, 0:B * M], c == 0, c == DC - 1)
            last.then_inc(sem("cn_ms"), 1)
            pe.wait_ge(*after("f6", 1))
            for c in range(DC):
                last = nc.tensor.transpose(ps[:, 2, 8 * c:8 * c + 6], F6C[0:6, c * P:(c + 1) * P], cn("ident", 6)[:, 0:6])
            last.then_inc(sem("s_mm"), 1)
            pe.wait_ge(*after("e6", 1))
            for c in range(DC):
                last = nc.tensor.transpose(ps[:, 3, 8 * c:8 * c + 6], E6[0:6, c * P:(c + 1) * P], cn("ident", 6)[:, 0:6])
            last.then_inc(sem("s_mm"), 1)
            pe.wait_ge(*after("ft6", 2))
            for t, to in ((FT6, 4), (ET6, 5)):
                for c in range(DC):
                    last = mm(ps[0:6, to, 0:6], t[:, c, :], t[:, c, :], c == 0, c == DC - 1)
                last.then_inc(sem("g6_mm"), 1)
            pe.wait_ge(*after("nxs", 1))
            pe.wait_ge(*after("nx", 2))
            pe.wait_ge(*after("ld_w12", 16))
            for b in BS:
                for c in range(DC):
                    last = mm(ps[0:M, 6, 8 * b:8 * b + 4], NX[:, c, b * M:(b + 1) * M], w("fc1T", 2)[:, c, :], c == 0, c == DC - 1)
            last.then_inc(sem("nf_mm"), 1)
            pe.wait_ge(*after("g6", 2))
            pe.wait_ge(*after("nf", 1))
            pe.wait_ge(*after("ft6", 2))
            norm_pe(pe, "l1", 0, SQ1, True, UNITS, bank1)
            for q in UNITS:
                b, span = part_of(q)
                pe.wait_ge(*after("f", DC * (q + 1)))
                for s in range(SUB):
                    for c in range(DC):
                        t = span.start + s * P
                        last = mm(bank1(q, 0)[:, s * M:(s + 1) * M], X[:, c, b, t:t + P], NXS[:, c, b * M:(b + 1) * M], c == 0, c == DC - 1)
                last.then_inc(sem("b1_sc"), 1)
            for q in UNITS:
                pe.wait_ge(*after("b1_pn", q + 1))
                for s in range(SUB):
                    last = nc.tensor.transpose(bank1(q, 1)[0:M, s * P:(s + 1) * P], PR[q % B][q // B][:, s, 0:M], cn("ident"))
                last.then_inc(sem("b1_tr"), 1)
            for q in UNITS:
                pe.wait_ge(*after("b1_pt", q + 1))
                mm(bank1(q, 0)[0:4, :], NF[0:M, q % B, :], PT1[q]).then_inc(sem("h4_mm"), 1)
            for q in UNITS:
                b, span = part_of(q)
                pe.wait_ge(*after("h4", q + 1))
                mm(bank1(q, 1)[0:6, :], G6[0:6, 0:6], U5[0:6, b, span]).then_inc(sem("wu_mm"), 1)
            for q in UNITS:
                pe.wait_ge(*after("wu", q + 1))
                for k in range(SUB):
                    last = mm(bank1(q, 0)[:, k:k + 1], WU1[q][0:6, k * P:(k + 1) * P], cn("ones", 6)[:, 0:1])
                last.then_inc(sem("var_mm"), 1)
            for q in UNITS:
                pe.wait_ge(*after("diag", DIAGS["l1"] + B * J + q + 1))
                spread_pe(bank1(q, 0), RT1[q], rows=6).then_inc(sem("var_r"), 1)
            for q in UNITS:
                pe.wait_ge(*after("u6", q + 1))
                mm(bank1(q, 1)[0:6, :], GS[0:6, 0:6], U6S[q][0:6, :]).then_inc(sem("y_mm"), 1)
                for s in range(SUB):
                    last = nc.tensor.transpose(bank1(q, 0)[:, 8 * s:8 * s + 6], U6S[q][0:6, s * P:(s + 1) * P], cn("ident", 6)[:, 0:6])
                last.then_inc(sem("ut_mm"), 1)
            pe.wait_ge(*after("utok", 8 * J))
            values_pe(pe, "a2", w("Wv2", 2))
            pe.wait_ge(*after("pairs", 16 * 18))
            for t in range(SUB * J):
                if t == 1:
                    pe.wait_ge(*after("kv_vs", LAYER["a2"] + 1))
                for b in BS:
                    if t >= 2:
                        pe.wait_ge(*after("mn", 2 * (t - 2) + b + 1))
                    for half in range(2):
                        last = mm(bank(b, 2 * (t % 2) + half), US[0:ROWS1, b, t * P:(t + 1) * P], YS[0:ROWS1, b, half * T:(half + 1) * T])
                    last.then_inc(sem("p1"), 1)
            for b in BS:
                pe.wait_ge(*after("m_parts", b + 1))
                for t in range(SUB * J):
                    last = nc.tensor.transpose(bank(b, t // 4)[0:3, (t % 4) * P:(t % 4 + 1) * P], MN[:, b, t, 1:4], cn("ident"))
                last.then_inc(sem("mr_mm"), 1)
            pe.wait_ge(*after("ld_w3", 16))
            for mo in range(DC):
                for c in range(DC):
                    last = mm(ps[:, 3, mo:mo + 1], feat(w("Wq3", 2), c, mo), v("cab", c), c == 0, c == DC - 1)
            last.then_inc(sem("q3b_mm"), 1)
            for half in range(2):
                for k in range(SUB * J + 1):
                    for b in BS:
                        n = (half * 8 + k) * 2 + b
                        if k < 8:
                            if k == 0 and half == 0:
                                pe.wait_ge(*after("pairs", 16 * 19))
                            if n >= 4:
                                pe.wait_ge(*after("p2e", n - 4 + 1))
                            mm(bank(b, k % 2), YS[0:ROWS1 + 3, b, k * P:(k + 1) * P], US[0:ROWS1 + 3, b, half * T:(half + 1) * T]).then_inc(sem("p2"), 1)
                        if k >= 1:
                            pe.wait_ge(*after("p2e", n - 2 + 1))
                            if k == 1 and half == 1:
                                pe.wait_ge(*after("o6", b + 1))
                            last = mm(bank(b, 2)[0:6, :], UT[:, b, k - 1, 0:6], PE1[b][(k - 1) % 4], k == 1, k == 8)
                            if k == 8:
                                last.then_inc(sem("o6_mm"), 1)
                for b in BS:
                    pe.wait_ge(*after("o6", 2 * half + b + 1))
                    for k in range(SUB):
                        last = mm(bank(b, 3)[:, k:k + 1], RM[b][0:6, k * P:(k + 1) * P], cn("den", 6)[:, 0:1])
                    last.then_inc(sem("den_mm"), 1)
                for b in BS:
                    pe.wait_ge(*after("diag", DIAGS["den"] + 2 * half + b + 1))
                    spread_pe(bank(b, 3), RTB[b], rows=6).then_inc(sem("den_r"), 1)
                for b in BS:
                    pe.wait_ge(*after("oo", 2 * half + b + 1))
                    for mo in range(DC):
                        if mo == 1:
                            pe.wait_ge(*after("x2", 4 * half + 2 * b + 1))
                        mm(bank(b, 3), EC[0:38, mo * P:(mo + 1) * P], U5[0:38, b, half * T:(half + 1) * T]).then_inc(sem("x2_mm"), 1)

            pe.wait_ge(*after("x2", 4 * B))
            keys_pe(pe, "a2", w("Wk2", 2))

            def queries2(j, batches):
                lin_pe(pe, "q2_mm", j, w("Wq2", 2), lambda b, c: X[:, c, b, tj(j)], (2, 3), None, batches)

            def half_of_layer2(j, meanwhile=None):
                pe.wait_ge(*after("x3", j * 4))
                attn_pe(pe, "a2", j, 2)
                for b in BS:
                    pe.wait_ge(*after("att_ctx", STEPS["a2"] + nk(j, 16, 14 + b)))
                    for mo in range(DC):
                        for c in range(DC):
                            last = mm(bank(b, mo), feat(w("Wo2", 2), c, mo), ST[b][:, c, :], c == 0, c == DC - 1)
                        last.then_inc(sem("o2_mm"), 1)
                for b in BS:
                    pe.wait_ge(*after("o2", nk(j, 4, 2 * b + 1)))
                norm_pe(pe, "x3", j, ST, True, meanwhile=meanwhile)

            queries2(0, BS)
            pe.wait_ge(*after("kv_kb", 4 * (LAYER["a2"] + 1)))
            pe.wait_ge(*after("kv_vs", LAYER["a2"] + 1))
            with pe.Fori(0, J - 1) as j:
                half_of_layer2(j, lambda b: queries2(j + 1, [b]))
            half_of_layer2(J - 1)

            pe.wait_ge(*after("x3", 4 * J))
            pe.wait_ge(*after("w3ready", 1))
            win = w("Win", 2)
            keys_pe(pe, "a3", w("Wk3", 2))
            values_pe(pe, "a3", w("Wv3", 2))
            pe.wait_ge(*after("q3w", 1))
            pe.wait_ge(*after("kv_kb", 4 * (LAYER["a3"] + 1)))
            pe.wait_ge(*after("kv_vs", LAYER["a3"] + 1))
            with pe.Fori(0, J) as j:
                pe.wait_ge(*after("x4", j * B))
                norm_pe(pe, "r3", j, SQ7, False)
                for b in BS:
                    for k in range(XBC):
                        if k == 0:
                            pe.wait_ge(*after("norm_xn", NORMS["r3"] + n2(j, b)))
                        if k >= 4:
                            pe.wait_ge(*after("xbc", nk(j, 12, XBC * b + k - 4)))
                        for c in range(DC):
                            last = mm(bank(b, k % 4), win[:, c, DI + k * P:DI + (k + 1) * P], XN3[b][:, c, :], c == 0, c == DC - 1)
                        last.then_inc(sem("xbc_mm"), 1)
                for b in BS:
                    pe.wait_ge(*after("xbc", nk(j, 12, XBC * b + 2)))
                    for c in range(DC):
                        last = mm(bank(b, 2)[0:8, :], win[:, c, 1280:1288], XN3[b][:, c, :], c == 0, c == DC - 1)
                    last.then_inc(sem("dt_mm"), 1)
                for s in range(SUB):
                    for b in BS:
                        k = 2 * s + b
                        to = (3, 0)[s % 2]
                        if s < 2:
                            pe.wait_ge(*after("xbc", nk(j, 12, XBC * b + 3 + s)))
                        if s >= 2:
                            pe.wait_ge(*after("zs", nk(j, 8, k - 4)))
                        for c in range(DC):
                            last = mm(bank(b, to), XN3[b][:, c, s * P:(s + 1) * P], win[:, c, 0:DI], c == 0, c == DC - 1)
                        last.then_inc(sem("z3_mm"), 1)
                for s in range(SUB):
                    for b in BS:
                        k = 2 * s + b
                        sub = slice(s * P, (s + 1) * P)
                        if s == 0:
                            pe.wait_ge(*after("futb", 1))
                            pe.wait_ge(*after("xs", n2(j, b)))
                            pe.wait_ge(*after("rows7", n2(j, b)))
                            pe.wait_ge(*after("zs", nk(j, 8, 6 + b)))
                        else:
                            pe.wait_ge(*after("y7", nk(j, 8, k - 2)))
                            pe.wait_ge(*after("s7", nk(j, 8, k - 2)))
                        for c in range(4):
                            last = nc.tensor.transpose(bank(b, 0)[:, c * P:(c + 1) * P], CV[b][:, c, sub], cn("ident"))
                        last.then_inc(sem("xtk_mm"), 1)
                        nc.tensor.transpose(bank(b, 1)[:, 0:P], CV[b][:, 4, sub], cn("ident"))
                        nc.tensor.transpose(bank(b, 1)[:, P:P + 96], ROWS[b][0:96, sub], cn("ident", 96)[:, 0:96])
                        mm(bank(b, 1)[:, 256:384], CV[b][:, 4, sub], CV[b][:, 5, sub]).then_inc(sem("bt_mm"), 1)
                        pe.wait_ge(*after("rb", nk(j, 8, k)))
                        for half in range(2):
                            mm(bank(b, 2 + half), LNG[b][0:40, sub], RB[b][0:40, 4 * half:4 * half + 4, :].rearrange("p h n -> p (h n)"), True, False)
                            last = mm(bank(b, 2 + half), IDB, bc(FUTB, 4, 1), False, True)
                        last.then_inc(sem("dmm"), 1)
                        pe.wait_ge(*after("bt", nk(j, 8, k)))
                        mm(bank(b, 1)[:, 384:392], cn("last"), BT[b][:, P + 32:P + 40]).then_inc(sem("een_mm"), 1)
                    for b in BS:
                        k = 2 * s + b
                        sub = slice(s * P, (s + 1) * P)
                        pe.wait_ge(*after("dme", nk(j, 8, k)))
                        if s == 0:
                            pe.wait_ge(*after("m0", 10))
                        else:
                            pe.wait_ge(*after("s7", nk(j, 8, k - 2)))
                        mm(bank(b, 3), CV[b][:, 5, sub], STATE[b]).then_inc(sem("y2_mm"), 1)
                        pe.wait_ge(*after("wx", nk(j, 8, k)))
                        pe.wait_ge(*after("xtk", nk(j, 8, k)))
                        mm(bank(b, 0), BT[b][:, 0:P], WX[b]).then_inc(sem("s_new"), 1)
                    for b in BS:
                        k = 2 * s + b
                        pe.wait_ge(*after("dm", nk(j, 8, k)))
                        pe.wait_ge(*after("dtx", nk(j, 8, k)))
                        for h in range(HM):
                            last = mm(bank(b, 2)[:, h * PD:(h + 1) * PD], DM[b][:, h, :], DTX[b][:, h * PD:(h + 1) * PD])
                        last.then_inc(sem("y1_mm"), 1)
                for b in BS:
                    for s in range(SUB):
                        if s == 0:
                            pe.wait_ge(*after("yn", n2(j, b)))
                            pe.wait_ge(*after("s7", nk(j, 8, 6 + b)))
                        if s >= 2:
                            pe.wait_ge(*after("ut", nk(j, 8, 4 * b + s - 2)))
                        for c in range(4):
                            last = nc.tensor.transpose(bank(b, s % 2)[:, c * P:(c + 1) * P], ZS[b][:, s, :][:, c * P:(c + 1) * P], cn("ident"))
                        last.then_inc(sem("ut7_mm"), 1)
                for b in BS:
                    pe.wait_ge(*after("ut", nk(j, 8, 4 * b + 3)))
                    for mo in range(DC):
                        for c in range(4):
                            last = mm(bank(b, 2 + mo), feat(w("Wout", 4), c, mo), CV[b][:, c, :], c == 0, c == 3)
                        last.then_inc(sem("x4_mm"), 1)

            pe.wait_ge(*after("x4", B * J))
            with pe.Fori(0, J) as j:
                pe.wait_ge(*after("y", j * B))
                norm_pe(pe, "l3", j, ST, True)
                lin_pe(pe, "q3_mm", j, w("Wq3", 2), lambda b, c: XC[b][:, c, :], (2, 3), lambda b: pe.wait_ge(*after("norm_xn", NORMS["l3"] + n2(j, b))))
                for b in BS:
                    pe.wait_ge(*after("att_q", CHUNKS["a3"] + nk(j, 4, 2 * b + 1)))
                attn_pe(pe, "a3", j, 1, True)
                for b in BS:
                    pe.wait_ge(*after("att_ctx", STEPS["a3"] + nk(j, 8, 6 + b)))
                    for mo in range(DC):
                        for c in range(DC):
                            last = mm(bank(b, mo), feat(w("Wo3", 2), c, mo), ST[b][:, c, :], c == 0, c == DC - 1)
                        last.then_inc(sem("y_mm3"), 1)

        @block.scalar
        def _(act):
            act.wait_ge(*after("ld_cn", 16))
            act.wait_ge(*after("ld_vec", 16))
            act.wait_ge(*after("ld_x", 16))
            norm_act(act, "r1", 0, lambda q: X[:, :, part_of(q)[0], part_of(q)[1]], SQR1, "eps6", False, None, UNITS, lambda q, k: ps[:, q, :])
            with act.Fori(0, J) as j:
                act.wait_ge(*after("opg", j * B))
                for b in BS:
                    for mo in range(DC):
                        act.wait_ge(*after("z_mm", nk(j, 4, 2 * b + mo)))
                        nc.scalar.activation(Z[:, mo, b, tj(j)], bank(b, 2 + mo), ACT.Identity, bias=v("bz", mo)).then_inc(sem("z"), 1)
                act.wait_ge(*after("wready", 1))
                for b in BS:
                    act.wait_ge(*after("g_mm", n2(j, b)))
                    nc.scalar.activation(GG[b], bank(b, 1), ACT.Gelu_apprx_tanh, bias=cb("gcb")).then_inc(sem("gg"), 1)
                for b in BS:
                    for k, (dst, bias, to) in enumerate(((GB[b][:, 0], v("bg2", 0), 3), (GB[b][:, 1], v("bg2", 1), 1),
                                                         (SQ[b][:, 0], v("bgc2", 0), 0), (SQ[b][:, 1], v("bgc2", 1), 2))):
                        act.wait_ge(*after("gam_mm", nk(j, 8, 4 * b + k)))
                        nc.scalar.activation(dst, bank(b, to), ACT.Sigmoid, bias=bias).then_inc(sem("gam"), 1)

            def gates(j, rough):
                for q in range(2 * B):
                    jj, b = q // B, q % B
                    for mo in range(DC):
                        if rough:
                            act.wait_ge(*after("hm", nk(j, 8, 2 * q + mo)))
                            act.wait_ge(*after("h", nk(j, 8, 4 + 2 * q + mo)))
                        else:
                            act.wait_ge(*after("u", nk(j - (SWEEPS_BF + 1), 8, 2 * q + mo)))
                        nc.scalar.activation(UG[b][mo], bank(b, 2 * jj + mo) if rough else UG[b][mo], ACT.Sigmoid).then_inc(sem("g"), 1)

            with act.Fori(0, SWEEPS_BF + 1) as j:
                gates(j, True)
            with act.Fori(SWEEPS_BF + 1, SWEEPS_BF + SWEEPS_F + 1) as j:
                gates(j, False)
            n = SWEEPS_BF + SWEEPS_F + 1
            for q in range(2 * B + 1):
                jj, b = q // B, q % B
                for mo in range(DC):
                    if q < 2 * B:
                        act.wait_ge(*after("u", nk(SWEEPS_F, 8, 2 * q + mo)))
                        nc.scalar.activation(UG[b][mo], UG[b][mo], ACT.Sigmoid).then_inc(sem("g"), 1)
                if q >= 1:
                    jj, b = (q - 1) // B, (q - 1) % B
                    for mo in range(DC):
                        act.wait_ge(*after("dd", 2 * (q - 1) + mo + 1))
                        nc.scalar.activation(GZ[b][mo], GZ[b][mo], ACT.Abs).then_inc(sem("ad"), 1)
                        nc.scalar.activation(AA[b][mo], H[:, mo, b, jj, 1:T + 1], ACT.Abs, scale=TOL).then_inc(sem("ad"), 1)
            prep_act(act, "a0")
            act.wait_ge(*after("flag", 1))
            need = act.value_load(FLAG[0:1, 0:1], min_val=0, max_val=1)
            with act.If(need == 1):
                with act.Fori(0, S) as t:
                    act.wait_ge(*after("xu", t + 1))
                    nc.scalar.activation(UX[:, 0], UX[:, 0], ACT.Sigmoid).then_inc(sem("xg"), 1)

            act.wait_ge(*after("decided", 1))
            with act.Fori(0, J) as j:
                act.wait_ge(*after("x1", j * B))
                for b in BS:
                    for mo in range(DC):
                        act.wait_ge(*after("q0_mm", nk(j, 4, 2 * b + mo)))
                        nc.scalar.activation(QS[b][:, mo, :], bank(b, mo), ACT.Identity, bias=cb("CQb", mo)).then_inc(sem("att_q"), 1)
                attn_act(act, "a0", j, 1)
                for b in BS:
                    act.wait_ge(*after("xr", n2(j, b)))
                norm_act(act, "r2", j, lambda b: xs(b, j), ST, "eps6", False)
                for k in range(8):
                    for b in BS:
                        act.wait_ge(*after("f1_mm", nk(j, 16, 2 * k + b)))
                        nc.scalar.activation(FH[b][k], bank(b, k % 2), ACT.Gelu_apprx_tanh, bias=v("bf1", k)).then_inc(sem("ff"), 1)

            act.wait_ge(*after("cn_xc", 1))
            nc.scalar.activation(ST[0][:, :, 0:B * M], XC[0][:, :, 0:B * M], ACT.Square).then_inc(sem("cn_sq"), 1)
            act.wait_ge(*after("cn_ms", 1))
            nc.scalar.activation(RTB[0][:, 0:B * M], bank(0, 1)[:, 0:B * M], ACT.Sqrt, bias=cn("eps5")).then_inc(sem("cn_rt"), 1)
            for t, k in ((FT6, 2), (ET6, 3)):
                act.wait_ge(*after("s_mm", k - 1))
                nc.scalar.activation(t[:, :, :], ps[:, k, 0:16].rearrange("p (c n) -> p c n", c=DC)[:, :, 0:6], ACT.Copy).then_inc(sem("ft6"), 1)
            act.wait_ge(*after("g6_mm", 2))
            nc.scalar.activation(G6[0:6, 0:6], ps[0:6, 4, 0:6], ACT.Copy, scale=1.0 / D).then_inc(sem("g6"), 1)
            nc.scalar.activation(GS[0:6, 0:6], ps[0:6, 5, 0:6], ACT.Copy, scale=D ** -0.5).then_inc(sem("g6"), 1)
            act.wait_ge(*after("nf_mm", 1))
            nc.scalar.activation(NF[0:M, :, :], ps[0:M, 6, 0:16].rearrange("p (b n) -> p b n", b=B)[:, :, 0:4], ACT.Copy).then_inc(sem("nf"), 1)
            norm_act(act, "l1", 0, None, SQ1, "eps5", True, XC1, UNITS, bank1)
            for q in UNITS:
                b, span = part_of(q)
                act.wait_ge(*after("norm_xn", NORMS["l1"] + q + 1))
                for c in range(DC):
                    nc.scalar.activation(X[:, c, b, span], XC1[q][:, c, :], ACT.Identity, bias=v("l1b2", c), scale=v("l1w2", c)).then_inc(sem("f"), 1)
            for q in UNITS:
                act.wait_ge(*after("b1_sh", q + 1))
                pr = PR[q % B][q // B][:, 0:4, 0:M]
                nc.scalar.activation(pr, pr, ACT.Exp).then_inc(sem("b1_ex"), 1)
            for q in UNITS:
                act.wait_ge(*after("b1_tr", q + 1))
                nc.scalar.activation(PT1[q], bank1(q, 1)[0:M, :], ACT.Copy).then_inc(sem("b1_pt"), 1)
            act.wait_ge(*after("us1", 1 + B * J))
            for q in UNITS:
                b, span = part_of(q)
                act.wait_ge(*after("h4_mm", q + 1))
                nc.scalar.activation(U5[0:4, b, span], bank1(q, 0)[0:4, :], ACT.Gelu, bias=v("fc1b")[0:4]).then_inc(sem("h4"), 1)
            for q in UNITS:
                act.wait_ge(*after("var_mm", q + 1))
                nc.scalar.activation(IR[:, q, :], bank1(q, 0)[:, 0:SUB], ACT.Sqrt, bias=cn("eps5")).then_inc(sem("rm"), 1)
            for q in UNITS:
                b, span = part_of(q)
                act.wait_ge(*after("u6", q + 1))
                nc.scalar.activation(UP[0:6, 0, b, span], U6S[q][0:6], ACT.Copy).then_inc(sem("u_parts"), 1)
                act.wait_ge(*after("y_mm", q + 1))
                nc.scalar.activation(YP[0:6, 0, b, span], bank1(q, 1)[0:6, :], ACT.Copy).then_inc(sem("y_parts"), 1)
            for q in UNITS:
                b, span = part_of(q)
                act.wait_ge(*after("ur", q + 1))
                nc.scalar.activation(UP[0:6, 1, b, span], UR[q][0:6, :], ACT.Copy).then_inc(sem("u_parts"), 1)
                act.wait_ge(*after("yr", q + 1))
                nc.scalar.activation(YP[0:6, 1, b, span], YR[q][0:6, :], ACT.Copy).then_inc(sem("y_parts"), 1)
            prep_act(act, "a2")
            for b in BS:
                act.wait_ge(*after("mr_mm", b + 1))
                nc.scalar.activation(MP3[0:3, b, :], ps[0:3, 4 * b:4 * b + 2, :].rearrange("p k n -> p (k n)"), ACT.Copy).then_inc(sem("mrow"), 1)
            nc.scalar.activation(cb("A")[0:8], v("alog")[0:8], ACT.Exp).then_inc(sem("expa"), 1)
            for half in range(2):
                for k in range(SUB * J):
                    for b in BS:
                        n = (half * 8 + k) * 2 + b
                        act.wait_ge(*after("p2", n + 1))
                        nc.scalar.activation(PE1[b][k % 4], bank(b, k % 2), ACT.Exp).then_inc(sem("p2e"), 1)

            with act.Fori(0, J) as j:
                for b in BS:
                    for mo in range(DC):
                        act.wait_ge(*after("q2_mm", nk(j, 4, 2 * b + mo)))
                        nc.scalar.activation(QS[b][:, mo, :], bank(b, 2 + mo), ACT.Identity, bias=v("bq2", mo)).then_inc(sem("att_q"), 1)
                attn_act(act, "a2", j, 2)
                norm_act(act, "x3", j, None, ST, "eps5", True, XC)

            prep_act(act, "a3")
            with act.Fori(0, J) as j:
                act.wait_ge(*after("x4", j * B))
                act.wait_ge(*after("x3", 4 * J))
                norm_act(act, "r3", j, lambda b: xs(b, j), SQ7, "eps5", False)
                for b in BS:
                    act.wait_ge(*after("hx", n2(j, b)))
                    act.wait_ge(*after("norm_xn", NORMS["r3"] + n2(j, b)))
                    for n in range(XBC + 1):
                        if n < XBC:
                            act.wait_ge(*after("xbc_mm", nk(j, 12, XBC * b + n)))
                            nc.scalar.activation(XB[b][:, n, TAPS - 1:], bank(b, n % 4), ACT.Copy).then_inc(sem("xbc"), 1)
                        if n == 0:
                            continue
                        k = n - 1
                        act.wait_ge(*after("xbc", nk(j, 12, XBC * b + k)))
                        nc.scalar.activation(CV[b][:, k, :], XB[b][:, k, 0:T], ACT.Identity, bias=v("convb", k), scale=v("convw", 4 * k)).then_inc(sem("cv0"), 1)
                for b in BS:
                    act.wait_ge(*after("dt1", n2(j, b)))
                    nc.scalar.activation(ET[b][0:8], ET[b][0:8], ACT.Exp, scale=-1.0).then_inc(sem("et"), 1)
                for b in BS:
                    act.wait_ge(*after("et", n2(j, b)))
                    nc.scalar.activation(ET[b][0:8], ET[b][0:8], ACT.Ln, bias=cn("ones", 8)[:, 0:1]).then_inc(sem("l1p"), 1)

                def gate(s):
                    for b in BS:
                        act.wait_ge(*after("z3_mm", nk(j, 8, 2 * s + b)))
                        nc.scalar.activation(ZS[b][:, s, :], bank(b, (3, 0)[s % 2]), ACT.Silu).then_inc(sem("zs"), 1)

                def squares(s, b):
                    act.wait_ge(*after("y7", nk(j, 8, 2 * s + b)))
                    if s >= 2:
                        act.wait_ge(*after("ssq", nk(j, 8, 2 * (s - 2) + b)))
                    nc.scalar.activation(XN3[b][:, s % 2, :], ZS[b][:, s, :], ACT.Square, accum_out=SSQ[:, b, s:s + 1]).then_inc(sem("ssq"), 1)

                for s in range(2):
                    gate(s)
                for b in BS:
                    act.wait_ge(*after("lam", n2(j, b)))
                    act.wait_ge(*after("m0", 10))
                    nc.scalar.activation(ROWS[b][32:40], LAM[b][0:8], ACT.Exp)
                    act.wait_ge(*after("led", n2(j, b)))
                    nc.scalar.activation(ROWS[b][64:72], ROWS[b][64:72], ACT.Exp).then_inc(sem("ew"), 1)
                for s in range(2, SUB):
                    gate(s)
                act.wait_ge(*after("cv", nk(j, 12, XBC - 1)))
                nc.scalar.activation(CV[0][:, :, :], CV[0][:, :, :], ACT.Silu).then_inc(sem("xs"), 1)
                act.wait_ge(*after("cv", nk(j, 12, XBC + 3)))
                nc.scalar.activation(CV[1][:, 0:4, :], CV[1][:, 0:4, :], ACT.Silu)
                act.wait_ge(*after("cv", nk(j, 12, 2 * XBC - 1)))
                nc.scalar.activation(CV[1][:, 4:XBC, :], CV[1][:, 4:XBC, :], ACT.Silu).then_inc(sem("xs"), 1)
                for s in range(SUB):
                    for b in BS:
                        k = 2 * s + b
                        act.wait_ge(*after("xtk_mm", nk(j, 8, k)))
                        act.wait_ge(*after("hist", n2(j, b)))
                        nc.scalar.activation(XTK[b], bank(b, 0), ACT.Copy).then_inc(sem("xtk"), 1)
                        act.wait_ge(*after("bt_mm", nk(j, 8, k)))
                        nc.scalar.activation(BT[b], bank(b, 1)[:, 0:224], ACT.Copy).then_inc(sem("bt"), 1)
                        act.wait_ge(*after("dmm", nk(j, 8, k)))
                        act.wait_ge(*after("cv", nk(j, 12, 11)))
                        nc.scalar.activation(DM[b], ps[:, 4 * b + 2:4 * b + 4, :].rearrange("p k (h n) -> p (k h) n", h=4), ACT.Exp).then_inc(sem("dme"), 1)
                    for b in BS:
                        if s:
                            squares(s - 1, b)
                for b in BS:
                    squares(SUB - 1, b)
                    act.wait_ge(*after("ssq", nk(j, 8, 2 * (SUB - 1) + b)))
                    nc.scalar.activation(SSR[:, b, :], SSQ[:, b, :], ACT.Sqrt, scale=1.0 / DI, bias=cn("eps5")).then_inc(sem("ssr"), 1)
                for b in BS:
                    for s in range(SUB):
                        act.wait_ge(*after("ut7_mm", nk(j, 8, 4 * b + s)))
                        nc.scalar.activation(CV[b][:, 0:4, s * P:(s + 1) * P], bank(b, s % 2).rearrange("p (c n) -> p c n", c=4), ACT.Copy).then_inc(sem("ut"), 1)
            with act.Fori(0, J) as j:
                act.wait_ge(*after("x4", B * J))
                act.wait_ge(*after("y", j * B))
                norm_act(act, "l3", j, None, ST, "eps5", True, XC)
                for b in BS:
                    for mo in range(DC):
                        act.wait_ge(*after("q3_mm", nk(j, 4, 2 * b + mo)))
                        nc.scalar.activation(QS[b][:, mo, :], bank(b, 2 + mo), ACT.Identity, bias=cb("q3b", mo)).then_inc(sem("att_q"), 1)
                attn_act(act, "a3", j, 1)

        @block.vector
        def _(dve):
            begin(dve, "vector")
            ch = Chain(dve, "dve_step")
            dve.wait_ge(*after("ld_vec", 16))
            dve.wait_ge(*after("ld_x", 16))
            dve.wait_ge(*after("ld_cn", 16))
            norm_dve(dve, ch, "r1", 0, lambda q: X[:, :, part_of(q)[0], part_of(q)[1]], RTR1, lambda q: XN[:, :, part_of(q)[0], part_of(q)[1]], False, None, SQR1,
                     UNITS, lambda q, k: ps[:, q, :])
            dve.wait_ge(*after("ld_w0", 16))
            TT, TS, STT = nc.vector.tensor_tensor, nc.vector.tensor_scalar, nc.vector.scalar_tensor_tensor
            TT(cb("zgb"), v("bgz", 0), v("bgh", 0), ALU.add)
            TT(cb("zgb", 1), v("bgz", 1), v("bgh", 1), ALU.add)
            for k in range(2):
                STT(out=cb("xob", k), in0=v("bv", k), scalar=0.1, in1=v("abo", k), op0=ALU.mult, op1=ALU.add)
                TS(w("Wz", 2)[:, k, :], w("Wz", 2)[:, k, :], v("n1", k), None, ALU.mult)
                TS(w("Wv", 2)[:, k, :], w("Wv", 2)[:, k, :], v("n1", k), 0.1, ALU.mult, ALU.mult)
                nc.vector.tensor_copy(WGB[:, k, :], w("Wgh", 2)[:, k, :])
            dve.wait_ge(*after("pw", 5))
            for k in range(2):
                TS(CQ[:, k, :], ps[:, 4, k * D:(k + 1) * D], v("n1", k), None, ALU.mult)
                TS(CG[:, k, 0:P], ps[:, 5, k * P:(k + 1) * P], v("n1", k), None, ALU.mult)
            TT(CB[:, 0:2], ps[:, 6, 0:2], VC[:, vcol["abq"][0]:vcol["abq"][1]], ALU.add)
            ch.link(TT(cb("gcb"), ps[:, 7, 0:1], v("bg1c"), ALU.add))
            dve.sem_inc(sem("wready"), 1)
            with dve.Fori(0, J) as j:
                ch.enter(j)
                for b in BS:
                    for mo in range(DC):
                        dve.wait_ge(*after("zg_mm", nk(j, 4, 2 * b + mo)))
                        TS(ZG[:, mo, b, tj(j)], bank(b, 2 * mo), cb("zgb", mo), None, ALU.add).then_inc(sem("zg"), 1)
                for b in BS:
                    dve.wait_ge(*after("gam", nk(j, 8, 4 * b + 3)))
                    ch.link(TT(GB[b], GB[b], SQ[b], ALU.mult))
                    ch.link(TS(GB[b], GB[b], 1e-6, 1.0 - 1e-6, ALU.max, ALU.min))
                    TS(OPG[:, :, b, tj(j)], GB[b], 1.0, None, ALU.add).then_inc(sem("opg"), 1)
                ch.turn()
            ch.leave(J)

            dve.wait_ge(*after("opg", B * J))
            nc.vector.memset(HB[:, :, :, :, :].rearrange("p c b j s -> p (c b j s)"), 0.0)
            ch.link(nc.vector.memset(H[:, :, :, :, :].rearrange("p c b j s -> p (c b j s)"), 0.0))
            dve.sem_inc(sem("h"), 8)

            def sweep(j, dst, checking=False, rough=False):
                for q in range(2 * B + 1):
                    jj, b = q // B, q % B
                    if q < 2 * B and not rough:
                        for mo in range(DC):
                            dve.wait_ge(*after("hm", nk(j, 8, 2 * q + mo)))
                            TT(UG[b][mo], bank(b, 2 * jj + mo), ZG[:, mo, b, jj * T:(jj + 1) * T], ALU.add).then_inc(sem("u"), 1)
                    if q >= 1:
                        jj, b = (q - 1) // B, (q - 1) % B
                        span = slice(1, T + 1)
                        if rough:
                            dve.wait_ge(*after("hm", nk(j, 8, 2 * q - 1)))
                        if jj == 1 and not checking:
                            nc.vector.tensor_copy(dst[:, :, b, 1, 0:1], dst[:, :, b, 0, T:T + 1])
                        for mo in range(DC):
                            k = 2 * (q - 1) + mo
                            dve.wait_ge(*after("g", nk(j, 8, k)))
                            if rough or checking or not pool_takes(q - 1, mo):
                                ch.link(TT(AA[b][mo], OPG[:, mo, b, jj * T:(jj + 1) * T], UG[b][mo], ALU.subtract))
                            dve.wait_ge(*after("gz", nk(j, 8, k)))
                            first = dst[:, mo, b, 0, T * jj:T * jj + 1]
                            scan = nc.vector.tensor_tensor_scan(UG[b][mo] if checking else dst[:, mo, b, jj, span], AA[b][mo], GZ[b][mo],
                                                                first, ALU.mult, ALU.add)
                            if not checking:
                                scan.then_inc(sem("h"), 1)
                                continue
                            ch.link(scan)
                            TT(GZ[b][mo], UG[b][mo], H[:, mo, b, jj, span], ALU.subtract).then_inc(sem("dd"), 1)
                        if checking:
                            for mo in range(DC):
                                k = 2 * (q - 1) + mo
                                dve.wait_ge(*after("ad", 2 * k + 2))
                                STT(out=UG[b][mo], in0=GZ[b][mo], scalar=-TOL, in1=AA[b][mo], op0=ALU.add, op1=ALU.is_le,
                                    accum_out=OKC[:, k:k + 1]).then_inc(sem("okc"), 1)
                                dve.wait_ge(*after("okc", k + 1))

            with dve.Fori(0, SWEEPS_BF) as j:
                ch.enter(j)
                sweep(j, HB, rough=True)
                ch.turn()
            ch.leave(SWEEPS_BF)
            sweep(SWEEPS_BF, H, rough=True)
            with dve.Fori(0, SWEEPS_F) as j:
                ch.enter(j)
                sweep(j + (SWEEPS_BF + 1), H)
                ch.turn()
            ch.leave(SWEEPS_F)
            sweep(SWEEPS_BF + SWEEPS_F + 1, H, checking=True)
            prep_dve(dve, ch, "a0", "abk0", 4)
            dve.wait_ge(*after("count", 1))
            ch.link(nc.vector.tensor_reduce(TOT[:, 0:1], ps[0:1, 7, 0:8], AX.X, ALU.add))
            nc.vector.tensor_scalar(FLAG[:, 0:1], TOT[:, 0:1], float(D * B * S) - 0.5, None, FALLBACK_TEST).then_inc(sem("flag"), 1)
            dve.wait_ge(*after("flag", 1))
            need = dve.value_load(FLAG[0:1, 0:1], min_val=0, max_val=1)
            with dve.If(need == 1):
                cx = Chain(dve, "exact_step")
                for jj in range(J):
                    if jj:
                        nc.vector.tensor_copy(H[:, :, :, jj, 0:1], H[:, :, :, jj - 1, T:T + 1]).then_inc(sem("xh"), 1)
                        dve.wait_ge(*after("xh", jj * (T + 1)))
                    with dve.Fori(0, T) as t:
                        cx.enter(t)
                        at, now = bass.ds(t, 1), bass.ds(t + jj * T, 1)
                        dve.wait_ge(*after("xm", t + (jj * T + 1)))
                        TT(UX[:, 0], ps[:, 7, 0:2 * B].rearrange("p (c b) -> p c b", c=DC), ZG[:, :, :, now].rearrange("p c b s -> p c (b s)"), ALU.add).then_inc(sem("xu"), 1)
                        dve.wait_ge(*after("xg", t + (jj * T + 1)))
                        TT(UX[:, 1], UX[:, 0], Z[:, :, :, now].rearrange("p c b s -> p c (b s)"), ALU.mult)
                        cx.link(TT(UX[:, 2], OPG[:, :, :, now].rearrange("p c b s -> p c (b s)"), UX[:, 0], ALU.subtract))
                        cx.link(TT(UX[:, 3], UX[:, 2], H[:, :, :, jj, at].rearrange("p c b s -> p c (b s)"), ALU.mult))
                        TT(H[:, :, :, jj, bass.ds(t + 1, 1)].rearrange("p c b s -> p c (b s)"), UX[:, 3], UX[:, 1], ALU.add).then_inc(sem("xh"), 1)
                        cx.turn()
                    cx.leave(T)
                    dve.wait_ge(*after("xh", jj * (T + 1) + T))
            dve.sem_inc(sem("decided"), 1)

            dve.wait_ge(*after("wf1", 2))
            dve.wait_ge(*after("pr0", 4))
            with dve.Fori(0, J) as j:
                ch.enter(j)
                attn_dve(dve, ch, "a0", j, 1, "abv0")
                for b in BS:
                    for mo in range(DC):
                        xd = X[:, mo, b, tj(j)]
                        dve.wait_ge(*after("xr_mm", nk(j, 4, 2 * b + mo)))
                        ch.link(STT(out=xd, in0=bank(b, mo), scalar=cb("xob", mo), in1=xd, op0=ALU.add, op1=ALU.add))
                        ins = TT(xd, xd, H[:, mo, b, bass.ds(j, 1), 1:T + 1].rearrange("p a n -> p (a n)"), ALU.add)
                    ins.then_inc(sem("xr"), 1)
                for b in BS:
                    dve.wait_ge(*after("xr", n2(j, b)))
                norm_dve(dve, ch, "r2", j, lambda b: xs(b, j), RTB, lambda b: XC[b], False, None, ST)
                for b in BS:
                    dve.wait_ge(*after("f2_mm", n2(j, b)))
                    for mo in range(DC):
                        xd = X[:, mo, b, tj(j)]
                        ins = STT(out=xd, in0=bank(b, 2 + mo), scalar=v("bf2", mo), in1=xd, op0=ALU.add, op1=ALU.add)
                    ins.then_inc(sem("x1"), 1)
                ch.turn()
            ch.leave(J)

            dve.wait_ge(*after("x1", B * J))
            dve.wait_ge(*after("ld_r6", 16))
            xc0 = XC[0][:, :, 0:B * M]
            dve.wait_ge(*after("cn_mean", 1))
            TT(xc0, CX[:, :, :], bc(bank(0, 0)[:, 0:B * M], DC, 1), ALU.subtract).then_inc(sem("cn_xc"), 1)
            dve.wait_ge(*after("cn_rt", 1))
            ch.link(nc.vector.reciprocal(RTB[0][:, 0:B * M], RTB[0][:, 0:B * M]))
            ch.link(TT(xc0, xc0, bc(RTB[0][:, 0:B * M], DC, 1), ALU.mult))
            for c in range(DC):
                TS(NX[:, c, :], XC[0][:, c, 0:B * M], v("l1w1", c), v("l1b1", c), ALU.mult, ALU.add).then_inc(sem("nx"), 1)
            dve.wait_ge(*after("nx", 2))
            TS(NXS[:, :, :], NX[:, :, :], D ** -0.5, None, ALU.mult).then_inc(sem("nxs"), 1)
            ch.link(nc.vector.tensor_reduce(TOT6[:, 0:1], R6[:, 0, :], AX.X, ALU.add))
            ch.link(TS(TOT6[:, 1:2], TOT6[:, 0:1], 1.0 / D, None, ALU.mult))
            TS(F6C[0:6], R6[:, 0, :], TOT6[:, 1:2], None, ALU.subtract).then_inc(sem("f6"), 1)
            dve.wait_ge(*after("f6", 1))
            ch.link(TT(E6[0:6], F6C[0:6], R6[:, 1, :], ALU.mult))
            TT(E6[0:6], E6[0:6], R6[:, 2, :], ALU.add).then_inc(sem("e6"), 1)
            dve.wait_ge(*after("e6", 1))
            ch.link(nc.vector.memset(EC[0:32], 0.0))
            ch.link(TT(E1[0:6], E6[0:6], R6[:, 3, :], ALU.mult))
            TT(EC[32:38], E1[0:6], R6[:, 4, :], ALU.mult)
            ch.link(TT(EC[0:6], R6[:, 0, :], R6[:, 4, :], ALU.mult))
            norm_dve(dve, ch, "l1", 0, lambda q: X[:, :, part_of(q)[0], part_of(q)[1]], RT1, lambda q: XC1[q], True, XC1, SQ1, UNITS, bank1)
            for q in UNITS:
                dve.wait_ge(*after("b1_sc", q + 1))
                b, k = q % B, q // B
                sc = bank1(q, 0)[:, 0:HALF].rearrange("p (h m) -> p h m", h=4)
                ch.link(nc.vector.tensor_reduce(MX[:, b, k, 0:4], sc, AX.X, ALU.max, negate=True))
                TT(PR[b][k][:, 0:4, 0:M], sc, bc(MX[:, b, k, 0:4], M, 2), ALU.add).then_inc(sem("b1_sh"), 1)
            for q in UNITS:
                dve.wait_ge(*after("b1_ex", q + 1))
                b, k = q % B, q // B
                ch.link(nc.vector.tensor_reduce(RS[:, b, k, 0:4], PR[b][k][:, 0:4, 0:M], AX.X, ALU.add))
                nc.vector.reciprocal(RS[:, b, k, 0:4], RS[:, b, k, 0:4]).then_inc(sem("b1_ri"), 1)
            for q in UNITS:
                b, span = part_of(q)
                dve.wait_ge(*after("wu_mm", q + 1))
                TT(WU1[q][0:6, :], bank1(q, 1)[0:6, :], U5[0:6, b, span], ALU.mult).then_inc(sem("wu"), 1)
            for q in UNITS:
                dve.wait_ge(*after("rm", q + 1))
                ch.link(nc.vector.reciprocal(IR[:, q, :], IR[:, q, :]))
                diagonal(RT1[q], IR[:, q, :])
            dve.wait_ge(*after("us1", 1 + B * J))
            for q in UNITS:
                b, span = part_of(q)
                dve.wait_ge(*after("var_r", q + 1))
                TT(U6S[q][0:5, :], U5[0:5, b, span], bank1(q, 0)[0:5, :], ALU.mult).then_inc(sem("u6"), 1)
            for q in UNITS:
                b, span = part_of(q)
                dve.wait_ge(*after("u_parts", q + 1))
                TT(UR[q][0:6, :], U6S[q][0:6], UP[0:6, 0, b, span], ALU.subtract).then_inc(sem("ur"), 1)
                dve.wait_ge(*after("y_parts", q + 1))
                TT(YR[q][0:6, :], bank1(q, 1)[0:6, :], YP[0:6, 0, b, span], ALU.subtract).then_inc(sem("yr"), 1)
            for q in UNITS:
                b, span = part_of(q)
                dve.wait_ge(*after("u_parts", B * J + q + 1))
                TT(UP[0:6, 2, b, span], UR[q][0:6, :], UP[0:6, 1, b, span], ALU.subtract).then_inc(sem("u_low"), 1)
                dve.wait_ge(*after("y_parts", B * J + q + 1))
                TT(YP[0:6, 2, b, span], YR[q][0:6, :], YP[0:6, 1, b, span], ALU.subtract).then_inc(sem("y_low"), 1)
            for q in UNITS:
                dve.wait_ge(*after("ut_mm", q + 1))
                for s in range(SUB):
                    nc.vector.tensor_copy(UT[:, q % B, q // B * SUB + s, 0:6], bank1(q, 0)[:, 8 * s:8 * s + 6]).then_inc(sem("utok"), 1)
            for t in range(SUB * J):
                for b in BS:
                    k = 2 * (t % 2)
                    dve.wait_ge(*after("p1", 2 * t + b + 1))
                    nc.vector.tensor_reduce(MN[:, b, t, 0:1], ps[:, 4 * b + k:4 * b + k + 2, :].rearrange("p k n -> p (k n)"), AX.X, ALU.max, negate=True).then_inc(sem("mn"), 1)
            for b in BS:
                dve.wait_ge(*after("mn", 2 * (SUB * J - 1) + b + 1))
                ch.link(nc.vector.tensor_copy(MB[:, b, :, 0], MN[:, b, :, 0]))
                ch.link(nc.vector.tensor_copy(MN[:, b, :, 1], MB[:, b, :, 0]))
                ch.link(TT(MR[:, b, :], MN[:, b, :, 0], MN[:, b, :, 1], ALU.subtract))
                ch.link(nc.vector.tensor_copy(MB[:, b, :, 1], MR[:, b, :]))
                ch.link(nc.vector.tensor_copy(MN[:, b, :, 2], MB[:, b, :, 1]))
                TT(MN[:, b, :, 3], MR[:, b, :], MN[:, b, :, 2], ALU.subtract).then_inc(sem("m_parts"), 1)
            dve.wait_ge(*after("ld_w3", 16))
            dve.wait_ge(*after("ld_mask", 16))
            ch.link(nc.vector.tensor_copy(KEEP[:, :], MKU[:, :].bitcast(U8)[:, 0:M]))
            TS(NEG3[:, :].rearrange("p (h m) -> p h m", h=4), bc(KEEP[0:3, :], 4, 1), cn("neg", 3), None, ALU.mult)
            ch.link(nc.vector.tensor_copy(ONESB[:, :], cn("ones", 3)))
            TS(KEEP[:, :], KEEP[:, :], -1.0, 1.0, ALU.mult, ALU.add)
            for c in range(DC):
                ins = TS(w("Win", 2)[:, c, :], w("Win", 2)[:, c, :], v("mnw", c), None, ALU.mult)
            ch.link(ins)
            dve.sem_inc(sem("w3ready"), 1)
            for c in range(4):
                TS(w("Wout", 4)[:, c, :], w("Wout", 4)[:, c, :], v("gnw", c), None, ALU.mult)
            dve.wait_ge(*after("q3b_mm", 1))
            for c in range(DC):
                TS(w("Wq3", 2)[:, c, :], w("Wq3", 2)[:, c, :], v("caw", c), None, ALU.mult)
            ch.link(nc.vector.tensor_copy(CB[:, 7:9], ps[:, 3, 0:2]))
            dve.sem_inc(sem("q3w"), 1)
            ET_A = cb("A")[0:8]
            dve.wait_ge(*after("expa", 1))
            ch.link(TS(ET_A, ET_A, -1.0, None, ALU.mult))
            for half in range(2):
                for b in BS:
                    dve.wait_ge(*after("o6_mm", 2 * half + b + 1))
                    nc.vector.tensor_copy(RM[b][0:6, :], bank(b, 2)[0:6, :]).then_inc(sem("o6"), 1)
                for b in BS:
                    dve.wait_ge(*after("den_mm", 2 * half + b + 1))
                    ch.link(nc.vector.reciprocal(IR[:, b, :], bank(b, 3)[:, 0:SUB]))
                    diagonal(RTB[b], IR[:, b, :])
                for b in BS:
                    dve.wait_ge(*after("den_r", 2 * half + b + 1))
                    TT(U5[32:38, b, half * T:(half + 1) * T], bank(b, 3)[0:6, :], RM[b][0:6, :], ALU.mult).then_inc(sem("oo"), 1)
                for b in BS:
                    for mo in range(DC):
                        xd = X[:, mo, b, half * T:(half + 1) * T]
                        dve.wait_ge(*after("x2_mm", 4 * half + 2 * b + mo + 1))
                        TT(xd, bank(b, 3), xd, ALU.add).then_inc(sem("x2"), 1)

            dve.wait_ge(*after("x2", 4 * B))
            prep_dve(dve, ch, "a2", "bk2", 8)
            with dve.Fori(0, J) as j:
                ch.enter(j)
                attn_dve(dve, ch, "a2", j, 2, "bv2")
                for b in BS:
                    for mo in range(DC):
                        xd = X[:, mo, b, tj(j)]
                        dve.wait_ge(*after("o2_mm", nk(j, 4, 2 * b + mo)))
                        TT(xd, bank(b, mo), xd, ALU.add).then_inc(sem("o2"), 1)
                dve.wait_ge(*after("o2", nk(j, 4, 3)))
                norm_dve(dve, ch, "x3", j, lambda b: xs(b, j), RTB, lambda b: XC[b], True, XC, ST)
                for b in BS:
                    dve.wait_ge(*after("norm_xn", NORMS["x3"] + n2(j, b)))
                    for c in range(DC):
                        TS(X[:, c, b, tj(j)], XC[b][:, c, :], v("lg2", c), v("lb2", c), ALU.mult, ALU.add).then_inc(sem("x3"), 1)
                ch.turn()
            ch.leave(J)

            dve.wait_ge(*after("x3", 4 * J))
            prep_dve(dve, ch, "a3", None, 4, masked=True)
            dve.wait_ge(*after("m0", B))
            TS(IDB, cn("ident"), 1.0, None, ALU.mult)
            ch.link(TS(FUTB, cn("future"), 1.0, None, ALU.mult))
            dve.sem_inc(sem("futb"), 1)
            reset = RC[:, HM * P:HM * P + T]
            with dve.Fori(0, J) as j:
                ch.enter(j)
                dve.wait_ge(*after("x4", j * B))
                for b in BS:
                    nc.vector.tensor_copy(XB[b][:, :, 0:TAPS - 1], HIST[b]).then_inc(sem("hx"), 1)
                norm_dve(dve, ch, "r3", j, lambda b: xs(b, j), RT7, lambda b: XN3[b], False, None, SQ7)
                def conv(b, ks):
                    for first in ks[::2]:
                        dve.wait_ge(*after("cv0", nk(j, 12, XBC * b + first + 1)))
                        for tap in range(1, TAPS):
                            for k in (first, first + 1):
                                ins = STT(out=CV[b][:, k, :], in0=XB[b][:, k, tap:tap + T], scalar=v("convw", 4 * k + tap), in1=CV[b][:, k, :],
                                          op0=ALU.mult, op1=ALU.add)
                                if tap == TAPS - 1:
                                    ins.then_inc(sem("cv"), 1)
                            if tap < TAPS - 1:
                                ch.link(ins)

                conv(0, range(XBC))
                for b in BS:
                    dve.wait_ge(*after("dt_mm", n2(j, b)))
                    ch.link(TS(LAM[b][0:8], bank(b, 2)[0:8, :], v("dtb")[0:8], None, ALU.add))
                    STT(out=ET[b][0:8], in0=LAM[b][0:8], scalar=-1.0, in1=LAM[b][0:8], op0=ALU.mult, op1=ALU.max).then_inc(sem("dt1"), 1)
                conv(1, range(2))
                dve.wait_ge(*after("m0", 5 * B))
                dve.wait_ge(*after("m1", 2 * B))
                for b in BS:
                    dve.wait_ge(*after("l1p", n2(j, b)))
                    ch.link(STT(out=ROWS[b][0:8], in0=LAM[b][0:8], scalar=0.0, in1=ET[b][0:8], op0=ALU.max, op1=ALU.add))
                    ch.link(TS(LAM[b][0:8], ROWS[b][0:8], ET_A, None, ALU.mult))
                    ch.link(nc.vector.tensor_tensor_scan(LAM[b][0:8], reset, LAM[b][0:8], 0.0, ALU.mult, ALU.add))
                    TS(LNG[b][0:8], LAM[b][0:8], -1.0, None, ALU.mult).then_inc(sem("lam"), 1)
                    lam = LAM[b][0:8].rearrange("p (s n) -> p s n", s=SUB)
                    TT(ROWS[b][64:72].rearrange("p (s n) -> p s n", s=SUB), lam[:, :, P - 1:P].broadcast_to([8, SUB, P]), lam, ALU.subtract).then_inc(sem("led"), 1)
                conv(1, range(2, 4))
                for b in BS:
                    dve.wait_ge(*after("ew", n2(j, b)))
                    ch.link(nc.vector.tensor_copy(ET[b][64:72], ROWS[b][0:8]))
                    TT(ROWS[b][64:72], ROWS[b][64:72], ET[b][64:72], ALU.mult).then_inc(sem("rows7"), 1)
                conv(1, range(4, XBC))
                for b in BS:
                    dve.wait_ge(*after("hx", n2(j, b)))
                    nc.vector.tensor_copy(HIST[b], XB[b][:, :, T:T + TAPS - 1]).then_inc(sem("hist"), 1)
                h3 = lambda a: a.rearrange("p (h n) -> p h n", h=HM)
                for s in range(SUB):
                    for b in BS:
                        k = 2 * s + b
                        dve.wait_ge(*after("xtk", nk(j, 8, k)))
                        dve.wait_ge(*after("bt", nk(j, 8, k)))
                        TT(h3(DTX[b]), h3(XTK[b]), bc(BT[b][:, P:P + 8], PD, 2), ALU.mult).then_inc(sem("dtx"), 1)
                        dve.wait_ge(*after("een_mm", nk(j, 8, k)))
                        nc.vector.tensor_copy(EEN[:, b, :], bank(b, 1)[:, 384:392]).then_inc(sem("een"), 1)
                    for b in BS:
                        k = 2 * s + b
                        dve.wait_ge(*after("dme", nk(j, 8, k)))
                        TT(DM[b], DM[b], bc(bank(b, 1)[:, 256:384], HM, 1), ALU.mult).then_inc(sem("dm"), 1)
                        dve.wait_ge(*after("een", nk(j, 8, k)))
                        TT(h3(SE[b]), h3(STATE[b]), bc(EEN[:, b, :], PD, 2), ALU.mult)
                        dve.wait_ge(*after("y2_mm", nk(j, 8, k)))
                        ch.link(TT(h3(YT[b]), h3(bank(b, 3)), bc(BT[b][:, P + 32:P + 40], PD, 2), ALU.mult))
                        dve.wait_ge(*after("dx", nk(j, 8, k)))
                        TT(YT[b], YT[b], XTK[b], ALU.add).then_inc(sem("yt"), 1)
                        dve.wait_ge(*after("s_new", nk(j, 8, k)))
                        TT(STATE[b], SE[b], bank(b, 0), ALU.add).then_inc(sem("s7"), 1)
                    for b in BS:
                        k = 2 * s + b
                        dve.wait_ge(*after("y1_mm", nk(j, 8, k)))
                        dve.wait_ge(*after("yt", nk(j, 8, k)))
                        ch.link(TT(YT[b], YT[b], bank(b, 2), ALU.add))
                        TT(ZS[b][:, s, :], ZS[b][:, s, :], YT[b], ALU.mult).then_inc(sem("y7"), 1)
                for b in BS:
                    dve.wait_ge(*after("ssr", n2(j, b)))
                    ch.link(nc.vector.reciprocal(SSR[:, b, :], SSR[:, b, :]))
                    ins = TT(ZS[b][:, :, :], ZS[b][:, :, :], bc(SSR[:, b, :], DI, 2), ALU.mult)
                    ins.then_inc(sem("yn"), 1)
                for b in BS:
                    for mo in range(DC):
                        xd = X[:, mo, b, tj(j)]
                        dve.wait_ge(*after("x4_mm", nk(j, 4, 2 * b + mo)))
                        ins = TT(xd, bank(b, 2 + mo), xd, ALU.add)
                    ins.then_inc(sem("x4"), 1)
                ch.turn()
            ch.leave(J)
            dve.wait_ge(*after("pr0", 8))
            dve.wait_ge(*after("x4", B * J))
            with dve.Fori(0, J) as j:
                ch.enter(j)
                norm_dve(dve, ch, "l3", j, lambda b: xs(b, j), RTB, lambda b: XC[b], True, XC, ST)
                attn_dve(dve, ch, "a3", j, 1, None)
                for b in BS:
                    for mo in range(DC):
                        xd = X[:, mo, b, tj(j)]
                        dve.wait_ge(*after("y_mm3", nk(j, 4, 2 * b + mo)))
                        ins = TT(xd, bank(b, mo), xd, ALU.add)
                    ins.then_inc(sem("y"), 1)
                ch.turn()
            ch.leave(J)


def pack_cols(a, n):
    out = np.zeros((n * P,), np.float32)
    a = np.asarray(a).reshape(-1)
    out[:a.size] = a
    return out.reshape(n, P).T


def kernel(**inputs):
    import concourse.bacc as bacc
    from concourse.bass_utils import run_bass_kernel_spmd

    i = {k: np.asarray(a) for k, a in inputs.items()}
    g0, g1, g2, g3 = (lambda n, k=k: i[f"L{k}_xattn_{n}"] for k in range(4))
    vcol, nvec, mats, sizes = layout()
    f = np.float32

    def chunks(a):
        k, n = a.shape
        return a.reshape(k // P, P, n).transpose(1, 0, 2).reshape(P, -1)

    vecs = np.zeros((P, nvec), f)

    def put(name, a, n):
        vecs[:, vcol[name][0]:vcol[name][1]] = pack_cols(a, n)

    for name, a in (("n1", g0("norm1_scale")), ("n2", g0("norm2_scale")), ("bq", g0("bq")), ("abq", g0("abq")),
                    ("bk", g0("bk")), ("bz", g0("bz")), ("bv", g0("bv")), ("abo", g0("abo")), ("bgz", g0("bgz")),
                    ("bgh", g0("bgh")), ("bg2", g0("bg2")), ("bgc2", g0("bgc2")), ("abk0", g0("abk")),
                    ("abv0", g0("abv")), ("bf2", g0("bf2")), ("l1w1", g1("norm1_w")), ("l1b1", g1("norm1_b")),
                    ("l1w2", g1("norm2_w")), ("l1b2", g1("norm2_b")), ("bq2", g2("bq")), ("bk2", g2("bk")),
                    ("bv2", g2("bv")), ("lg2", g2("ln_gamma")), ("lb2", g2("ln_beta")), ("mnw", g3("m_norm_w")),
                    ("caw", g3("ca_ln_w")), ("cab", g3("ca_ln_b"))):
        put(name, a, 2)
    put("bg1c", np.concatenate([g0("bg1"), g0("bgc1")]), 1)
    put("bf1", g0("bf1"), 8)
    put("fc1b", g1("fc1_b"), 1)
    put("convb", g3("conv_b"), XBC)
    vecs[:, vcol["convw"][0]:vcol["convw"][1]] = g3("conv_w").reshape(XBC, P, TAPS).transpose(1, 0, 2).reshape(P, -1)
    put("dtb", g3("dt_bias"), 1)
    put("alog", g3("A_log"), 1)
    vecs[:, vcol["dskip"][0]:vcol["dskip"][1]] = g3("D_skip")[None, :]
    put("gnw", g3("gnorm_w"), 4)

    packs = [np.zeros((P, n), f) for n in sizes]

    def putm(name, a):
        which, lo, hi = mats[name]
        packs[which][:, lo:hi] = a

    for name, a in (("Awk", g0("Awk")), ("Awv", g0("Awv")), ("WqT", g0("Wq").T), ("Awq", g0("Awq")), ("WkT", g0("Wk").T),
                    ("Wgc1", g0("Wgc1")), ("WzT", g0("Wz").T), ("Wg1", g0("Wg1")), ("Wz", g0("Wz")), ("Wgz", g0("Wgz")),
                    ("Wgh", g0("Wgh")), ("Wv", g0("Wv")), ("Awo", g0("Awo")), ("Wf1", g0("Wf1")), ("Wf2", g0("Wf2")),
                    ("Win", g3("in_proj_w")), ("Wout", g3("out_proj_w")), ("Wq3", g3("Wq")), ("Wk3", g3("Wk")),
                    ("Wv3", g3("Wv")), ("Wo3", g3("Wo")), ("Wq2", g2("Wq")), ("Wk2", g2("Wk")), ("Wv2", g2("Wv")),
                    ("Wo2", g2("Wo")), ("fc1T", g1("fc1_w").T)):
        putm(name, chunks(a))
    putm("Wg2c", np.concatenate([g0("Wg2"), g0("Wgc2")], 0))
    rows6 = np.zeros((6, 5, D), f)
    rows6[0:4, 0] = g1("fc2_w").T
    rows6[4, 0] = g1("fc2_b")
    rows6[0:5, 1] = g1("norm3_w")
    rows6[5, 2] = g1("norm3_b")
    rows6[:, 3] = g1("gamma1")
    rows6[:, 4] = g1("gamma2")
    cst, rowc = constants()
    mask = np.zeros((1, 4 * -(-M // 4)), np.uint8)
    mask[:, 0:M] = i["mask_1xS2_bf0"].view(np.uint8)
    xT = i["x"].transpose(2, 0, 1).reshape(DC, P, B, S).transpose(1, 0, 2, 3).reshape(P, -1)
    cT = i["ctx_1024"].transpose(2, 0, 1).reshape(DC, P, B * M).transpose(1, 0, 2).reshape(P, -1)
    arrays = {"xT": xT, "ctxT": cT, "mask": mask.view(np.int32), "vecs": vecs, "m0": packs[0], "m1": packs[1],
              "m2": packs[2], "rows6": rows6.reshape(6, -1), "consts": cst, "rowconsts": rowc}
    arrays = {k: np.ascontiguousarray(a) for k, a in arrays.items()}
    nc = bacc.Bacc("TRN2", target_bir_lowering=False, num_devices=1)
    args = [nc.dram_tensor(f"in_{k}", a.shape, mybir.dt.from_np(a.dtype), kind="ExternalInput").ap() for k, a in arrays.items()]
    out = nc.dram_tensor("out", (P, DC, B, S), F32, kind="ExternalOutput").ap()
    xattn_stack_kernel(nc, *args, out)
    r = run_bass_kernel_spmd(nc, [{f"in_{k}": a for k, a in arrays.items()}], core_ids=[0])
    got = r.results[0]["out"].reshape(P, DC, B, S)
    return np.ascontiguousarray(got.transpose(2, 3, 1, 0).reshape(B, S, D))
```
